# Optimizing a Trainium2 kernel written in Bass

```python
import numpy as np
import jax
import jax.numpy as jnp

def _softmax(x, axis=-1):
    return jax.nn.softmax(x, axis=axis)

def _gelu(x):
    return jax.nn.gelu(x, approximate=True)

def _silu(x):
    return jax.nn.silu(x)

def _sigmoid(x):
    return jax.nn.sigmoid(x)

def _layernorm(x, axis=-1, eps=1e-05):
    m = jnp.mean(x, axis=axis, keepdims=True)
    v = jnp.var(x, axis=axis, keepdims=True)
    return (x - m) / jnp.sqrt(v + eps)

def _scatter_add(tgt, idx, src, axis=0):
    return tgt.at[idx].add(src)

def _segment_sum(src, seg, n):
    return jax.ops.segment_sum(src, seg, n)
kernel_name = 'mk_recurrent_d1_jaxref_r4_57a778'

def setup_inputs(seed: int=0):
    np.random.seed(seed)
    _w = jnp.asarray

    def _L0_attn_setup():
        import jax, jax.numpy as jnp
        import numpy as np
        B, T, C = (4, 1024, 256)
        NUM_LAYERS = 24
        LAYER_ID = 0
        EPS = 1e-05

        def _ln(x, w, b):
            m = x.mean(-1, keepdims=True)
            v = x.var(-1, keepdims=True)
            return (x - m) / jnp.sqrt(v + EPS) * w + b

        def _time_shift(x):
            return jnp.pad(x, ((0, 0), (1, 0), (0, 0)))[:, :-1]

        def _wkv(w, u, k, v):

            def step(carry, kv_t):
                aa, bb, pp = carry
                kt, vt = kv_t
                ww = u + kt
                p = jnp.maximum(pp, ww)
                e1 = jnp.exp(pp - p)
                e2 = jnp.exp(ww - p)
                y = (e1 * aa + e2 * vt) / (e1 * bb + e2)
                ww2 = pp + w
                p2 = jnp.maximum(ww2, kt)
                e1 = jnp.exp(ww2 - p2)
                e2 = jnp.exp(kt - p2)
                return ((e1 * aa + e2 * vt, e1 * bb + e2, p2), y)
            Bz, Tz, Cz = k.shape
            init = (jnp.zeros((Bz, Cz), k.dtype), jnp.zeros((Bz, Cz), k.dtype), jnp.full((Bz, Cz), -1e+38, k.dtype))
            kT = jnp.swapaxes(k, 0, 1)
            vT = jnp.swapaxes(v, 0, 1)
            _, y = jax.lax.scan(step, init, (kT, vT))
            return jnp.swapaxes(y, 0, 1)
        key = jax.random.key(seed)
        ks = jax.random.split(key, 9)
        s = 0.02
        ratio_0_to_1 = LAYER_ID / (NUM_LAYERS - 1)
        ratio_1_to_almost0 = 1.0 - LAYER_ID / NUM_LAYERS
        h = np.arange(C, dtype=np.float64)
        time_decay = (-5.0 + 8.0 * (h / (C - 1)) ** (0.7 + 1.3 * ratio_0_to_1)).astype(np.float32)
        zigzag = ((np.arange(C) + 1) % 3 - 1) * 0.5
        time_first = (np.ones(C) * np.log(0.3) + zigzag).astype(np.float32)
        xi = np.arange(C, dtype=np.float64) / C
        tmk = (xi ** ratio_1_to_almost0).astype(np.float32)
        tmv = (xi ** ratio_1_to_almost0 + 0.3 * ratio_0_to_1).astype(np.float32)
        tmr = (xi ** (0.5 * ratio_1_to_almost0)).astype(np.float32)
        cmk = (xi ** ratio_1_to_almost0).astype(np.float32)
        H = 4 * C
        return {'x': jax.random.normal(ks[0], (B, T, C), jnp.float32), 'ln0_w': jnp.ones(C), 'ln0_b': jnp.zeros(C), 'ln1_w': jnp.ones(C), 'ln1_b': jnp.zeros(C), 'ln2_w': jnp.ones(C), 'ln2_b': jnp.zeros(C), 'time_decay': jnp.asarray(time_decay), 'time_first': jnp.asarray(time_first), 'tmk': jnp.asarray(tmk), 'tmv': jnp.asarray(tmv), 'tmr': jnp.asarray(tmr), 'Wk': jax.random.normal(ks[1], (C, C), jnp.float32) * s, 'Wv': jax.random.normal(ks[2], (C, C), jnp.float32) * s, 'Wr': jax.random.normal(ks[3], (C, C), jnp.float32) * s, 'Wo': jax.random.normal(ks[4], (C, C), jnp.float32) * s, 'cmk': jnp.asarray(cmk), 'cmr': jnp.asarray(cmk), 'Wfk': jax.random.normal(ks[5], (H, C), jnp.float32) * s, 'Wfr': jax.random.normal(ks[6], (C, C), jnp.float32) * s, 'Wfv': jax.random.normal(ks[7], (C, H), jnp.float32) * s}
    _L0_attn_in = _L0_attn_setup()

    def _L0_ffn_setup():
        import jax, jax.numpy as jnp
        import numpy as np
        key = jax.random.key(seed)
        k0, k1, k2, k3 = jax.random.split(key, 4)
        B, S, D, F, E = (8, 512, 256, 512, 8)
        x = jax.random.normal(k0, (B, S, D), dtype=jnp.float32)
        Wg = jax.random.normal(k1, (D, E), dtype=jnp.float32) * 0.02
        W1 = jax.random.normal(k2, (E, D, F), dtype=jnp.float32) * 0.02
        W2 = jax.random.normal(k3, (E, F, D), dtype=jnp.float32) * 0.02
        return {'x': x, 'Wg': Wg, 'W1': W1, 'W2': W2}
    _L0_ffn_in = _L0_ffn_setup()
    _d = {'L0_attn_x': _L0_attn_in['x'], 'L0_attn_ln0_w': _L0_attn_in['ln0_w'], 'L0_attn_ln0_b': _L0_attn_in['ln0_b'], 'L0_attn_ln1_w': _L0_attn_in['ln1_w'], 'L0_attn_ln1_b': _L0_attn_in['ln1_b'], 'L0_attn_ln2_w': _L0_attn_in['ln2_w'], 'L0_attn_ln2_b': _L0_attn_in['ln2_b'], 'L0_attn_time_decay': _L0_attn_in['time_decay'], 'L0_attn_time_first': _L0_attn_in['time_first'], 'L0_attn_tmk': _L0_attn_in['tmk'], 'L0_attn_tmv': _L0_attn_in['tmv'], 'L0_attn_tmr': _L0_attn_in['tmr'], 'L0_attn_Wk': _L0_attn_in['Wk'], 'L0_attn_Wv': _L0_attn_in['Wv'], 'L0_attn_Wr': _L0_attn_in['Wr'], 'L0_attn_Wo': _L0_attn_in['Wo'], 'L0_attn_cmk': _L0_attn_in['cmk'], 'L0_attn_cmr': _L0_attn_in['cmr'], 'L0_attn_Wfk': _L0_attn_in['Wfk'], 'L0_attn_Wfr': _L0_attn_in['Wfr'], 'L0_attn_Wfv': _L0_attn_in['Wfv'], 'L0_ffn_Wg': _L0_ffn_in['Wg'], 'L0_ffn_W1': _L0_ffn_in['W1'], 'L0_ffn_W2': _L0_ffn_in['W2']}
    _x0 = _d['L0_attn_x']
    _d['L0_attn_x'] = jax.random.normal(jax.random.fold_in(jax.random.key(seed), 1), (16, 512, 256), dtype=_x0.dtype)
    del _x0
    return _d

def reference(L0_attn_x, L0_attn_ln0_w, L0_attn_ln0_b, L0_attn_ln1_w, L0_attn_ln1_b, L0_attn_ln2_w, L0_attn_ln2_b, L0_attn_time_decay, L0_attn_time_first, L0_attn_tmk, L0_attn_tmv, L0_attn_tmr, L0_attn_Wk, L0_attn_Wv, L0_attn_Wr, L0_attn_Wo, L0_attn_cmk, L0_attn_cmr, L0_attn_Wfk, L0_attn_Wfr, L0_attn_Wfv, L0_ffn_Wg, L0_ffn_W1, L0_ffn_W2):

    def _L0_attn_ref(x, ln0_w, ln0_b, ln1_w, ln1_b, ln2_w, ln2_b, time_decay, time_first, tmk, tmv, tmr, Wk, Wv, Wr, Wo, cmk, cmr, Wfk, Wfr, Wfv):
        import jax, jax.numpy as jnp
        import numpy as np
        B, T, C = (4, 1024, 256)
        NUM_LAYERS = 24
        LAYER_ID = 0
        EPS = 1e-05

        def _ln(x, w, b):
            m = x.mean(-1, keepdims=True)
            v = x.var(-1, keepdims=True)
            return (x - m) / jnp.sqrt(v + EPS) * w + b

        def _time_shift(x):
            return jnp.pad(x, ((0, 0), (1, 0), (0, 0)))[:, :-1]

        def _wkv(w, u, k, v):

            def step(carry, kv_t):
                aa, bb, pp = carry
                kt, vt = kv_t
                ww = u + kt
                p = jnp.maximum(pp, ww)
                e1 = jnp.exp(pp - p)
                e2 = jnp.exp(ww - p)
                y = (e1 * aa + e2 * vt) / (e1 * bb + e2)
                ww2 = pp + w
                p2 = jnp.maximum(ww2, kt)
                e1 = jnp.exp(ww2 - p2)
                e2 = jnp.exp(kt - p2)
                return ((e1 * aa + e2 * vt, e1 * bb + e2, p2), y)
            Bz, Tz, Cz = k.shape
            init = (jnp.zeros((Bz, Cz), k.dtype), jnp.zeros((Bz, Cz), k.dtype), jnp.full((Bz, Cz), -1e+38, k.dtype))
            kT = jnp.swapaxes(k, 0, 1)
            vT = jnp.swapaxes(v, 0, 1)
            _, y = jax.lax.scan(step, init, (kT, vT))
            return jnp.swapaxes(y, 0, 1)
        x = _ln(x, ln0_w, ln0_b)
        h = _ln(x, ln1_w, ln1_b)
        xx = _time_shift(h)
        xk = h * tmk + xx * (1 - tmk)
        xv = h * tmv + xx * (1 - tmv)
        xr = h * tmr + xx * (1 - tmr)
        k = jnp.einsum('btc,oc->bto', xk, Wk)
        v = jnp.einsum('btc,oc->bto', xv, Wv)
        sr = jax.nn.sigmoid(jnp.einsum('btc,oc->bto', xr, Wr))
        w = -jnp.exp(time_decay)
        att = _wkv(w, time_first, k, v)
        rwkv = jnp.einsum('btc,oc->bto', sr * att, Wo)
        x = x + rwkv
        h2 = _ln(x, ln2_w, ln2_b)
        xx2 = _time_shift(h2)
        xk2 = h2 * cmk + xx2 * (1 - cmk)
        xr2 = h2 * cmr + xx2 * (1 - cmr)
        kf = jnp.einsum('btc,hc->bth', xk2, Wfk)
        kf = jnp.square(jax.nn.relu(kf))
        kv = jnp.einsum('bth,ch->btc', kf, Wfv)
        rkv = jax.nn.sigmoid(jnp.einsum('btc,oc->bto', xr2, Wfr)) * kv
        return x + rkv

    def _L0_ffn_ref(x, Wg, W1, W2):
        import jax, jax.numpy as jnp
        import numpy as np
        B, S, D = x.shape
        E = Wg.shape[1]
        T = B * S
        cap = max(1, T // E)
        xt = x.reshape(T, D)
        logits = xt @ Wg
        probs = jax.nn.softmax(logits, axis=-1)
        pT = probs.T
        _, top_idx = jax.lax.top_k(pT, cap)
        sel = jnp.zeros((E, T), dtype=bool).at[jnp.arange(E)[:, None], top_idx].set(True)
        masked = jnp.where(sel, pT, -jnp.inf)
        assigned = sel.any(axis=0)
        tok2exp = jnp.where(assigned, jnp.argmax(masked, axis=0), jnp.argmax(pT, axis=0))
        weights = jnp.take_along_axis(probs, tok2exp[:, None], axis=1)[:, 0]
        out = jnp.zeros_like(xt)
        for e in range(E):
            gate = jnp.where(tok2exp == e, weights, 0.0)
            h = jax.nn.gelu(xt @ W1[e], approximate=False) @ W2[e]
            out = out + gate[:, None] * h
        return out.reshape(B, S, D)
    x = L0_attn_x
    xn = _layernorm(x, axis=-1)
    s = _L0_attn_ref(xn, L0_attn_ln0_w, L0_attn_ln0_b, L0_attn_ln1_w, L0_attn_ln1_b, L0_attn_ln2_w, L0_attn_ln2_b, L0_attn_time_decay, L0_attn_time_first, L0_attn_tmk, L0_attn_tmv, L0_attn_tmr, L0_attn_Wk, L0_attn_Wv, L0_attn_Wr, L0_attn_Wo, L0_attn_cmk, L0_attn_cmr, L0_attn_Wfk, L0_attn_Wfr, L0_attn_Wfv)
    g = _silu(_L0_ffn_ref(xn, L0_ffn_Wg, L0_ffn_W1, L0_ffn_W2))
    x = x + s * g
    return x

_drawn_inputs = setup_inputs


def setup_inputs(seed=0):
    import zlib

    import numpy as np

    out = dict(_drawn_inputs(seed))
    spreads = {'L0_attn_ln0_w': (1.0, 0.2),
     'L0_attn_ln0_b': (0.0, 0.1),
     'L0_attn_ln1_w': (1.0, 0.2),
     'L0_attn_ln1_b': (0.0, 0.1),
     'L0_attn_ln2_w': (1.0, 0.2),
     'L0_attn_ln2_b': (0.0, 0.1)}
    factors = {}
    for name, (base, spread) in spreads.items():
        noise = np.random.default_rng([zlib.crc32(name.encode()), seed]).standard_normal(out[name].shape)
        drawn = base * np.exp(spread * noise) if base else spread * noise
        out[name] = jnp.asarray(drawn.astype(out[name].dtype))
    for name, factor in factors.items():
        out[name] = (out[name] * factor).astype(out[name].dtype)
    return out
```

```python
from contextlib import ExitStack

import concourse.bass as bass
from concourse import mybir

F32 = mybir.dt.float32
I32 = mybir.dt.int32
ALU = mybir.AluOpType
ACT = mybir.ActivationFunctionType
AX_X = mybir.AxisListType.X
ds = bass.ds

P = 128
BITS = 30
R_PEXP, R_COUNTS, R_SEL, R_ONEHOT, R_ALL = 7, 9, 14, 26, 44
PARAMS = ["ln1_w", "ln1_b", "ln2_w", "ln2_b", "decay", "first", "tmk", "tmv", "tmr", "cmk", "cmr"]


class Steps:

    def __init__(self, eng, sem, per_run, run, waited):
        self.eng, self.sem, self.per_run, self.run, self.waited = eng, sem, per_run, run, waited
        self.k = 0

    def then(self, ins):
        ins.then_inc(self.sem, 1)
        self.k += 1
        return self.k

    def wait(self, k=None):
        self.eng.wait_ge(self.sem, self.run * self.per_run + (self.k if k is None else k))
        if not isinstance(self.run, int):
            self.eng.sem_inc(self.waited)

    def end(self):
        assert self.k == self.per_run, (self.k, self.per_run)


def rwkv_times_moe(nc, x, xT, vec, ln0_w, ln0_b, WkT, WvT, WrT, WoT, WfkT, WfrT, WfvT, Wg, W1, W2,
                   consts, tile_iota, slots_sorted, moe_out, out):
    T, C = x.shape
    SEQ = 512
    NB = T // SEQ
    CH = C // P
    J = SEQ // P
    NTILE = T // P
    HID = WfkT.shape[1]
    HC = HID // P
    E, _, F = W1.shape
    FK = F // P
    CAP = max(1, T // E)
    EPS = 1e-5
    NT = slots_sorted.shape[0] // P
    NCH = NTILE // J
    assert CH == 2 and J == 4 and E * NCH == P and NT >= NTILE + E - 1 and NT % 2 == 0

    with ExitStack() as ctx:
        def sb(name, shape, dt=F32):
            return ctx.enter_context(nc.sbuf_tensor(name, shape, dt))

        def sem(name):
            return ctx.enter_context(nc.semaphore(name))

        s_all = sb("s_all", [P, NTILE * C])
        vecs = sb("vecs", [P, CH, len(PARAMS)])
        V = {n: i for i, n in enumerate(PARAMS)}
        wneg = sb("wneg", [P, CH])
        uneg = sb("uneg", [P, CH])
        w0_bc = sb("w0_bc", [P, C])
        b0_bc = sb("b0_bc", [P, C])
        cst = sb("cst", [P, 5, P])
        ident, esum, eprefix, prefix, ones = (cst[:, i, :] for i in range(5))
        tok_stats = sb("tok_stats", [P, NTILE, 4])
        slot_i = sb("slot_i", [P, NTILE], I32)
        gate = sb("gate", [P, NTILE])
        expert_at = sb("expert_at", [1, NT], I32)
        stats_cur = sb("stats_cur", [P, 4, 4])
        slot_cur = sb("slot_cur", [P, J], I32)
        bnst = sb("bnst", [P, J, 6])
        mv1 = sb("mv1", [P, J, 2])
        mv2 = sb("mv2", [P, J, 2])
        cf1 = sb("cf1", [P, 2, J])
        cf2 = sb("cf2", [P, 2, J])
        lnw1 = sb("lnw1", [P, 2, J])
        lnw2 = sb("lnw2", [P, 2, J])
        minus_half = sb("minus_half", [P, NTILE])

        arena = sb("arena", [P, 34800])
        at = [0]

        def part(n):
            at[0] += n
            assert at[0] <= 34800
            return arena[:, at[0] - n:at[0]]

        first_dead = at[0]
        mixA = part(3 * CH * SEQ).rearrange("p (m c t) -> p m c t", m=3, c=CH)
        dmix = part(CH * SEQ).rearrange("p (c t) -> p c t", c=CH)
        kvs = part(3 * CH * SEQ).rearrange("p (m c t) -> p m c t", m=3, c=CH)
        E1 = [part(2 * SEQ).rearrange("p (m t) -> p m t", m=2) for _ in range(CH)]
        E2 = [part(2 * SEQ).rearrange("p (m t) -> p m t", m=2) for _ in range(CH)]
        qb = [part(SEQ) for _ in range(CH)]
        evb = [part(SEQ) for _ in range(CH)]
        t1b = [part(SEQ) for _ in range(CH)]
        pp = part(SEQ + 1)
        aa = part(SEQ + 1)
        bb = part(SEQ + 1)
        att = part(CH * SEQ).rearrange("p (c t) -> p c t", c=CH)
        moe_end = at[0]
        hT = part(CH * (SEQ + 1)).rearrange("p (c t) -> p c t", c=CH)
        hn = part(J * C).rearrange("p (j c) -> p j c", j=J)
        x_in = part(J * C).rearrange("p (j c) -> p j c", j=J)
        mixB = part(2 * CH * SEQ).rearrange("p (m c t) -> p m c t", m=2, c=CH)
        kf2 = part(HC * SEQ).rearrange("p (h t) -> p h t", h=HC)
        sigf = part(J * C)
        wk, wv, wr, wo, wfr = (part(CH * C).rearrange("p (k n) -> p k n", k=CH) for _ in range(5))
        wfk = part(CH * HID).rearrange("p (k n) -> p k n", k=CH)
        wfv = part(HC * C).rearrange("p (k n) -> p k n", k=HC)
        xa = [arena[:, i * 1024:(i + 1) * 1024].rearrange("p (j c) -> p j c", j=J) for i in range(2)]
        xta = [arena[:, 2048 + i * 1024:3072 + i * 1024].rearrange("p (k t) -> p k t", k=CH) for i in range(2)]
        lgT = [arena[0:E, 4096 + i * 512:4608 + i * 512] for i in range(2)]
        ra = 5120
        NE = NTILE * E

        def routing(n=NE, dt=None):
            nonlocal ra
            ra += n
            v = arena[:, ra - n:ra]
            return v

        logits, probs, work, pexp, selT, oneT, win, mask8 = (routing() for _ in range(8))
        small = routing(8 * NTILE)
        mvA = routing(2 * NTILE)
        wg_sb = routing(CH * E)
        wgc = routing(CH * E)
        erev = routing(E)
        reset = routing(NE)
        tiny = routing(64)
        iota_sb = routing(NT)
        tw = routing(NT * E)
        zero_rows = routing(1024)
        assert ra <= 34800 - 5 * CH * C - CH * HID - HC * C
        w1_sb = arena[:, first_dead:first_dead + E * CH * F]
        w2_sb = arena[:, first_dead + E * CH * F:first_dead + 2 * E * CH * F]
        assert first_dead + 2 * E * CH * F <= moe_end + CH * (SEQ + 1) + J * C
        rc = [moe_end + CH * (SEQ + 1) + J * C]

        def ring(n):
            rc[0] += n
            assert rc[0] <= 34800
            return arena[:, rc[0] - n:rc[0]]

        xs_t = [ring(C) for _ in range(2)]
        xsT = [ring(C).rearrange("p (k t) -> p k t", k=CH) for _ in range(2)]
        hg = [ring(F) for _ in range(2)]
        hgT = [ring(F).rearrange("p (k t) -> p k t", k=FK) for _ in range(2)]
        y_t = [ring(C) for _ in range(2)]
        yg = [ring(J * C).rearrange("p (j c) -> p j c", j=J) for _ in range(2)]
        xd = [ring(J * C).rearrange("p (j c) -> p j c", j=J) for _ in range(2)]
        g_slot = [sb(f"g_slot{i}", [P, J], I32) for i in range(2)]
        g_gate = [sb(f"g_gate{i}", [P, J]) for i in range(2)]

        psT = ctx.enter_context(nc.psum_tensor("psT", [P, 2, 512], F32))
        psM = ctx.enter_context(nc.psum_tensor("psM", [P, 3, 512], F32))
        psKV = ctx.enter_context(nc.psum_tensor("psKV", [P, 2, 512], F32))
        psR = ctx.enter_context(nc.psum_tensor("psR", [P, 512], F32))

        names = """waited params_in consts_in xa_in0 xa_in1 xta_in0 xta_in1 weights_in wg_in
        zeroed zeros_out a_step a_stats logits_done logits_copied logitsT_done logits_kept
        wg_mean wg_ready decay_exp pool_const
        var_ready pow_ready bit_step bit_counted bit_summed route_step route_pe route_exp_in route_exp_out routed
        x_in fetched x0_ready xn_ready scattered embed_step ln1_stats cf1_ready hn1_ready tr1_done
        h1_ready mix1_step mix1_done proj_done kvr_ready wkv_step pre_done exp_done att_done o_done
        x2_done ln2_step ln2_stats cf2_ready hn2_ready tr2_done h2_ready mix2_step mix2_done
        kf_done relu_done sq_done fr_done sigf_done kv_done s_done s_step rstd1_step rstd2_step
        moe_w_in xs_in0 xs_in1 xsT_done xsT_ready h_done gelu_done hgT_done hgT_ready y_done y_ready
        y_out0 y_out1 d_fetched d_x_in0 d_x_in1 gathered0 gathered1 d_silu d_step d_ready d_out0 d_out1
        """.split()
        S = {n: sem(n) for n in names}

        def tile_row(b):
            return s_all[:, ds(b * (J * C), J * C)]

        def wait_run(eng, s, value):
            eng.wait_ge(s, value)
            if not isinstance(value, int):
                eng.sem_inc(S["waited"])

        xT_k = xT.rearrange("(k p) t -> p k t", p=P)
        xrows = x.rearrange("(n p) c -> p n c", p=P)
        orows = out.rearrange("(n p) c -> p n c", p=P)
        srows = slots_sorted.rearrange("(n p) c -> p n c", p=P)
        y_ps = [psM[:, 2, 0:C], psR[:, 0:C]]

        block = ctx.enter_context(nc.Block())

        @block.sync
        def _(sp):
            sp.dma_start(vecs[:], vec.rearrange("(c p) n -> p c n", p=P)).then_inc(S["params_in"], 16)
            sp.dma_start(wg_sb.rearrange("p (k e) -> p k e", k=CH),
                         Wg.rearrange("(k p) e -> p k e", p=P)).then_inc(S["wg_in"], 16)
            sp.dma_start(cst[:], consts[:, 0:5 * P].rearrange("p (i q) -> p i q", i=5)).then_inc(S["consts_in"], 16)
            sp.dma_start(erev, consts[:, 5 * P:5 * P + E]).then_inc(S["consts_in"], 16)
            sp.dma_start(iota_sb[0:1, :], tile_iota).then_inc(S["consts_in"], 16)
            sp.dma_start(w0_bc[:], ln0_w.partition_broadcast(P)).then_inc(S["params_in"], 16)
            sp.dma_start(b0_bc[:], ln0_b.partition_broadcast(P)).then_inc(S["params_in"], 16)
            for i in range(2):
                sp.dma_start(xa[i], xrows[:, i * J:(i + 1) * J, :]).then_inc(S[f"xa_in{i}"], 16)
                sp.dma_start(xta[i], xT_k[:, :, i * SEQ:(i + 1) * SEQ]).then_inc(S[f"xta_in{i}"], 16)
            with sp.Fori(1, NB // 2) as g:
                for i in range(2):
                    sp.wait_ge(S["a_stats"], 2 * g + (i - 1))
                    sp.dma_start(xa[i], xrows[:, ds(g * (2 * J) + i * J, J), :]).then_inc(S[f"xa_in{i}"], 16)
                    sp.wait_ge(S["logits_done"], 2 * g + (i - 1))
                    sp.dma_start(xta[i], xT_k[:, :, ds(g * (2 * SEQ) + i * SEQ, SEQ)]).then_inc(S[f"xta_in{i}"], 16)
            for w_sb, w_dram in ((wk, WkT), (wv, WvT), (wr, WrT), (wo, WoT), (wfr, WfrT), (wfk, WfkT), (wfv, WfvT)):
                sp.dma_start(w_sb, w_dram.rearrange("(k p) n -> p k n", p=P)).then_inc(S["weights_in"], 16)
            sp.wait_ge(S["zeroed"], 1)
            for n in range(0, NT, J):
                sp.dma_start(srows[:, n:n + J, :], zero_rows.rearrange("p (n c) -> p n c", c=C)).then_inc(S["zeros_out"], 16)
            sp.wait_ge(S["routed"], 1)
            sp.dma_start(x_in, xrows[:, 0:J, :]).then_inc(S["x_in"], 16)
            with sp.Fori(1, NB) as b:
                sp.wait_ge(S["scattered"], b * (16 * J))
                sp.dma_start(x_in, xrows[:, ds(b * J, J), :]).then_inc(S["x_in"], 16)
            sp.wait_ge(S["mix2_done"], 2 * NB)
            for e in range(E):
                sp.dma_start(w1_sb.rearrange("p (e k f) -> p e k f", e=E, k=CH)[:, e],
                             W1[e].rearrange("(k p) f -> p k f", p=P)).then_inc(S["moe_w_in"], 16)
                sp.dma_start(w2_sb.rearrange("p (e k f) -> p e k f", e=E, k=FK)[:, e],
                             W2[e].rearrange("(k p) f -> p k f", p=P)).then_inc(S["moe_w_in"], 16)
            sp.wait_ge(S["scattered"], NB * 16 * J)
            sp.wait_ge(S["s_done"], NB)
            for i in range(2):
                sp.dma_start(xs_t[i], slots_sorted[i * P:(i + 1) * P, :]).then_inc(S[f"xs_in{i}"], 16)
            with sp.Fori(1, NT // 2) as g:
                for i in range(2):
                    sp.wait_ge(S["xsT_done"], 2 * g + (i - 1))
                    sp.dma_start(xs_t[i], slots_sorted[ds(g * (2 * P) + i * P, P), :]).then_inc(S[f"xs_in{i}"], 16)
            for i in range(2):
                sp.dma_start(xd[i], xrows[:, i * J:(i + 1) * J, :]).then_inc(S[f"d_x_in{i}"], 16)
            with sp.Fori(0, NB // 2 - 1) as g:
                for i in range(2):
                    sp.wait_ge(S["d_ready"], 2 * g + (i + 1))
                    sp.dma_start(orows[:, ds(g * (2 * J) + i * J, J), :], xd[i]).then_inc(S[f"d_out{i}"], 16)
                    sp.wait_ge(S[f"d_out{i}"], 16 * g + 16)
                    sp.dma_start(xd[i], xrows[:, ds(g * (2 * J) + (2 + i) * J, J), :]).then_inc(S[f"d_x_in{i}"], 16)
            for i in range(2):
                sp.wait_ge(S["d_ready"], NB - 1 + i)
                sp.dma_start(orows[:, (NB - 2 + i) * J:(NB - 1 + i) * J, :], xd[i]).then_inc(S[f"d_out{i}"], 16)
            for i in range(2):
                sp.wait_ge(S[f"d_out{i}"], 16 * (NB // 2))

        @block.gpsimd
        def _(pool):
            pool.memset(zero_rows, 0.0).then_inc(S["zeroed"], 1)
            pool.memset(minus_half[:], -0.5).then_inc(S["pool_const"], 1)
            pool.wait_ge(S["pool_const"], 1)

            st = Steps(pool, S["pow_ready"], 8, 0, S["waited"])
            mv = mvA.rearrange("p (n s) -> p n s", s=2)
            mean, var = mv[:, :, 0], mv[:, :, 1]
            sv = small.rearrange("p (k n) -> p k n", n=NTILE)
            pool.wait_ge(S["var_ready"], 1)
            st.then(pool.tensor_scalar(sv[:, 0], var, EPS, 1.0, ALU.add, ALU.mult))
            st.wait()
            st.then(pool.tensor_tensor(tok_stats[:, :, 2], sv[:, 0], minus_half[:], ALU.pow))
            st.wait()
            pool.tensor_tensor(sv[:, 1], var, tok_stats[:, :, 2], ALU.mult)
            st.then(pool.tensor_scalar(sv[:, 2], mean, -1.0, 0.0, ALU.mult, ALU.add))
            st.wait()
            st.then(pool.tensor_tensor(sv[:, 3], sv[:, 1], tok_stats[:, :, 2], ALU.mult))
            st.wait()
            st.then(pool.tensor_scalar(sv[:, 4], sv[:, 3], EPS, 1.0, ALU.add, ALU.mult))
            st.wait()
            st.then(pool.tensor_tensor(sv[:, 5], sv[:, 4], minus_half[:], ALU.pow))
            st.wait()
            st.then(pool.tensor_tensor(tok_stats[:, :, 0], sv[:, 5], tok_stats[:, :, 2], ALU.mult))
            st.wait()
            pool.tensor_tensor(tok_stats[:, :, 1], sv[:, 2], tok_stats[:, :, 0], ALU.mult)
            st.then(pool.tensor_tensor(tok_stats[:, :, 3], sv[:, 2], tok_stats[:, :, 2], ALU.mult))
            st.end()

            def scatter(b):
                wait_run(pool, S["fetched"], b + 1)
                wait_run(pool, S["xn_ready"], b + 1)
                if isinstance(b, int) and b == 0:
                    pool.wait_ge(S["zeros_out"], 16 * (NT // J))
                for j in range(J):
                    pool.indirect_dma_start(slots_sorted[:, :], bass.IndirectOffsetOnAxis(slot_cur[:, j:j + 1], axis=0),
                                            x_in[:, j, :], None).then_inc(S["scattered"], 16)

            def rstd(b, stats, mv, lnw, cf, step, ready):
                st = Steps(pool, S[step], 2, b, S["waited"])
                wait_run(pool, S[stats], b + 1)
                pool.tensor_scalar(lnw[:, 0], mv[:, :, 1], EPS, 1.0, ALU.add, ALU.mult)
                st.then(pool.tensor_scalar(lnw[:, 1], mv[:, :, 0], -1.0, 0.0, ALU.mult, ALU.add))
                st.wait()
                st.then(pool.tensor_tensor(cf[:, 0], lnw[:, 0], minus_half[:, 0:J], ALU.pow))
                st.wait()
                pool.tensor_tensor(cf[:, 1], lnw[:, 1], cf[:, 0], ALU.mult).then_inc(S[ready], 1)
                st.end()

            def rstd1(b):
                rstd(b, "ln1_stats", mv1, lnw1, cf1, "rstd1_step", "cf1_ready")

            def rstd2(b):
                rstd(b, "ln2_stats", mv2, lnw2, cf2, "rstd2_step", "cf2_ready")

            scatter(0)
            rstd1(0)
            with pool.Fori(0, NB - 1) as b:
                scatter(b + 1)
                rstd1(b + 1)
                rstd2(b)
            rstd2(NB - 1)
            with pool.Fori(0, NT // 2) as g:
                for i in range(2):
                    wait_run(pool, S["y_ready"], 2 * g + (i + 1))
                    pool.dma_start(moe_out[ds(g * (2 * P) + i * P, P), :], y_t[i]).then_inc(S[f"y_out{i}"], 16)
            for i in range(2):
                pool.wait_ge(S[f"y_out{i}"], 16 * (NT // 2))

            def gather(b, i):
                wait_run(pool, S["d_fetched"], b + 1)
                for j in range(J):
                    pool.indirect_dma_start(yg[i][:, j, :], None, moe_out[:, :],
                                            bass.IndirectOffsetOnAxis(g_slot[i][:, j:j + 1], axis=0)
                                            ).then_inc(S[f"gathered{i}"], 16)

            with pool.Fori(0, NB // 2) as g:
                for i in range(2):
                    gather(2 * g + i, i)

        @block.scalar
        def _(act):
            act.wait_ge(S["params_in"], 48)
            act.activation(wneg[:], vecs[:, :, V["decay"]], ACT.Exp).then_inc(S["decay_exp"], 1)

            def copy_logits(b, i):
                act.wait_ge(S["logits_done"], b + 1)
                act.activation(lgT[i], psM[0:E, i, :], ACT.Copy).then_inc(S["logits_copied"], 1)

            with act.Fori(0, NB // 2) as g:
                for i in range(2):
                    copy_logits(2 * g + i, i)
            act.wait_ge(S["route_exp_in"], 1)
            act.activation(probs, logits, ACT.Exp).then_inc(S["route_exp_out"], 1)
            act.wait_ge(S["routed"], 1)
            act.wait_ge(S["zeros_out"], 16 * (NT // J))

            def norm0(b):
                wait_run(act, S["fetched"], b + 1)
                wait_run(act, S["x_in"], 16 * b + 16)
                if not (isinstance(b, int) and b == 0):
                    wait_run(act, S["tr2_done"], b - 1) if not (isinstance(b, int) and b == 1) else None
                for j in range(J):
                    ins = act.activation(hn[:, j], x_in[:, j], ACT.Identity,
                                         scale=stats_cur[:, j, 0:1], bias=stats_cur[:, j, 1:2])
                ins.then_inc(S["x0_ready"], 1)
                wait_run(act, S["x0_ready"], b + 1)
                for j in range(J):
                    ins = act.activation(x_in[:, j], x_in[:, j], ACT.Identity,
                                         scale=stats_cur[:, j, 2:3], bias=stats_cur[:, j, 3:4])
                ins.then_inc(S["xn_ready"], 1)

            def norm(b, cf, cf_ready, ready):
                wait_run(act, S[cf_ready], b + 1)
                xs = tile_row(b)
                for j in range(J):
                    ins = act.activation(hn[:, j], xs[:, j * C:(j + 1) * C], ACT.Identity,
                                         scale=cf[:, 0, j:j + 1], bias=cf[:, 1, j:j + 1])
                ins.then_inc(S[ready], 1)

            def affine(b, tr_done, w, bias, ready):
                wait_run(act, S[tr_done], b + 1)
                for c in range(CH):
                    act.activation(hT[:, c, 1:SEQ + 1], psT[:, c, :], ACT.Identity,
                                   scale=vecs[:, c, V[w]:V[w] + 1], bias=vecs[:, c, V[bias]:V[bias] + 1]
                                   ).then_inc(S[ready], 1)

            def norm1(b):
                norm(b, cf1, "cf1_ready", "hn1_ready")

            def affine1(b):
                affine(b, "tr1_done", "ln1_w", "ln1_b", "h1_ready")

            def norm2(b):
                if not (isinstance(b, int) and b == NB - 1):
                    wait_run(act, S["tr1_done"], b + 2)
                norm(b, cf2, "cf2_ready", "hn2_ready")

            def affine2(b):
                if not (isinstance(b, int) and b == NB - 1):
                    wait_run(act, S["mix1_done"], 3 * b + 6)
                affine(b, "tr2_done", "ln2_w", "ln2_b", "h2_ready")

            def take_kvr(b):
                if not (isinstance(b, int) and b == 0):
                    wait_run(act, S["att_done"], 2 * b)
                for u in range(3 * CH):
                    act.wait_ge(S["proj_done"], b * (3 * CH) + (u + 1))
                    act.activation(kvs[:, u // CH, u % CH, :], psM[:, u % 3, :],
                                   ACT.Sigmoid if u // CH == 2 else ACT.Copy).then_inc(S["kvr_ready"], 1)

            def exps(b, c):
                act.wait_ge(S["pre_done"], b * CH + (c + 1))
                act.activation(E1[c], E1[c], ACT.Exp).then_inc(S["exp_done"], 1)
                act.activation(E2[c], E2[c], ACT.Exp, scale=-1.0).then_inc(S["exp_done"], 1)

            def relu(b, h):
                if h == 0:
                    wait_run(act, S["tr2_done"], b + 1)
                act.wait_ge(S["kf_done"], b * HC + (h + 1))
                act.activation(kf2[:, h], psM[:, h % 3, :], ACT.Relu).then_inc(S["relu_done"], 1)

            def square(b, h):
                act.wait_ge(S["relu_done"], b * HC + (h + 1))
                act.activation(kf2[:, h], kf2[:, h], ACT.Square).then_inc(S["sq_done"], 1)

            def sigmoid_fr(b):
                wait_run(act, S["mix2_done"], 2 * b + 2)
                for u in range(2):
                    act.wait_ge(S["fr_done"], 2 * b + (u + 1))
                    act.activation(sigf[:, u * 512:(u + 1) * 512], psM[:, (HC + u) % 3, :],
                                   ACT.Sigmoid).then_inc(S["sigf_done"], 1)

            def relus(b, lo, hi):
                for h in range(lo, hi):
                    relu(b, h)
                    if h:
                        square(b, h - 1)

            def round_(b, ffn, ahead):
                if ffn:
                    relus(b - 1, 0, 2)
                exps(b, 0)
                if ffn:
                    relus(b - 1, 2, 4)
                exps(b, 1)
                if ffn:
                    relus(b - 1, 4, HC)
                    square(b - 1, HC - 1)
                if ahead:
                    norm0(b + 1)
                if ffn:
                    sigmoid_fr(b - 1)
                if ahead:
                    norm1(b + 1)
                    affine1(b + 1)
                norm2(b)
                affine2(b)
                if ahead:
                    take_kvr(b + 1)

            norm0(0)
            norm1(0)
            affine1(0)
            take_kvr(0)
            round_(0, False, True)
            with act.Fori(1, NB - 1) as b:
                round_(b, True, True)
            round_(NB - 1, True, False)
            relus(NB - 1, 0, HC)
            square(NB - 1, HC - 1)
            sigmoid_fr(NB - 1)

            def gelu(t, i):
                if not (isinstance(t, int) and t < 2):
                    wait_run(act, S["hgT_done"], t - 1)
                act.wait_ge(S["h_done"], t + 1)
                act.activation(hg[i], psM[:, i, :], ACT.Gelu).then_inc(S["gelu_done"], 1)

            def take_y(t, i, stored):
                if stored is not None:
                    wait_run(act, S[f"y_out{i}"], stored)
                act.wait_ge(S["y_done"], t + 1)
                act.activation(y_t[i], y_ps[i], ACT.Copy).then_inc(S["y_ready"], 1)

            gelu(0, 0)
            gelu(1, 1)
            gelu(2, 0)
            take_y(0, 0, None)
            gelu(3, 1)
            take_y(1, 1, None)
            gelu(4, 0)
            take_y(2, 0, 16)
            with act.Fori(2, NT // 2 - 1) as g:
                gelu(2 * g + 1, 1)
                take_y(2 * g - 1, 1, g * 16 - 16)
                gelu(2 * g + 2, 0)
                take_y(2 * g, 0, g * 16)
            gelu(NT - 1, 1)
            take_y(NT - 3, 1, (NT - 4) // 2 * 16)
            take_y(NT - 2, 0, (NT - 2) // 2 * 16)
            take_y(NT - 1, 1, (NT - 2) // 2 * 16)

            def silu(b, i, g):
                act.wait_ge(S[f"gathered{i}"], g * (16 * J) + 16 * J)
                wait_run(act, S["d_fetched"], b + 1)
                for j in range(J):
                    ins = act.activation(yg[i][:, j], yg[i][:, j], ACT.Silu, scale=g_gate[i][:, j:j + 1])
                ins.then_inc(S["d_silu"], 1)

            with act.Fori(0, NB // 2) as g:
                for i in range(2):
                    silu(2 * g + i, i, g)

        @block.tensor
        def _(pe):
            pe.wait_ge(S["consts_in"], 48)
            pe.wait_ge(S["wg_in"], 16)
            for k in range(CH):
                ins = pe.matmul(psR[:, 0:E], ones, wg_sb[:, k * E:(k + 1) * E], start=(k == 0), stop=(k == CH - 1))
            ins.then_inc(S["wg_mean"], 1)
            pe.wait_ge(S["wg_ready"], 1)

            def router(g, first):
                for i in range(2):
                    pe.wait_ge(S[f"xta_in{i}"], g * 16 + 16)
                    if not first:
                        pe.wait_ge(S["logits_copied"], 2 * g + (i - 1))
                    for k in range(CH):
                        ins = pe.matmul(psM[0:E, i, :], wgc[:, k * E:(k + 1) * E], xta[i][:, k, :],
                                        start=(k == 0), stop=(k == CH - 1))
                    ins.then_inc(S["logits_done"], 1)
                for i in range(2):
                    wait_run(pe, S["logits_copied"], 2 * g + (i + 1))
                    if not first:
                        wait_run(pe, S["logits_kept"], 2 * g + (i - 1))
                    for j in range(J):
                        ins = pe.transpose(psKV[:, i, j * E:(j + 1) * E], lgT[i][:, j * P:(j + 1) * P],
                                           ident[0:E, 0:E])
                    ins.then_inc(S["logitsT_done"], 1)

            router(0, True)
            with pe.Fori(1, NB // 2) as g:
                router(g, False)
            pe.wait_ge(S["route_step"], R_PEXP)
            for j in range(J):
                ins = pe.transpose(psT[:, 0, j * P:(j + 1) * P], pexp[:, j * P:(j + 1) * P], ident)
            ins.then_inc(S["route_pe"], 1)
            with pe.Fori(0, BITS) as k:
                pe.wait_ge(S["bit_counted"], k + 1)
                pe.matmul(psR[:, 0:1], esum, tiny[:, 4:5], start=True, stop=True).then_inc(S["bit_summed"], 1)
            pe.wait_ge(S["route_step"], R_COUNTS)
            pe.matmul(psR[:, 0:1], esum, tiny[:, 5:6], start=True, stop=True)
            pe.matmul(psR[:, 1:2], eprefix, tiny[:, 6:7], start=True, stop=True).then_inc(S["route_pe"], 1)
            pe.wait_ge(S["route_step"], R_SEL)
            for j in range(J):
                ins = pe.transpose(psT[:, 1, j * P:(j + 1) * P], oneT[:, j * P:(j + 1) * P], ident)
            ins.then_inc(S["route_pe"], 1)
            pe.wait_ge(S["route_step"], R_ONEHOT)
            pe.matmul(psM[:, 0, :], prefix, pexp, start=True, stop=True)
            pe.matmul(psM[:, 1, :], ones, pexp, start=True, stop=True).then_inc(S["route_pe"], 1)

            def turn(b, ready, done):
                wait_run(pe, S[ready], b + 1)
                for c in range(CH):
                    for j in range(J):
                        ins = pe.transpose(psT[:, c, j * P:(j + 1) * P], hn[:, j, c * P:(c + 1) * P], ident)
                ins.then_inc(S[done], 1)

            def turn1(b):
                if not (isinstance(b, int) and b < 2):
                    wait_run(pe, S["h2_ready"], CH * b - CH)
                turn(b, "hn1_ready", "tr1_done")

            def turn2(b):
                wait_run(pe, S["h1_ready"], CH * b + 2 * CH) if not (isinstance(b, int) and b == NB - 1) else None
                turn(b, "hn2_ready", "tr2_done")

            def project(b):
                for m, w in enumerate((wk, wv, wr)):
                    pe.wait_ge(S["mix1_done"], 3 * b + (m + 1))
                    for c in range(CH):
                        u = m * CH + c
                        if u >= 3:
                            pe.wait_ge(S["kvr_ready"], b * (3 * CH) + (u - 2))
                        elif not (isinstance(b, int) and b == 0):
                            if u == 0:
                                wait_run(pe, S["kvr_ready"], b * (3 * CH))
                                if not (isinstance(b, int) and b == 1):
                                    wait_run(pe, S["sigf_done"], 2 * b - 2)
                            else:
                                wait_run(pe, S["x2_done"], b)
                        for k in range(CH):
                            ins = pe.matmul(psM[:, u % 3, :], w[:, k, c * P:(c + 1) * P], mixA[:, m, k, :],
                                            start=(k == 0), stop=(k == CH - 1))
                        ins.then_inc(S["proj_done"], 1)

            def project_out(b):
                wait_run(pe, S["att_done"], CH * b + CH)
                if not (isinstance(b, int) and b == 0):
                    wait_run(pe, S["relu_done"], HC * b)
                    wait_run(pe, S["sigf_done"], 2 * b - 1)
                for j in range(J):
                    for c in range(CH):
                        ins = pe.matmul(psM[:, 1 + j // 2, (j % 2) * C:(j % 2 + 1) * C],
                                        att[:, c, j * P:(j + 1) * P], wo[:, c, :], start=(c == 0), stop=(c == CH - 1))
                ins.then_inc(S["o_done"], 1)

            def hidden(b):
                wait_run(pe, S["mix2_done"], 2 * b + 1)
                for h in range(HC):
                    if h < 3:
                        if isinstance(b, int) and b == NB - 1:
                            pe.wait_ge(S["x2_done"], NB)
                            pe.wait_ge(S["sigf_done"], 2 * NB - 2)
                        else:
                            wait_run(pe, S["kvr_ready"], b * (3 * CH) + (3 * CH + 4 + h))
                    else:
                        pe.wait_ge(S["relu_done"], b * HC + (h - 2))
                    for k in range(CH):
                        ins = pe.matmul(psM[:, h % 3, :], wfk[:, k, h * P:(h + 1) * P], mixB[:, 0, k, :],
                                        start=(k == 0), stop=(k == CH - 1))
                    ins.then_inc(S["kf_done"], 1)

            def receptance(b):
                wait_run(pe, S["mix2_done"], 2 * b + 2)
                for u in range(2):
                    pe.wait_ge(S["relu_done"], b * HC + (HC + u - 2))
                    for j in (2 * u, 2 * u + 1):
                        for k in range(CH):
                            ins = pe.matmul(psM[:, (HC + u) % 3, (j % 2) * C:(j % 2 + 1) * C],
                                            mixB[:, 1, k, j * P:(j + 1) * P], wfr[:, k, :],
                                            start=(k == 0), stop=(k == CH - 1))
                    ins.then_inc(S["fr_done"], 1)

            def channel_out(b, j):
                if j == 0:
                    pe.wait_ge(S["sq_done"], b * HC + HC)
                    wait_run(pe, S["mix2_done"], 2 * b + 2)
                for h in range(HC):
                    ins = pe.matmul(psKV[:, j // 2, (j % 2) * C:(j % 2 + 1) * C], kf2[:, h, j * P:(j + 1) * P],
                                    wfv[:, h, :], start=(h == 0), stop=(h == HC - 1))
                ins.then_inc(S["kv_done"], 1)

            def round_(b, ffn, ahead):
                if ffn:
                    hidden(b - 1)
                    receptance(b - 1)
                    channel_out(b - 1, 0)
                    channel_out(b - 1, 1)
                project_out(b)
                if ahead:
                    turn1(b + 1)
                if ffn:
                    channel_out(b - 1, 2)
                    channel_out(b - 1, 3)
                turn2(b)
                if ahead:
                    project(b + 1)

            pe.wait_ge(S["weights_in"], 16 * 7)
            turn1(0)
            project(0)
            round_(0, False, True)
            with pe.Fori(1, NB - 1) as b:
                round_(b, True, True)
            round_(NB - 1, True, False)
            hidden(NB - 1)
            receptance(NB - 1)
            for j in range(J):
                channel_out(NB - 1, j)

            def weights_of(t):
                src = expert_at[0:1, t:t + 1] if isinstance(t, int) else expert_at[0:1, ds(t, 1)]
                return pe.value_load(src, min_val=0, max_val=(E - 1) * CH * F)

            def turn_x(t, i, load_count):
                pe.wait_ge(S[f"xs_in{i}"], load_count)
                if not (isinstance(t, int) and t < 2):
                    pe.wait_ge(S["xsT_ready"], t - 1)
                for k in range(CH):
                    ins = pe.transpose(psT[:, i, k * P:(k + 1) * P], xs_t[i][:, k * P:(k + 1) * P], ident)
                ins.then_inc(S["xsT_done"], 1)

            def mlp_in(t, i):
                w = weights_of(t)
                wait_run(pe, S["xsT_ready"], t + 1)
                if not (isinstance(t, int) and t < 2):
                    wait_run(pe, S["gelu_done"], t - 1)
                for k in range(CH):
                    ins = pe.matmul(psM[:, i, :], xsT[i][:, k, :], w1_sb[:, ds(w + k * F, F)],
                                    start=(k == 0), stop=(k == CH - 1))
                ins.then_inc(S["h_done"], 1)

            def turn_h(t, i):
                pe.wait_ge(S["gelu_done"], t + 1)
                if not (isinstance(t, int) and t < 2):
                    pe.wait_ge(S["hgT_ready"], t - 1)
                for k in range(FK):
                    ins = pe.transpose(psKV[:, i, k * P:(k + 1) * P], hg[i][:, k * P:(k + 1) * P], ident)
                ins.then_inc(S["hgT_done"], 1)

            def mlp_out(t, i):
                w = weights_of(t)
                wait_run(pe, S["hgT_ready"], t + 1)
                if not (isinstance(t, int) and t < 2):
                    wait_run(pe, S["y_ready"], t - 1)
                for k in range(FK):
                    ins = pe.matmul(y_ps[i], hgT[i][:, k, :], w2_sb[:, ds(w + k * C, C)],
                                    start=(k == 0), stop=(k == FK - 1))
                ins.then_inc(S["y_done"], 1)

            pe.wait_ge(S["s_done"], NB)
            pe.wait_ge(S["moe_w_in"], 16 * 2 * E)
            turn_x(0, 0, 16)
            turn_x(1, 1, 16)
            mlp_in(0, 0)
            turn_x(2, 0, 32)
            mlp_in(1, 1)
            turn_h(0, 0)
            turn_x(3, 1, 32)
            mlp_in(2, 0)
            turn_h(1, 1)
            mlp_out(0, 0)
            with pe.Fori(1, NT // 2 - 1) as g:
                turn_x(2 * g + 2, 0, g * 16 + 32)
                mlp_in(2 * g + 1, 1)
                turn_h(2 * g, 0)
                mlp_out(2 * g - 1, 1)
                turn_x(2 * g + 3, 1, g * 16 + 32)
                mlp_in(2 * g + 2, 0)
                turn_h(2 * g + 1, 1)
                mlp_out(2 * g, 0)
            mlp_in(NT - 1, 1)
            turn_h(NT - 2, 0)
            mlp_out(NT - 3, 1)
            turn_h(NT - 1, 1)
            mlp_out(NT - 2, 0)
            mlp_out(NT - 1, 1)

        @block.vector
        def _(v):
            v.wait_ge(S["decay_exp"], 1)
            v.tensor_scalar(wneg[:], wneg[:], -1.0, None, ALU.mult)
            v.tensor_scalar(uneg[:], vecs[:, :, V["first"]], -1.0, None, ALU.mult)
            v.wait_ge(S["wg_mean"], 1)
            for k in range(CH):
                ins = v.scalar_tensor_tensor(wgc[:, k * E:(k + 1) * E], psR[:, 0:E], -1.0 / C,
                                             wg_sb[:, k * E:(k + 1) * E], ALU.mult, ALU.add)
            ins.then_inc(S["wg_ready"], 1)

            def statistics(b, i, g):
                st = Steps(v, S["a_step"], 2, b, S["waited"])
                v.wait_ge(S[f"xa_in{i}"], g * 16 + 16)
                for j in range(J):
                    ins = v.bn_stats(bnst[:, j], xa[i][:, j])
                ins.then_inc(S["a_stats"], 1)
                wait_run(v, S["a_stats"], b + 1)
                for j in range(J):
                    ins = v.bn_aggr(mv1[:, j], bnst[:, j])
                st.then(ins)
                st.wait()
                st.then(v.tensor_copy(mvA[:, ds(b * (2 * J), 2 * J)], mv1[:].rearrange("p j s -> p (j s)")))
                st.wait()
                st.end()

            def keep_logits(b, i):
                wait_run(v, S["logitsT_done"], b + 1)
                v.tensor_copy(logits[:, ds(b * (J * E), J * E)], psKV[:, i, 0:J * E]).then_inc(S["logits_kept"], 1)

            with v.Fori(0, NB // 2) as g:
                for i in range(2):
                    statistics(2 * g + i, i, g)
                for i in range(2):
                    keep_logits(2 * g + i, i)
            v.memset(tiny[:, 0:1], 0.0)
            v.memset(tiny[:, 1:2].bitcast(I32), 1 << 29)
            v.memset(reset, 1.0).then_inc(S["var_ready"], 1)

            R = Steps(v, S["route_step"], R_ALL, 0, S["waited"])
            te = lambda a: a.rearrange("p (t e) -> p t e", e=E)
            et = lambda a: a.rearrange("p (e t) -> p e t", e=E)
            over_e = lambda a: a.rearrange("p (t o) -> p t o", o=1).to_broadcast([P, NTILE, E])
            sm = lambda k: small[:, k * NTILE:(k + 1) * NTILE]
            v.wait_ge(S["logits_kept"], NB)
            v.wait_ge(S["var_ready"], 1)
            R.then(v.memset(et(reset)[:, :, 0], 0.0))
            v.wait_ge(S["pow_ready"], 8)
            R.then(v.tensor_tensor(te(logits), te(logits), tok_stats[:, :, 2:3].to_broadcast([P, NTILE, E]), ALU.mult))
            R.wait()
            R.then(v.tensor_reduce(sm(6), te(logits), AX_X, ALU.max))
            R.wait()
            v.tensor_tensor(te(logits), te(logits), over_e(sm(6)), ALU.subtract).then_inc(S["route_exp_in"], 1)
            v.wait_ge(S["route_exp_out"], 1)
            R.then(v.tensor_reduce(sm(7), te(probs), AX_X, ALU.add))
            R.wait()
            R.then(v.reciprocal(sm(6), sm(7)))
            R.wait()
            R.then(v.tensor_tensor(te(probs), te(probs), over_e(sm(6)), ALU.mult))
            R.wait()
            R.then(v.tensor_copy(pexp.rearrange("p (j t e) -> p j t e", j=J, e=E),
                                 probs.rearrange("p (t j e) -> p j t e", j=J, e=E)))
            assert R.k == R_PEXP
            v.wait_ge(S["route_pe"], 1)
            R.then(v.tensor_copy(selT, psT[:, 0, :]))
            R.wait()
            t_f, bit, cand, kept, cnt = (tiny[:, k:k + 1] for k in range(5))
            with v.Fori(0, BITS) as k:
                B = Steps(v, S["bit_step"], 3, k, S["waited"])
                B.then(v.tensor_tensor(cand.bitcast(I32), t_f.bitcast(I32), bit.bitcast(I32), ALU.bitwise_or))
                B.wait()
                v.tensor_scalar(work, selT, cand, None, ALU.is_ge, ALU.add, accum_out=cnt).then_inc(S["bit_counted"], 1)
                v.tensor_scalar(bit.bitcast(I32), bit.bitcast(I32), 1, None, ALU.logical_shift_right)
                v.wait_ge(S["bit_summed"], k + 1)
                v.wait_ge(S["bit_counted"], k + 1)
                B.then(v.scalar_tensor_tensor(kept, psR[:, 0:1], float(CAP), cand, ALU.is_ge, ALU.mult))
                B.wait()
                B.then(v.tensor_tensor(t_f, t_f, kept, ALU.max))
                B.wait()
                B.end()
            v.tensor_scalar(oneT, selT, t_f, None, ALU.is_gt, ALU.add, accum_out=tiny[:, 5:6])
            R.then(v.tensor_scalar(work, selT, t_f, None, ALU.is_equal, ALU.add, accum_out=tiny[:, 6:7]))
            R.wait()
            R_c = R.k
            assert R_c == R_COUNTS, R_c
            R.then(v.tensor_tensor_scan(win, ones[:, 0:1].to_broadcast([P, SEQ]), work, 0.0, ALU.mult, ALU.add))
            v.wait_ge(S["route_pe"], 2)
            R.then(v.tensor_scalar(tiny[:, 7:8], psR[:, 0:1], -1.0, float(CAP), ALU.mult, ALU.add))
            R.wait()
            R.then(v.tensor_tensor(tiny[:, 8:9], tiny[:, 7:8], psR[:, 1:2], ALU.subtract))
            R.wait()
            R.then(v.scalar_tensor_tensor(win, win, tiny[:, 8:9], work, ALU.is_le, ALU.mult))
            R.wait()
            R.then(v.tensor_tensor(oneT, oneT, win, ALU.add))
            assert R.k == R_SEL
            v.wait_ge(S["route_pe"], 3)
            R.then(v.tensor_copy(work.rearrange("p (t j e) -> p j t e", j=J, e=E),
                                 psT[:, 1, :].rearrange("p (j t e) -> p j t e", j=J, e=E)))
            R.wait()
            R.then(v.tensor_reduce(sm(6), te(work), AX_X, ALU.max))
            R.wait()
            R.then(v.tensor_scalar(sm(7), sm(6), 0.5, None, ALU.is_lt))
            R.wait()
            R.then(v.tensor_tensor(te(work), te(work), over_e(sm(7)), ALU.max))
            R.wait()
            R.then(v.tensor_tensor(win, probs, work, ALU.mult))
            R.then(v.tensor_scalar(mask8, work, -1.0, None, ALU.add))
            R.wait()
            R.then(v.tensor_tensor(win, win, mask8, ALU.add))
            R.wait()
            R.then(v.tensor_reduce(gate[:], te(win), AX_X, ALU.max))
            R.wait()
            R.then(v.tensor_tensor(te(work), te(win), over_e(gate[:]), ALU.is_equal))
            R.wait()
            R.then(v.tensor_tensor(te(work), te(work),
                                   erev.rearrange("p (o e) -> p o e", o=1).to_broadcast([P, NTILE, E]), ALU.mult))
            R.wait()
            R.then(v.tensor_reduce(sm(6), te(work), AX_X, ALU.max))
            R.wait()
            R.then(v.tensor_tensor(te(pexp), te(work), over_e(sm(6)), ALU.is_equal))
            assert R.k == R_ONEHOT
            v.wait_ge(S["route_pe"], 4)
            R.then(v.tensor_copy(et(logits), psM[:, 1, :].rearrange("p (t e) -> p e t", e=E)))
            R.wait()
            R.then(v.tensor_tensor_scan(work, reset, logits, 0.0, ALU.mult, ALU.add))
            R.wait()
            c8 = lambda k: tiny[:, 16 + k * E:16 + (k + 1) * E]
            R.then(v.tensor_scalar(c8(0).bitcast(I32), et(work)[:, :, NTILE - 1], float(P - 1), None, ALU.add))
            R.wait()
            R.then(v.tensor_scalar(c8(1).bitcast(I32), c8(0).bitcast(I32), 7, None, ALU.logical_shift_right))
            R.wait()
            R.then(v.tensor_copy(c8(2), c8(1).bitcast(I32)))
            R.wait()
            R.then(v.tensor_tensor_scan(c8(3), ones[:, 0:E], c8(2), 0.0, ALU.mult, ALU.add))
            R.wait()
            R.then(v.tensor_tensor(c8(4), c8(3), c8(2), ALU.subtract))
            R.wait()
            R.then(v.tensor_scalar(c8(5), c8(4), float(P), -1.0, ALU.mult, ALU.add))
            R.then(v.tensor_tensor(work, work, logits, ALU.subtract))
            R.wait()
            R.then(v.tensor_tensor(et(work), et(work), c8(5).rearrange("p (e o) -> p e o", o=1).to_broadcast([P, E, NTILE]),
                                   ALU.add))
            R.wait()
            R.then(v.tensor_tensor(te(win), te(psM[:, 0, :]), work.rearrange("p (e t) -> p t e", e=E), ALU.add))
            R.wait()
            R.then(v.tensor_tensor(win, win, pexp, ALU.mult))
            R.wait()
            R.then(v.tensor_reduce(sm(6), te(win), AX_X, ALU.add))
            R.wait()
            R.then(v.tensor_copy(slot_i[:], sm(6)))
            tw3 = tw[0:1, :].rearrange("p (n e) -> p n e", e=E)
            R.then(v.tensor_tensor(tw3, iota_sb[0:1, :].rearrange("p (n o) -> p n o", o=1).to_broadcast([1, NT, E]),
                                   c8(3)[0:1, :].rearrange("p (o e) -> p o e", o=1).to_broadcast([1, NT, E]), ALU.is_ge))
            R.wait()
            R.then(v.tensor_reduce(win[0:1, 0:NT], tw3, AX_X, ALU.add))
            R.wait()
            R.then(v.tensor_scalar(expert_at[:], win[0:1, 0:NT], float(E - 1), float(CH * F), ALU.min, ALU.mult))
            R.wait()
            v.memset(hT[:, :, 0:1], 0.0)
            v.memset(pp[:, 0:1], -1e38)
            v.memset(aa[:, 0:1], 0.0)
            R.then(v.memset(bb[:, 0:1], 0.0))
            R.wait()
            v.tensor_copy(tiny[:, 60:61], tiny[:, 0:1]).then_inc(S["routed"], 1)
            R.end()
            wait_run(v, S["zeros_out"], 16 * (NT // J))
            wait_run(v, S["routed"], 1)

            def fetch(b):
                if not (isinstance(b, int) and b == 0):
                    wait_run(v, S["xn_ready"], b)
                    wait_run(v, S["scattered"], b * (16 * J))
                v.tensor_copy(stats_cur[:].rearrange("p j s -> p (j s)"),
                              tok_stats[:].rearrange("p t s -> p (t s)")[:, ds(b * (4 * J), 4 * J)])
                v.tensor_copy(slot_cur[:], slot_i[:, ds(b * J, J)]).then_inc(S["fetched"], 1)

            def moments(b, mv, st, ready):
                xs = tile_row(b)
                for j in range(J):
                    ins = v.bn_stats(bnst[:, j], xs[:, j * C:(j + 1) * C])
                st.then(ins)
                st.wait()
                for j in range(J):
                    ins = v.bn_aggr(mv[:, j], bnst[:, j])
                ins.then_inc(S[ready], 1)

            def embed(b):
                st = Steps(v, S["embed_step"], 3, b, S["waited"])
                wait_run(v, S["x0_ready"], b + 1)
                over_j = lambda a: a[:].rearrange("p (o c) -> p o c", o=1).to_broadcast([P, J, C])
                st.then(v.tensor_tensor(hn, hn, over_j(w0_bc), ALU.mult))
                st.wait()
                st.then(v.tensor_tensor(tile_row(b).rearrange("p (j c) -> p j c", j=J), hn, over_j(b0_bc), ALU.add))
                st.wait()
                moments(b, mv1, st, "ln1_stats")
                st.end()

            def mix(b, ready, step, outs, done):
                st = Steps(v, S[step], 1, b, S["waited"])
                for c in range(CH):
                    v.wait_ge(S[ready], CH * b + (c + 1))
                    ins = v.tensor_tensor(dmix[:, c], hT[:, c, 1:SEQ + 1], hT[:, c, 0:SEQ], ALU.subtract)
                st.then(ins)
                st.wait()
                for dst, m in outs:
                    for c in range(CH):
                        ins = v.scalar_tensor_tensor(dst[:, c], dmix[:, c], vecs[:, c, V[m]:V[m] + 1],
                                                     hT[:, c, 0:SEQ], ALU.mult, ALU.add)
                    ins.then_inc(S[done], 1)
                st.end()

            def mix1(b):
                if not (isinstance(b, int) and b == 0):
                    wait_run(v, S["mix2_done"], 2 * b - 2) if not (isinstance(b, int) and b == 1) else None
                mix(b, "h1_ready", "mix1_step", [(mixA[:, 0], "tmk"), (mixA[:, 1], "tmv"), (mixA[:, 2], "tmr")],
                    "mix1_done")

            def mix2(b):
                if not (isinstance(b, int) and b == NB - 1):
                    wait_run(v, S["mix1_done"], 3 * b + 6)
                mix(b, "h2_ready", "mix2_step", [(mixB[:, 0], "cmk"), (mixB[:, 1], "cmr")], "mix2_done")

            def wkv_before(b, c, st):
                k = kvs[:, 0, c, :]
                v.wait_ge(S["kvr_ready"], b * (3 * CH) + (c + 1))
                st.then(v.tensor_tensor_scan(pp[:, 1:SEQ + 1], wneg[:, c:c + 1].to_broadcast([P, SEQ]), k, -1e38,
                                             ALU.add, ALU.max))
                st.wait()
                st.then(v.tensor_tensor(qb[c], pp[:, 0:SEQ], k, ALU.subtract))
                st.wait()
                w, u = wneg[:, c:c + 1], uneg[:, c:c + 1]
                v.tensor_scalar(E1[c][:, 0], qb[c], w, 0.0, ALU.add, ALU.min)
                v.tensor_scalar(E1[c][:, 1], qb[c], u, 0.0, ALU.add, ALU.min)
                v.tensor_scalar(E2[c][:, 0], qb[c], w, 0.0, ALU.add, ALU.max)
                v.tensor_scalar(E2[c][:, 1], qb[c], u, 0.0, ALU.add, ALU.max).then_inc(S["pre_done"], 1)

            def wkv_after(b, c, st):
                e1, f1, e2, f2 = E1[c][:, 0], E1[c][:, 1], E2[c][:, 0], E2[c][:, 1]
                val = kvs[:, 1, c, :]
                v.wait_ge(S["exp_done"], b * (2 * CH) + (2 * c + 2))
                v.wait_ge(S["kvr_ready"], b * (3 * CH) + (CH + c + 1))
                v.tensor_tensor_scan(bb[:, 1:SEQ + 1], e1, e2, 0.0, ALU.mult, ALU.add)
                st.then(v.tensor_tensor(evb[c], e2, val, ALU.mult))
                st.wait()
                v.tensor_tensor_scan(aa[:, 1:SEQ + 1], e1, evb[c], 0.0, ALU.mult, ALU.add)
                v.tensor_tensor(t1b[c], f2, val, ALU.mult)
                st.then(v.tensor_tensor(qb[c], f1, bb[:, 0:SEQ], ALU.mult))
                st.wait()
                v.tensor_tensor(e1, f1, aa[:, 0:SEQ], ALU.mult)
                st.then(v.tensor_tensor(qb[c], qb[c], f2, ALU.add))
                st.wait()
                v.reciprocal(e2, qb[c])
                st.then(v.tensor_tensor(e1, e1, t1b[c], ALU.add))
                st.wait()
                st.then(v.tensor_tensor(e1, e1, e2, ALU.mult))
                st.wait()
                v.wait_ge(S["kvr_ready"], b * (3 * CH) + (2 * CH + c + 1))
                v.tensor_tensor(att[:, c], e1, kvs[:, 2, c, :], ALU.mult).then_inc(S["att_done"], 1)

            def wkv(b):
                st = Steps(v, S["wkv_step"], 14, b, S["waited"])
                for c in range(CH):
                    wkv_before(b, c, st)
                for c in range(CH):
                    if c == 0 and not (isinstance(b, int) and b == 0):
                        wait_run(v, S["o_done"], b)
                    wkv_after(b, c, st)
                st.end()

            def residual1(b):
                st = Steps(v, S["ln2_step"], 1, b, S["waited"])
                v.wait_ge(S["o_done"], b + 1)
                xs = tile_row(b)
                v.tensor_tensor(xs, xs, psM[:, 1:3, :].rearrange("p b n -> p (b n)"), ALU.add).then_inc(S["x2_done"], 1)
                wait_run(v, S["x2_done"], b + 1)
                moments(b, mv2, st, "ln2_stats")
                st.end()

            def residual2(b):
                st = Steps(v, S["s_step"], 1, b, S["waited"])
                v.wait_ge(S["kv_done"], J * b + J)
                v.wait_ge(S["sigf_done"], 2 * b + 2)
                st.then(v.tensor_tensor(sigf, sigf, psKV[:].rearrange("p b n -> p (b n)"), ALU.mult))
                st.wait()
                xs = tile_row(b)
                v.tensor_tensor(xs, xs, sigf, ALU.add).then_inc(S["s_done"], 1)
                st.end()

            def round_(b, ffn, ahead):
                if ahead:
                    fetch(b + 1)
                wkv(b)
                if ahead:
                    embed(b + 1)
                residual1(b)
                if ahead:
                    mix1(b + 1)
                if ffn:
                    residual2(b - 1)
                mix2(b)

            fetch(0)
            embed(0)
            mix1(0)
            round_(0, False, True)
            with v.Fori(1, NB - 1) as b:
                round_(b, True, True)
            round_(NB - 1, True, False)
            residual2(NB - 1)

            def take_xT(t, i):
                if not (isinstance(t, int) and t < 2):
                    v.wait_ge(S["h_done"], t - 1)
                v.wait_ge(S["xsT_done"], t + 1)
                v.tensor_copy(xsT[i].rearrange("p k t -> p (k t)"), psT[:, i, 0:C]).then_inc(S["xsT_ready"], 1)

            def take_hT(t, i):
                if not (isinstance(t, int) and t < 2):
                    v.wait_ge(S["y_done"], t - 1)
                v.wait_ge(S["hgT_done"], t + 1)
                v.tensor_copy(hgT[i].rearrange("p k t -> p (k t)"), psKV[:, i, :]).then_inc(S["hgT_ready"], 1)

            take_xT(0, 0)
            take_xT(1, 1)
            take_xT(2, 0)
            take_hT(0, 0)
            take_xT(3, 1)
            take_hT(1, 1)
            with v.Fori(1, NT // 2 - 1) as g:
                for i in range(2):
                    take_xT(2 * g + (2 + i), i)
                    take_hT(2 * g + i, i)
            take_hT(NT - 2, 0)
            take_hT(NT - 1, 1)

            def fetch_d(b, i, first):
                if not first:
                    wait_run(v, S["d_silu"], b - 1)
                v.tensor_copy(g_gate[i][:], gate[:, ds(b * J, J)])
                v.tensor_copy(g_slot[i][:], slot_i[:, ds(b * J, J)]).then_inc(S["d_fetched"], 1)

            def combine(b, i, g):
                st = Steps(v, S["d_step"], 1, b, S["waited"])
                v.wait_ge(S["d_silu"], b + 1)
                y = yg[i].rearrange("p j c -> p (j c)")
                xf = xd[i].rearrange("p j c -> p (j c)")
                st.then(v.tensor_tensor(y, y, tile_row(b), ALU.mult))
                v.wait_ge(S[f"d_x_in{i}"], g * 16 + 16)
                st.wait()
                v.tensor_tensor(xf, xf, y, ALU.add).then_inc(S["d_ready"], 1)
                st.end()

            for i in range(2):
                fetch_d(i, i, True)
            with v.Fori(0, NB // 2 - 1) as g:
                for i in range(2):
                    combine(2 * g + i, i, g)
                    wait_run(v, S["d_ready"], 2 * g + (i + 1))
                    fetch_d(2 * g + (2 + i), i, False)
            for i in range(2):
                combine(NB - 2 + i, i, NB // 2 - 1)


def kernel(**inputs):
    import numpy as np
    import concourse.bacc as bacc
    from concourse.bass_utils import run_bass_kernel_spmd

    a = {k: np.asarray(v) for k, v in inputs.items()}
    x = np.ascontiguousarray(a["L0_attn_x"]).reshape(-1, a["L0_attn_x"].shape[-1])
    T, C = x.shape
    E = a["L0_ffn_Wg"].shape[1]
    names = dict(ln1_w="ln1_w", ln1_b="ln1_b", ln2_w="ln2_w", ln2_b="ln2_b", decay="time_decay",
                 first="time_first", tmk="tmk", tmv="tmv", tmr="tmr", cmk="cmk", cmr="cmr")
    p = np.arange(P)
    same = p[:, None] % E == p[None, :] % E
    consts = np.concatenate([
        p[:, None] == p[None, :], same, same & (p[:, None] < p[None, :]), p[:, None] <= p[None, :],
        np.ones((P, P)), np.broadcast_to(E - np.arange(E), (P, E))], axis=1).astype(np.float32)
    NT = T // P + E
    arrays = {
        "x": x,
        "xT": np.ascontiguousarray(x.T),
        "vec": np.stack([a["L0_attn_" + names[n]] for n in PARAMS], axis=1),
        "ln0_w": a["L0_attn_ln0_w"],
        "ln0_b": a["L0_attn_ln0_b"],
        **{n + "T": np.ascontiguousarray(a["L0_attn_" + n].T) for n in ("Wk", "Wv", "Wr", "Wo", "Wfk", "Wfr", "Wfv")},
        "Wg": a["L0_ffn_Wg"],
        "W1": a["L0_ffn_W1"],
        "W2": a["L0_ffn_W2"],
        "consts": consts,
        "tile_iota": np.arange(NT, dtype=np.float32)[None, :],
    }
    nc = bacc.Bacc("TRN2", target_bir_lowering=False, num_devices=1)
    feeds = {f"in_{n}": np.ascontiguousarray(v) for n, v in arrays.items()}
    args = [nc.dram_tensor(n, v.shape, mybir.dt.from_np(v.dtype), kind="ExternalInput").ap() for n, v in feeds.items()]
    args.append(nc.dram_tensor("slots_sorted", (NT * P, C), F32, kind="Internal").ap())
    args.append(nc.dram_tensor("moe_out", (NT * P, C), F32, kind="Internal").ap())
    args.append(nc.dram_tensor("out_0_dram", (T, C), F32, kind="ExternalOutput").ap())
    rwkv_times_moe(nc, *args)
    r = run_bass_kernel_spmd(nc, [feeds], core_ids=[0])
    return r.results[0]["out_0_dram"].reshape(a["L0_attn_x"].shape)
```

```python
from contextlib import ExitStack

import concourse.bass as bass
from concourse import mybir

F32 = mybir.dt.float32
I32 = mybir.dt.int32
ALU = mybir.AluOpType
ACT = mybir.ActivationFunctionType
AX_X = mybir.AxisListType.X
ds = bass.ds

P = 128
ROUTER_ROUNDS = 3
BIT_ROUND = 4
SELECT_ROUND = BIT_ROUND + 7
LIST_ROUND = SELECT_ROUND + 1
RING = 6
R_PEXP, R_COUNTS, R_SEL, R_ONEHOT, R_KEPT, R_ALL = 9, 13, 18, 30, 31, 54
PARAMS = ["ln1_w", "ln1_b", "ln2_w", "ln2_b", "decay", "first", "tmk", "tmv", "tmr", "cmk", "cmr"]


class Steps:

    def __init__(self, eng, sem, per_run, run, waited):
        self.eng, self.sem, self.per_run, self.run, self.waited = eng, sem, per_run, run, waited
        self.k = 0

    def then(self, ins):
        ins.then_inc(self.sem, 1)
        self.k += 1
        return self.k

    def wait(self, k=None):
        self.eng.wait_ge(self.sem, self.run * self.per_run + (self.k if k is None else k))
        if not isinstance(self.run, int):
            self.eng.sem_inc(self.waited)

    def end(self):
        assert self.k == self.per_run, (self.k, self.per_run)


def rwkv_times_moe(nc, x, xT, vec, ln0_w, ln0_b, WkT, WvT, WrT, WoT, WfkT, WfrT, WfvT, Wg, W1, W2,
                   consts, tile_iota, token_ids, pad_rows, sorted_list, xs_rows, out):
    T, C = x.shape
    SEQ = 512
    NB = T // SEQ
    CH = C // P
    J = SEQ // P
    NTILE = T // P
    HID = WfkT.shape[1]
    HC = HID // P
    E, _, F = W1.shape
    FK = F // P
    CAP = max(1, T // E)
    EPS = 1e-5
    NT = sorted_list.shape[0] // P
    NCH = NTILE // J
    LT = NTILE // (NB - LIST_ROUND)
    assert CH == 2 and J == 4 and E * NCH == P and NT >= NTILE + E - 1 and NT % RING == 0
    assert NB == 4 * (ROUTER_ROUNDS + 1) and BIT_ROUND == ROUTER_ROUNDS + 1 and NTILE % LT == 0

    with ExitStack() as ctx:
        def sb(name, shape, dt=F32):
            return ctx.enter_context(nc.sbuf_tensor(name, shape, dt))

        def sem(name):
            return ctx.enter_context(nc.semaphore(name))

        s_ring = sb("s_ring", [P, 4 * J * C])
        vecs = sb("vecs", [P, CH, len(PARAMS)])
        V = {n: i for i, n in enumerate(PARAMS)}
        wneg = sb("wneg", [P, CH])
        uneg = sb("uneg", [P, CH])
        w0_bc = sb("w0_bc", [P, C])
        b0_bc = sb("b0_bc", [P, C])
        cst = sb("cst", [P, 5, P])
        ident, esum, eprefix, prefix, ones = (cst[:, i, :] for i in range(5))
        stats0 = sb("stats0", [P, NTILE, 2])
        info = sb("info", [P, NTILE, 4])
        place = sb("place", [P, NTILE], I32)
        expert_at = sb("expert_at", [1, NT], I32)
        stats_cur = sb("stats_cur", [P, J, 2])
        place_cur = sb("place_cur", [P, LT], I32)
        info_cur = sb("info_cur", [P, LT, 4], I32)
        bnst = sb("bnst", [P, J, 6])
        bnst0 = sb("bnst0", [P, J, 6])
        mv0 = sb("mv0", [P, J, 2])
        mv1 = sb("mv1", [P, J, 2])
        mv2 = sb("mv2", [P, J, 2])
        cf1 = sb("cf1", [P, 2, J])
        cf2 = sb("cf2", [P, 2, J])
        lnw1 = sb("lnw1", [P, 2, J])
        lnw2 = sb("lnw2", [P, 2, J])
        minus_half = sb("minus_half", [P, NTILE])

        ARENA = 33800
        arena = sb("arena", [P, ARENA])
        at = [0]

        def part(n):
            at[0] += n
            assert at[0] <= ARENA
            return arena[:, at[0] - n:at[0]]

        first_dead = at[0]
        mixA = part(3 * CH * SEQ).rearrange("p (m c t) -> p m c t", m=3, c=CH)
        dmix = part(CH * SEQ).rearrange("p (c t) -> p c t", c=CH)
        kvs = part(3 * CH * SEQ).rearrange("p (m c t) -> p m c t", m=3, c=CH)
        E1 = [part(2 * SEQ).rearrange("p (m t) -> p m t", m=2) for _ in range(CH)]
        E2 = [part(2 * SEQ).rearrange("p (m t) -> p m t", m=2) for _ in range(CH)]
        qb = [part(SEQ) for _ in range(CH)]
        evb = [part(SEQ) for _ in range(CH)]
        t1b = [part(SEQ) for _ in range(CH)]
        pp = part(SEQ + 1)
        aa = part(SEQ + 1)
        bb = part(SEQ + 1)
        att = part(CH * SEQ).rearrange("p (c t) -> p c t", c=CH)
        hT = part(CH * (SEQ + 1)).rearrange("p (c t) -> p c t", c=CH)
        moe_end = at[0]
        hn = part(J * C).rearrange("p (j c) -> p j c", j=J)
        x_in = part(J * C).rearrange("p (j c) -> p j c", j=J)
        mixB = part(2 * CH * SEQ).rearrange("p (m c t) -> p m c t", m=2, c=CH)
        kf2 = part(HC * SEQ).rearrange("p (h t) -> p h t", h=HC)
        sigf = part(J * C)
        wk, wv, wr, wo, wfr = (part(CH * C).rearrange("p (k n) -> p k n", k=CH) for _ in range(5))
        wfk = part(CH * HID).rearrange("p (k n) -> p k n", k=CH)
        wfv = part(HC * C).rearrange("p (k n) -> p k n", k=HC)
        DESK = 10240
        desk = sb("desk", [P, DESK])
        xa = [desk[:, i * 1024:(i + 1) * 1024].rearrange("p (j c) -> p j c", j=J) for i in range(2)]
        xta = [desk[:, 2048 + i * 1024:3072 + i * 1024].rearrange("p (k t) -> p k t", k=CH) for i in range(2)]
        ra = 4096
        NE = NTILE * E

        def routing(n=NE):
            nonlocal ra
            ra += n
            assert ra <= DESK
            return desk[:, ra - n:ra]

        logits, probs, work, pexp, selT, oneT, win, mask8 = (routing() for _ in range(8))
        small = routing(8 * NTILE)
        mvA = routing(2 * NTILE)
        wg_sb = routing(CH * E)
        wgc = routing(CH * E)
        erev = routing(E)
        gate = routing(NTILE)
        reset = routing(NE)
        ids_sb = routing(NTILE).bitcast(I32)
        tiny = routing(64)
        iota_sb = routing(NT)
        tw = routing(NT * E)
        w2_sb = desk[:, 0:E * CH * F]
        w1_sb = arena[:, first_dead:first_dead + E * CH * F]
        rc = [first_dead + E * CH * F]

        def ring(n, depth):
            rc[0] += n * depth
            assert rc[0] <= moe_end
            return [arena[:, rc[0] - n * (d + 1):rc[0] - n * d] for d in range(depth)]

        rows = ring(2 * C, RING)
        xn_t = ring(C, 2)
        xnT = [a.rearrange("p (k t) -> p k t", k=CH) for a in ring(C, 2)]
        w1_t = [a.rearrange("p (k f) -> p k f", k=CH) for a in ring(CH * F, 2)]
        hT_t = [a.rearrange("p (f t) -> p f t", f=FK) for a in ring(F, 2)]
        th_t = ring(C, 2)
        out_t = ring(C, RING)
        list_sb = sb("list_sb", [P, NT, 4], I32)
        row_idx = [sb(f"row_idx{i}", [P, 1], I32) for i in range(RING)]
        s_idx = sb("s_idx", [P, RING], I32)
        out_idx = [sb(f"out_idx{i}", [P, 1], I32) for i in range(RING)]
        info_t = [sb(f"info_t{i}", [P, 4]) for i in range(RING)]

        psT = ctx.enter_context(nc.psum_tensor("psT", [P, 2, 512], F32))
        psM = ctx.enter_context(nc.psum_tensor("psM", [P, 3, 512], F32))
        psKV = ctx.enter_context(nc.psum_tensor("psKV", [P, 2, 512], F32))
        psR = ctx.enter_context(nc.psum_tensor("psR", [P, 512], F32))

        names = """waited params_in ident_in consts_in xa_in0 xa_in1 xta_in0 xta_in1 weights_in proj_w_in wg_in halved
        a_step a_stats logits_done logits_kept wg_mean wg_ready decay_exp pool_const columns_set
        var_ready pow_ready bit_step bit_counted bit_summed route_step route_pe route_exp_in route_exp_out
        probs_turned routed pads_out list_cur list_scattered list_in w1_in w2_in
        x_in x_out s_out fetched x0_ready scaled0 embedded moments_step ln1_stats cf1_ready hn1_ready tr1_done
        h1_ready mix1_step mix1_done mixr_scaled mixr1_done proj_done kvr_ready wkv_step pre_done relu2_done exp_done att_done o_done
        x2_done ln2_step ln2_stats cf2_ready hn2_ready tr2_done h2_ready mix2_step mix2_done mixr2_done
        kf_done relu_done sq_done fr_done sigf_done kv_done s_done s_mult rstd1_step rstd2_step
        rows_zeroed idx_ready s_idx_ready info_ready xn_done turned mlp_in_ready h_done gelu_done y_done tanh_done
        combine_step combined""".split()
        names += [f"{n}{i}" for n in ("gathered", "s_gathered") for i in range(RING)] + [f"rows_out{i}" for i in range(RING)]
        S = {n: sem(n) for n in names}

        def tile_row(b):
            return s_ring[:, ds((b & 3) * (J * C), J * C)]

        def wait_run(eng, s, value):
            eng.wait_ge(s, value)
            if not isinstance(value, int):
                eng.sem_inc(S["waited"])

        xT_k = xT.rearrange("(k p) t -> p k t", p=P)
        xrows = x.rearrange("(n p) c -> p n c", p=P)
        xs_store = xs_rows.rearrange("(n p) c -> p n c", p=P)
        y_ps = [psM[:, 2, 0:C], psR[:, 0:C]]

        def steps(eng, step):
            for t in range(-3, RING):
                step(t, t % RING, t // RING)
            with eng.Fori(1, NT // RING - 1) as g:
                for i in range(RING):
                    step(RING * g + i, i, g)
            for t in range(NT - RING, NT):
                step(t, t % RING, t // RING)

        block = ctx.enter_context(nc.Block())

        @block.sync
        def _(sp):
            def load_tokens(n):
                if n >= 2:
                    sp.wait_ge(S["a_stats"], n - 1)
                sp.dma_start(xa[n % 2], xrows[:, n * J:(n + 1) * J, :]).then_inc(S[f"xa_in{n % 2}"], 16)

            def load_channels(n):
                if n >= 2:
                    sp.wait_ge(S["logits_done"], n - 1)
                sp.dma_start(xta[n % 2], xT_k[:, :, n * SEQ:(n + 1) * SEQ]).then_inc(S[f"xta_in{n % 2}"], 16)

            def load_weights(ready, *pairs):
                for w_sb, w_dram in pairs:
                    sp.dma_start(w_sb, w_dram.rearrange("(k p) n -> p k n", p=P)).then_inc(S[ready], 16)

            load_tokens(0)
            sp.dma_start(x_in, xrows[:, 0:J, :]).then_inc(S["x_in"], 16)
            load_tokens(1)
            sp.dma_start(cst[:], consts[:, 0:5 * P].rearrange("p (i q) -> p i q", i=5)).then_inc(S["ident_in"], 16)
            sp.dma_start(wg_sb.rearrange("p (k e) -> p k e", k=CH),
                         Wg.rearrange("(k p) e -> p k e", p=P)).then_inc(S["wg_in"], 16)
            sp.dma_start(vecs[:], vec.rearrange("(c p) n -> p c n", p=P)).then_inc(S["params_in"], 16)
            sp.dma_start(w0_bc[:], ln0_w.partition_broadcast(P)).then_inc(S["params_in"], 16)
            sp.dma_start(b0_bc[:], ln0_b.partition_broadcast(P)).then_inc(S["params_in"], 16)
            load_channels(0)
            load_channels(1)
            load_weights("proj_w_in", (wk, WkT), (wv, WvT), (wr, WrT))
            for n in (2, 3):
                load_tokens(n)
                load_channels(n)
            load_weights("weights_in", (wo, WoT), (wfv, WfvT), (wfk, WfkT), (wfr, WfrT))
            sp.dma_start(erev, consts[:, 5 * P:5 * P + E]).then_inc(S["consts_in"], 16)
            sp.dma_start(iota_sb[0:1, :], tile_iota).then_inc(S["consts_in"], 16)
            sp.dma_start(ids_sb, token_ids).then_inc(S["consts_in"], 16)
            sp.dma_start(sorted_list, pad_rows).then_inc(S["pads_out"], 16)

            def load_x(b):
                sp.dma_start(x_in, xrows[:, ds(b * J, J), :]).then_inc(S["x_in"], 16)
                store_x(b)

            def store_x(b):
                wait_run(sp, S["x_in"], b * 16 + 16)
                sp.dma_start(xs_store[:, ds(b * J, J), 0:C], x_in).then_inc(S["x_out"], 16)

            def x_free(b):
                wait_run(sp, S["x0_ready"], b)
                wait_run(sp, S["x_out"], b * 16)

            def store_s(b):
                wait_run(sp, S["s_done"], b + 1)
                sp.dma_start(xs_store[:, ds(b * J, J), C:2 * C],
                             tile_row(b).rearrange("p (j c) -> p j c", j=J)).then_inc(S["s_out"], 16)

            store_x(0)
            x_free(1)
            load_x(1)
            for n in (4, 5):
                load_tokens(n)
                load_channels(n)
            for b in range(ROUTER_ROUNDS):
                for n in range(4 * b + 6, min(4 * b + 10, NB)):
                    load_tokens(n)
                    load_channels(n)
                    if b + 2 <= ROUTER_ROUNDS and n == 4 * b + 7:
                        x_free(b + 2)
                        load_x(b + 2)
            store_s(0)
            with sp.Fori(4, NB) as b:
                x_free(b)
                wait_run(sp, S["s_out"], (b - 3) * 16)
                load_x(b)
                store_s(b - 3)
            sp.wait_ge(S["routed"], 1)
            for e in range(E):
                sp.dma_start(w2_sb.rearrange("p (e k f) -> p e k f", e=E, k=FK)[:, e],
                             W2[e].rearrange("(k p) f -> p k f", p=P)).then_inc(S["w2_in"], 16)
            store_s(NB - 3)
            sp.wait_ge(S["list_scattered"], 16 * NTILE)
            sp.dma_start(list_sb[:].rearrange("p n w -> p (n w)"),
                         sorted_list.rearrange("(p n) w -> p (n w)", p=P)).then_inc(S["list_in"], 16)
            sp.wait_ge(S["mix2_done"], NB)
            sp.wait_ge(S["mixr2_done"], NB)
            for e in range(E):
                sp.dma_start(w1_sb.rearrange("p (e k f) -> p e k f", e=E, k=CH)[:, e],
                             W1[e].rearrange("(k p) f -> p k f", p=P)).then_inc(S["w1_in"], 16)
            store_s(NB - 2)
            store_s(NB - 1)

        @block.gpsimd
        def _(pool):
            pool.memset(minus_half[:], -0.5).then_inc(S["pool_const"], 1)
            pool.wait_ge(S["pool_const"], 1)

            mv = mvA.rearrange("p (n s) -> p n s", s=2)
            sv = small.rearrange("p (k n) -> p k n", n=NTILE)

            def norm_scales(g, first, last):
                st = Steps(pool, S["pow_ready"], 8, g, S["waited"])
                n = slice(first * J, (last + 1) * J)
                mean, var, half = mv[:, n, 0], mv[:, n, 1], minus_half[:, n]
                scale0, offset0, r, offset = stats0[:, n, 0], stats0[:, n, 1], info[:, n, 2], info[:, n, 3]
                pool.wait_ge(S["a_step"], 2 * last + 2)
                st.then(pool.tensor_scalar(sv[:, 0, n], var, EPS, 1.0, ALU.add, ALU.mult))
                st.wait()
                st.then(pool.tensor_tensor(r, sv[:, 0, n], half, ALU.pow))
                st.wait()
                pool.tensor_tensor(sv[:, 1, n], var, r, ALU.mult)
                st.then(pool.tensor_scalar(sv[:, 2, n], mean, -1.0, 0.0, ALU.mult, ALU.add))
                st.wait()
                st.then(pool.tensor_tensor(sv[:, 3, n], sv[:, 1, n], r, ALU.mult))
                st.wait()
                st.then(pool.tensor_scalar(sv[:, 4, n], sv[:, 3, n], EPS, 1.0, ALU.add, ALU.mult))
                st.wait()
                st.then(pool.tensor_tensor(sv[:, 5, n], sv[:, 4, n], half, ALU.pow))
                st.wait()
                st.then(pool.tensor_tensor(scale0, sv[:, 5, n], r, ALU.mult))
                st.wait()
                pool.tensor_tensor(offset0, sv[:, 2, n], scale0, ALU.mult)
                st.then(pool.tensor_tensor(offset, sv[:, 2, n], r, ALU.mult))
                st.end()

            def add_to_list(b, half):
                wait_run(pool, S["list_cur"], b - (LIST_ROUND - 1))
                if isinstance(b, int) and b == LIST_ROUND:
                    pool.wait_ge(S["pads_out"], 16)
                for j in range(half * LT // 2, (half + 1) * LT // 2):
                    pool.indirect_dma_start(sorted_list[:, :], bass.IndirectOffsetOnAxis(place_cur[:, j:j + 1], axis=0),
                                            info_cur[:, j, :], None).then_inc(S["list_scattered"], 16)

            def rstd(b, stats, mv, lnw, cf, step, ready):
                st = Steps(pool, S[step], 2, b, S["waited"])
                wait_run(pool, S[stats], b + 1)
                pool.tensor_scalar(lnw[:, 0], mv[:, :, 1], EPS, 1.0, ALU.add, ALU.mult)
                st.then(pool.tensor_scalar(lnw[:, 1], mv[:, :, 0], -1.0, 0.0, ALU.mult, ALU.add))
                st.wait()
                st.then(pool.tensor_tensor(cf[:, 0], lnw[:, 0], minus_half[:, 0:J], ALU.pow))
                st.wait()
                pool.tensor_tensor(cf[:, 1], lnw[:, 1], cf[:, 0], ALU.mult).then_inc(S[ready], 1)
                st.end()

            def embed(b):
                wait_run(pool, S["x0_ready"], b + 1)
                if isinstance(b, int) and b == 0:
                    pool.wait_ge(S["params_in"], 48)
                over_j = lambda a: a[:].rearrange("p (o c) -> p o c", o=1).to_broadcast([P, J, C])
                pool.tensor_tensor(hn, hn, over_j(w0_bc), ALU.mult).then_inc(S["scaled0"], 1)
                wait_run(pool, S["scaled0"], b + 1)
                pool.tensor_tensor(tile_row(b).rearrange("p (j c) -> p j c", j=J), hn, over_j(b0_bc), ALU.add
                                   ).then_inc(S["embedded"], 1)

            def mix_r(b, step, dst, m, done, scaled):
                wait_run(pool, S[step], b + 1)
                for c in range(CH):
                    ins = pool.tensor_scalar(dst[:, c], dmix[:, c], vecs[:, c, V[m]:V[m] + 1], 0.0, ALU.mult, ALU.add)
                ins.then_inc(S["mixr_scaled"], 1)
                wait_run(pool, S["mixr_scaled"], scaled)
                pool.tensor_tensor(dst, dst, hT[:, :, 0:SEQ], ALU.add).then_inc(S[done], 1)

            def mix_r1(b):
                mix_r(b, "mix1_step", mixA[:, 2], "tmr", "mixr1_done", 2 * b if not isinstance(b, int) or b else 1)

            def mix_r2(b):
                mix_r(b, "mix2_step", mixB[:, 1], "cmr", "mixr2_done", 2 * b + (2 if isinstance(b, int) and b == NB - 1 else 3))

            def residual2(b):
                wait_run(pool, S["s_mult"], b + 1)
                xs = tile_row(b)
                pool.tensor_tensor(xs, xs, sigf, ALU.add).then_inc(S["s_done"], 1)

            def rstd1(b):
                rstd(b, "ln1_stats", mv1, lnw1, cf1, "rstd1_step", "cf1_ready")

            def rstd2(b):
                rstd(b, "ln2_stats", mv2, lnw2, cf2, "rstd2_step", "cf2_ready")

            def round_(b, ffn=True, listing=False, ahead=True):
                if ahead:
                    embed(b + 1)
                if listing:
                    add_to_list(b, 0)
                if ahead:
                    rstd1(b + 1)
                if listing:
                    add_to_list(b, 1)
                if ahead:
                    mix_r1(b + 1)
                rstd2(b)
                if ffn:
                    residual2(b - 1)
                mix_r2(b)

            norm_scales(0, 0, 0)
            embed(0)
            rstd1(0)
            norm_scales(1, 1, 3)
            mix_r1(0)
            for b in range(ROUTER_ROUNDS):
                round_(b, b > 0)
                norm_scales(b + 2, 4 * b + 4, 4 * b + 7)
            with pool.Fori(ROUTER_ROUNDS, LIST_ROUND) as b:
                round_(b)
            round_(LIST_ROUND, listing=True)
            with pool.Fori(LIST_ROUND + 1, NB - 1) as b:
                round_(b, listing=True)
            round_(NB - 1, listing=True, ahead=False)

            def gather(t, i, columns=slice(0, 2 * C), source=xs_rows[:, :]):
                wait_run(pool, S["idx_ready"], t + 1)
                pool.indirect_dma_start(rows[i][:, columns], None, source,
                                        bass.IndirectOffsetOnAxis(row_idx[i][:, 0:1], axis=0),
                                        bounds_check=T - 1, oob_is_err=False).then_inc(S[f"gathered{i}"], 16)

            def gather_s(t):
                pool.wait_ge(S["s_idx_ready"], 1)
                pool.indirect_dma_start(rows[t][:, C:2 * C], None, xs_rows.rearrange("t (h c) -> (t h) c", h=2),
                                        bass.IndirectOffsetOnAxis(s_idx[:, t:t + 1], axis=0),
                                        bounds_check=2 * T - 1, oob_is_err=False).then_inc(S[f"s_gathered{t}"], 16)

            def scatter(t, i):
                wait_run(pool, S["combined"], t + 1)
                pool.indirect_dma_start(out[:, :], bass.IndirectOffsetOnAxis(out_idx[i][:, 0:1], axis=0),
                                        out_t[i], None, bounds_check=T - 1, oob_is_err=False
                                        ).then_inc(S[f"rows_out{i}"], 16)

            pool.wait_ge(S["mix2_done"], NB)
            pool.wait_ge(S["mixr2_done"], NB)
            for i in range(RING):
                ins = pool.memset(rows[i], 0.0)
            ins.then_inc(S["rows_zeroed"], 1)
            pool.wait_ge(S["rows_zeroed"], 1)
            for t in range(RING):
                gather(t, t, slice(0, C), x[:, :])
            residual2(NB - 1)
            pool.wait_ge(S["x_out"], 16 * NB)
            pool.wait_ge(S["s_out"], 16 * NB)
            for t in range(RING):
                gather_s(t)
            with pool.Fori(0, NT // RING - 1) as g:
                for i in range(RING):
                    scatter(RING * g + i, i)
                    gather(RING * g + (RING + i), i)
            for i in range(RING):
                scatter(NT - RING + i, i)
            for i in range(RING):
                pool.wait_ge(S[f"rows_out{i}"], 16 * (NT // RING))

        @block.scalar
        def _(act):
            act.wait_ge(S["params_in"], 48)
            act.activation(wneg[:], vecs[:, :, V["decay"]], ACT.Exp).then_inc(S["decay_exp"], 1)

            def norm0(b):
                wait_run(act, S["fetched"], b + 1)
                wait_run(act, S["x_in"], 16 * b + 16)
                if not (isinstance(b, int) and b < 2):
                    wait_run(act, S["tr2_done"], b - 1)
                for j in range(J):
                    ins = act.activation(hn[:, j], x_in[:, j], ACT.Identity,
                                         scale=stats_cur[:, j, 0:1], bias=stats_cur[:, j, 1:2])
                ins.then_inc(S["x0_ready"], 1)

            def norm(b, cf, cf_ready, ready):
                wait_run(act, S[cf_ready], b + 1)
                xs = tile_row(b)
                for j in range(J):
                    ins = act.activation(hn[:, j], xs[:, j * C:(j + 1) * C], ACT.Identity,
                                         scale=cf[:, 0, j:j + 1], bias=cf[:, 1, j:j + 1])
                ins.then_inc(S[ready], 1)

            def affine(b, tr_done, w, bias, ready):
                wait_run(act, S[tr_done], b + 1)
                for c in range(CH):
                    act.activation(hT[:, c, 1:SEQ + 1], psT[:, c, :], ACT.Identity,
                                   scale=vecs[:, c, V[w]:V[w] + 1], bias=vecs[:, c, V[bias]:V[bias] + 1]
                                   ).then_inc(S[ready], 1)

            def norm1(b):
                norm(b, cf1, "cf1_ready", "hn1_ready")

            def affine1(b):
                if not (isinstance(b, int) and b < 2):
                    wait_run(act, S["mixr2_done"], b - 1)
                affine(b, "tr1_done", "ln1_w", "ln1_b", "h1_ready")

            def norm2(b):
                if not (isinstance(b, int) and b == NB - 1):
                    wait_run(act, S["tr1_done"], b + 2)
                norm(b, cf2, "cf2_ready", "hn2_ready")

            def affine2(b):
                if not (isinstance(b, int) and b == NB - 1):
                    wait_run(act, S["mix1_done"], 2 * b + 4)
                    wait_run(act, S["mixr1_done"], b + 2)
                affine(b, "tr2_done", "ln2_w", "ln2_b", "h2_ready")

            def take_kvr(b, lo, hi):
                if lo == 0 and not (isinstance(b, int) and b == 0):
                    wait_run(act, S["att_done"], 2 * b)
                for u in range(lo, hi):
                    act.wait_ge(S["proj_done"], b * (3 * CH) + (u + 1))
                    dst, src = kvs[:, u // CH, u % CH, :], psM[:, u % 3, :]
                    if u // CH == 2:
                        act.activation(dst, src, ACT.Tanh, scale=0.5).then_inc(S["kvr_ready"], 1)
                    else:
                        act.activation(dst, src, ACT.Copy).then_inc(S["kvr_ready"], 1)

            def exps(b, c):
                wait_run(act, S["pre_done"], b * CH + (c + 1))
                act.activation(E2[c][:, 0], qb[c], ACT.Relu, bias=wneg[:, c:c + 1])
                act.activation(E2[c][:, 1], qb[c], ACT.Relu, bias=uneg[:, c:c + 1]).then_inc(S["relu2_done"], 1)
                act.activation(E1[c], E1[c], ACT.Exp).then_inc(S["exp_done"], 1)
                wait_run(act, S["relu2_done"], b * CH + (c + 1))
                act.activation(E2[c], E2[c], ACT.Exp, scale=-1.0).then_inc(S["exp_done"], 1)

            def relu(b, h):
                if h == 0:
                    wait_run(act, S["tr2_done"], b + 1)
                act.wait_ge(S["kf_done"], b * HC + (h + 1))
                act.activation(kf2[:, h], psM[:, h % 3, :], ACT.Relu).then_inc(S["relu_done"], 1)

            def square(b, h):
                act.wait_ge(S["relu_done"], b * HC + (h + 1))
                act.activation(kf2[:, h], kf2[:, h], ACT.Square).then_inc(S["sq_done"], 1)

            def sigmoid_fr(b):
                if not (isinstance(b, int) and b == 0):
                    wait_run(act, S["s_done"], b)
                for u in range(2):
                    act.wait_ge(S["fr_done"], 2 * b + (u + 1))
                    act.activation(sigf[:, u * 512:(u + 1) * 512], psM[:, (HC + u) % 3, :],
                                   ACT.Tanh, scale=0.5).then_inc(S["sigf_done"], 1)

            def relus(b, lo, hi):
                for h in range(lo, hi):
                    relu(b, h)
                    if h:
                        square(b, h - 1)

            def round_(b, ffn, ahead, softmax=False):
                if ffn:
                    if ahead:
                        norm0(b + 1)
                    relus(b - 1, 0, 1)
                    exps(b, 0)
                    relus(b - 1, 1, 3)
                    exps(b, 1)
                if softmax:
                    act.wait_ge(S["route_exp_in"], 1)
                    act.activation(probs, logits, ACT.Exp).then_inc(S["route_exp_out"], 1)
                if ffn:
                    relus(b - 1, 3, HC)
                    square(b - 1, HC - 1)
                if ahead:
                    norm1(b + 1)
                if ffn:
                    sigmoid_fr(b - 1)
                if ahead:
                    affine1(b + 1)
                    take_kvr(b + 1, 0, 2)
                norm2(b)
                if ahead:
                    take_kvr(b + 1, 2, 4)
                affine2(b)
                if ahead:
                    take_kvr(b + 1, 4, 6)

            norm0(0)
            norm1(0)
            affine1(0)
            take_kvr(0, 0, 2)
            exps(0, 0)
            take_kvr(0, 2, 4)
            exps(0, 1)
            norm0(1)
            take_kvr(0, 4, 6)
            round_(0, False, True)
            with act.Fori(1, ROUTER_ROUNDS) as b:
                round_(b, True, True)
            round_(ROUTER_ROUNDS, True, True, softmax=True)
            with act.Fori(BIT_ROUND, NB - 1) as b:
                round_(b, True, True)
            round_(NB - 1, True, False)
            relus(NB - 1, 0, HC)
            square(NB - 1, HC - 1)
            sigmoid_fr(NB - 1)

            def xn(t, i, g):
                act.wait_ge(S[f"gathered{i}"], g * 16 + 16)
                wait_run(act, S["info_ready"], t + 1)
                if not (isinstance(t, int) and t < 2):
                    wait_run(act, S["turned"], t - 1)
                nf = info_t[i]
                act.activation(xn_t[i % 2], rows[i][:, 0:C], ACT.Identity, scale=nf[:, 2:3], bias=nf[:, 3:4]
                               ).then_inc(S["xn_done"], 1)

            def gelu(t, i):
                if not (isinstance(t, int) and t < 2):
                    wait_run(act, S["y_done"], t - 1)
                act.wait_ge(S["h_done"], t + 1)
                act.activation(hT_t[i % 2].rearrange("p f t -> p (f t)"), psM[:, i % 2, :], ACT.Gelu
                               ).then_inc(S["gelu_done"], 1)

            def tanh(t, i):
                if not (isinstance(t, int) and t < 2):
                    wait_run(act, S["combined"], t - 1)
                wait_run(act, S["y_done"], t + 1)
                act.activation(th_t[i % 2], y_ps[i % 2], ACT.Tanh, scale=info_t[i][:, 1:2]
                               ).then_inc(S["tanh_done"], 1)

            def step(t, i, g):
                if not isinstance(t, int) or -3 <= t < NT - 3:
                    xn(t + 3, (i + 3) % RING, g + (i + 3) // RING)
                if not isinstance(t, int) or -1 <= t < NT - 1:
                    gelu(t + 1, (i + 1) % RING)
                if not isinstance(t, int) or t >= 0:
                    tanh(t, i)

            steps(act, step)

        @block.tensor
        def _(pe):
            def router_weights():
                pe.wait_ge(S["wg_in"], 16)
                for k in range(CH):
                    ins = pe.matmul(psR[:, 0:E], ones, wg_sb[:, k * E:(k + 1) * E], start=(k == 0), stop=(k == CH - 1))
                ins.then_inc(S["wg_mean"], 1)
                pe.wait_ge(S["wg_ready"], 1)

            def router(n, q, g):
                pe.wait_ge(S[f"xta_in{q % 2}"], g * 16 + 16)
                if not (isinstance(n, int) and n < 4):
                    wait_run(pe, S["logits_kept"], n - 3)
                for j in range(J):
                    for k in range(CH):
                        ins = pe.matmul(psR[:, (q * J + j) * E:(q * J + j + 1) * E], xta[q % 2][:, k, j * P:(j + 1) * P],
                                        wgc[:, k * E:(k + 1) * E], start=(k == 0), stop=(k == CH - 1))
                ins.then_inc(S["logits_done"], 1)

            def router_point(b, point):
                router(b * 4 + (4 + point), point, b * 2 + (2 + point // 2))

            def sum_bit(b, point):
                pe.wait_ge(S["bit_counted"], (b - BIT_ROUND) * 4 + (point + 3))
                pe.matmul(psR[:, 0:1], esum, tiny[:, 4:5], start=True, stop=True).then_inc(S["bit_summed"], 1)

            def softmax(b, point):
                if point == 1:
                    pe.wait_ge(S["route_step"], R_PEXP)
                    for j in range(J):
                        ins = pe.transpose(psR[:, j * P:(j + 1) * P], pexp[:, j * P:(j + 1) * P], ident)
                    ins.then_inc(S["probs_turned"], 1)
                elif point >= 2:
                    sum_bit(b, point)

            def route(b, point):
                pe.wait_ge(S["route_step"], (R_COUNTS, R_SEL, R_ONEHOT, R_KEPT)[point])
                if point == 0:
                    pe.matmul(psR[:, 0:1], esum, tiny[:, 5:6], start=True, stop=True)
                    ins = pe.matmul(psR[:, 1:2], eprefix, tiny[:, 6:7], start=True, stop=True)
                elif point == 1:
                    for j in range(J):
                        ins = pe.transpose(psR[:, j * P:(j + 1) * P], oneT[:, j * P:(j + 1) * P], ident)
                elif point == 2:
                    ins = pe.matmul(psR[:], prefix, pexp, start=True, stop=True)
                else:
                    ins = pe.matmul(psR[:], ones, pexp, start=True, stop=True)
                ins.then_inc(S["route_pe"], 1)

            nothing = lambda b, point: None

            def turn(b, ready, done):
                wait_run(pe, S[ready], b + 1)
                for c in range(CH):
                    for j in range(J):
                        ins = pe.transpose(psT[:, c, j * P:(j + 1) * P], hn[:, j, c * P:(c + 1) * P], ident)
                ins.then_inc(S[done], 1)

            def turn1(b):
                if not (isinstance(b, int) and b < 2):
                    wait_run(pe, S["h2_ready"], CH * b - CH)
                turn(b, "hn1_ready", "tr1_done")

            def turn2(b):
                wait_run(pe, S["h1_ready"], CH * b + 2 * CH) if not (isinstance(b, int) and b == NB - 1) else None
                turn(b, "hn2_ready", "tr2_done")

            def project(b, *ms):
                for m in ms:
                    w = (wk, wv, wr)[m]
                    if m < 2:
                        wait_run(pe, S["mix1_done"], 2 * b + (m + 1))
                    else:
                        wait_run(pe, S["mixr1_done"], b + 1)
                    for c in range(CH):
                        u = m * CH + c
                        if u >= 3:
                            pe.wait_ge(S["kvr_ready"], b * (3 * CH) + (u - 2))
                        elif not (isinstance(b, int) and b == 0):
                            if u == 0:
                                wait_run(pe, S["kvr_ready"], b * (3 * CH))
                                if not (isinstance(b, int) and b == 1):
                                    wait_run(pe, S["sigf_done"], 2 * b - 2)
                            else:
                                wait_run(pe, S["x2_done"], b)
                        for k in range(CH):
                            ins = pe.matmul(psM[:, u % 3, :], w[:, k, c * P:(c + 1) * P], mixA[:, m, k, :],
                                            start=(k == 0), stop=(k == CH - 1))
                        ins.then_inc(S["proj_done"], 1)

            def project_out(b):
                wait_run(pe, S["att_done"], CH * b + CH)
                if not (isinstance(b, int) and b == 0):
                    wait_run(pe, S["relu_done"], HC * b)
                    wait_run(pe, S["sigf_done"], 2 * b - 1)
                for j in range(J):
                    for c in range(CH):
                        ins = pe.matmul(psM[:, 1 + j // 2, (j % 2) * C:(j % 2 + 1) * C],
                                        att[:, c, j * P:(j + 1) * P], wo[:, c, :], start=(c == 0), stop=(c == CH - 1))
                ins.then_inc(S["o_done"], 1)

            def hidden(b, extra, rnd):
                wait_run(pe, S["mix2_done"], b + 1)
                for h in range(HC):
                    if h < 3:
                        if isinstance(b, int) and b == NB - 1:
                            pe.wait_ge(S["x2_done"], NB)
                            pe.wait_ge(S["sigf_done"], 2 * NB - 2)
                        else:
                            wait_run(pe, S["kvr_ready"], b * (3 * CH) + (3 * CH + 4 + h))
                    else:
                        pe.wait_ge(S["relu_done"], b * HC + (h - 2))
                    for k in range(CH):
                        ins = pe.matmul(psM[:, h % 3, :], wfk[:, k, h * P:(h + 1) * P], mixB[:, 0, k, :],
                                        start=(k == 0), stop=(k == CH - 1))
                    ins.then_inc(S["kf_done"], 1)
                    if h == 5:
                        extra(rnd, 0)

            def receptance(b):
                wait_run(pe, S["mixr2_done"], b + 1)
                for u in range(2):
                    pe.wait_ge(S["relu_done"], b * HC + (HC + u - 2))
                    for j in (2 * u, 2 * u + 1):
                        for k in range(CH):
                            ins = pe.matmul(psM[:, (HC + u) % 3, (j % 2) * C:(j % 2 + 1) * C],
                                            mixB[:, 1, k, j * P:(j + 1) * P], wfr[:, k, :],
                                            start=(k == 0), stop=(k == CH - 1))
                    ins.then_inc(S["fr_done"], 1)

            def channel_out(b, j):
                if j == 0:
                    pe.wait_ge(S["sq_done"], b * HC + HC)
                    wait_run(pe, S["mix2_done"], b + 1)
                for h in range(HC):
                    ins = pe.matmul(psKV[:, j // 2, (j % 2) * C:(j % 2 + 1) * C], kf2[:, h, j * P:(j + 1) * P],
                                    wfv[:, h, :], start=(h == 0), stop=(h == HC - 1))
                ins.then_inc(S["kv_done"], 1)

            def round_(b, extra, ffn=True, ahead=True):
                if ffn:
                    hidden(b - 1, extra, b)
                    receptance(b - 1)
                    extra(b, 1)
                    channel_out(b - 1, 0)
                    channel_out(b - 1, 1)
                else:
                    extra(b, 0)
                    extra(b, 1)
                if ahead:
                    turn1(b + 1)
                if ffn:
                    channel_out(b - 1, 2)
                project_out(b)
                if ffn:
                    channel_out(b - 1, 3)
                if ahead:
                    project(b + 1, 0)
                extra(b, 2)
                if ahead:
                    project(b + 1, 1)
                turn2(b)
                if ahead:
                    project(b + 1, 2)
                extra(b, 3)

            pe.wait_ge(S["ident_in"], 16)
            router_weights()
            for n in range(4):
                router(n, n, n // 2)
            turn1(0)
            pe.wait_ge(S["proj_w_in"], 48)
            project(0, 0, 1, 2)
            pe.wait_ge(S["halved"], 1)
            round_(0, router_point, ffn=False)
            with pe.Fori(1, ROUTER_ROUNDS) as b:
                round_(b, router_point)
            round_(ROUTER_ROUNDS, softmax)
            with pe.Fori(BIT_ROUND, SELECT_ROUND) as b:
                round_(b, sum_bit)
            round_(SELECT_ROUND, route)
            with pe.Fori(LIST_ROUND, NB - 1) as b:
                round_(b, nothing)
            round_(NB - 1, nothing, ahead=False)
            hidden(NB - 1, nothing, NB)
            receptance(NB - 1)
            for j in range(J):
                channel_out(NB - 1, j)

            def turn_x(t, i):
                wait_run(pe, S["xn_done"], t + 1)
                if not (isinstance(t, int) and t < 2):
                    wait_run(pe, S["mlp_in_ready"], t - 1)
                for k in range(CH):
                    ins = pe.transpose(psT[:, i % 2, k * P:(k + 1) * P], xn_t[i % 2][:, k * P:(k + 1) * P], ident)
                ins.then_inc(S["turned"], 1)

            def mlp_in(t, i):
                wait_run(pe, S["mlp_in_ready"], t + 1)
                if not (isinstance(t, int) and t < 2):
                    wait_run(pe, S["gelu_done"], t - 1)
                for f in range(FK):
                    for k in range(CH):
                        ins = pe.matmul(psM[:, i % 2, f * P:(f + 1) * P], w1_t[i % 2][:, k, f * P:(f + 1) * P],
                                        xnT[i % 2][:, k, :], start=(k == 0), stop=(k == CH - 1))
                ins.then_inc(S["h_done"], 1)

            def mlp_out(t, i):
                src = expert_at[0:1, t:t + 1] if isinstance(t, int) else expert_at[0:1, ds(t, 1)]
                w = pe.value_load(src, min_val=0, max_val=(E - 1) * FK * C)
                wait_run(pe, S["gelu_done"], t + 1)
                if not (isinstance(t, int) and t < 2):
                    wait_run(pe, S["combined"], t - 1)
                for f in range(FK):
                    ins = pe.matmul(y_ps[i % 2], hT_t[i % 2][:, f, :], w2_sb[:, ds(w + f * C, C)],
                                    start=(f == 0), stop=(f == FK - 1))
                ins.then_inc(S["y_done"], 1)

            def step(t, i, g):
                if not isinstance(t, int) or -2 <= t < NT - 2:
                    turn_x(t + 2, (i + 2) % RING)
                if not isinstance(t, int) or -1 <= t < NT - 1:
                    mlp_in(t + 1, (i + 1) % RING)
                if not isinstance(t, int) or t >= 0:
                    mlp_out(t, i)

            pe.wait_ge(S["w2_in"], 16 * E)
            pe.wait_ge(S["relu_done"], HC * NB)
            pe.wait_ge(S["sigf_done"], 2 * NB)
            steps(pe, step)

        @block.vector
        def _(v):
            v.memset(hT[:, :, 0:1], 0.0)
            v.memset(pp[:, 0:1], -1e38)
            v.memset(aa[:, 0:1], 0.0)
            v.memset(bb[:, 0:1], 0.0).then_inc(S["columns_set"], 1)
            v.wait_ge(S["columns_set"], 1)

            def prepare():
                v.wait_ge(S["decay_exp"], 1)
                v.tensor_scalar(wneg[:], wneg[:], -1.0, None, ALU.mult)
                v.tensor_scalar(uneg[:], vecs[:, :, V["first"]], -1.0, None, ALU.mult)
                v.wait_ge(S["weights_in"], 16 * 4)
                v.tensor_scalar(wo.rearrange("p k n -> p (k n)"), wo.rearrange("p k n -> p (k n)"), 0.5, None, ALU.mult)
                v.tensor_scalar(wfv.rearrange("p k n -> p (k n)"), wfv.rearrange("p k n -> p (k n)"), 0.5, None,
                                ALU.mult).then_inc(S["halved"], 1)
                v.wait_ge(S["halved"], 1)

            def router_weights():
                v.wait_ge(S["wg_mean"], 1)
                for k in range(CH):
                    ins = v.scalar_tensor_tensor(wgc[:, k * E:(k + 1) * E], psR[:, 0:E], -1.0 / C,
                                                 wg_sb[:, k * E:(k + 1) * E], ALU.mult, ALU.add)
                ins.then_inc(S["wg_ready"], 1)

            def statistics(b, i, g):
                st = Steps(v, S["a_step"], 2, b, S["waited"])
                wait_run(v, S[f"xa_in{i}"], g * 16 + 16)
                for j in range(J):
                    ins = v.bn_stats(bnst0[:, j], xa[i][:, j])
                ins.then_inc(S["a_stats"], 1)
                wait_run(v, S["a_stats"], b + 1)
                for j in range(J):
                    ins = v.bn_aggr(mv0[:, j], bnst0[:, j])
                st.then(ins)
                st.wait()
                st.then(v.tensor_copy(mvA[:, ds(b * (2 * J), 2 * J)], mv0[:].rearrange("p j s -> p (j s)")))
                st.wait()
                st.end()

            def keep_logits(n, q):
                wait_run(v, S["logits_done"], n + 4)
                v.tensor_copy(logits[:, ds(n * (J * E), J * E)], psR[:, q * J * E:(q + 1) * J * E]
                              ).then_inc(S["logits_kept"], 1)

            def router_point(b, point):
                statistics(b * 4 + (4 + point), point % 2, b * 2 + (2 + point // 2))
                keep_logits(b * 4 + point, point)

            R = Steps(v, S["route_step"], R_ALL, 0, S["waited"])
            te = lambda a: a.rearrange("p (t e) -> p t e", e=E)
            et = lambda a: a.rearrange("p (e t) -> p e t", e=E)
            over_e = lambda a: a.rearrange("p (t o) -> p t o", o=1).to_broadcast([P, NTILE, E])
            sm = lambda k: small[:, k * NTILE:(k + 1) * NTILE]
            def scores():
                v.wait_ge(S["logits_done"], NB)
                R.then(v.tensor_copy(logits[:, (NB - 4) * J * E:NB * J * E], psR[:, 0:4 * J * E]))
                v.wait_ge(S["logits_kept"], NB - 4)
                v.wait_ge(S["consts_in"], 48)
                v.tensor_copy(info[:, :, 0:1].rearrange("p t o -> p (t o)").bitcast(I32), ids_sb)
                R.then(v.memset(reset, 1.0))
                R.wait()
                R.then(v.memset(et(reset)[:, :, 0], 0.0))
                v.wait_ge(S["pow_ready"], 8 * (ROUTER_ROUNDS + 2))
                R.then(v.tensor_tensor(te(logits), te(logits), info[:, :, 2:3].to_broadcast([P, NTILE, E]), ALU.mult))
                R.wait()
                R.then(v.tensor_reduce(sm(6), te(logits), AX_X, ALU.max))
                R.wait()
                v.tensor_tensor(te(logits), te(logits), over_e(sm(6)), ALU.subtract).then_inc(S["route_exp_in"], 1)

            def probabilities():
                v.wait_ge(S["route_exp_out"], 1)
                R.then(v.tensor_reduce(sm(7), te(probs), AX_X, ALU.add))
                R.wait()
                R.then(v.reciprocal(sm(6), sm(7)))
                R.wait()
                R.then(v.tensor_tensor(te(probs), te(probs), over_e(sm(6)), ALU.mult))
                R.wait()
                R.then(v.tensor_copy(pexp.rearrange("p (j t e) -> p j t e", j=J, e=E),
                                     probs.rearrange("p (t j e) -> p j t e", j=J, e=E)))
                assert R.k == R_PEXP, R.k

            def turned_probabilities():
                v.wait_ge(S["probs_turned"], 1)
                R.then(v.tensor_copy(selT, psR[:]))
                R.wait()
            t_f, bit, cand, kept, cnt = (tiny[:, k:k + 1] for k in range(5))

            def try_bit(b, point):
                bits = 2 + point
                st = Steps(v, S["bit_step"], 3 * 4, b - BIT_ROUND, S["waited"])
                st.k = 3 * bits
                if isinstance(b, int) and b == ROUTER_ROUNDS and point == 2:
                    st.then(v.memset(t_f, 0.0))
                    st.then(v.memset(bit.bitcast(I32), 1 << 29))
                else:
                    wait_run(v, S["bit_summed"], (b - BIT_ROUND) * 4 + bits)
                    v.tensor_scalar(bit.bitcast(I32), bit.bitcast(I32), 1, None, ALU.logical_shift_right)
                    st.then(v.scalar_tensor_tensor(kept, psR[:, 0:1], float(CAP), cand, ALU.is_ge, ALU.mult))
                    st.wait()
                    st.then(v.tensor_tensor(t_f, t_f, kept, ALU.max))
                st.wait()
                st.then(v.tensor_tensor(cand.bitcast(I32), t_f.bitcast(I32), bit.bitcast(I32), ALU.bitwise_or))
                st.wait()
                v.tensor_scalar(work, selT, cand, None, ALU.is_ge, ALU.add, accum_out=cnt).then_inc(S["bit_counted"], 1)

            def softmax(b, point):
                if point < 3:
                    (scores, probabilities, turned_probabilities)[point]()
                if point >= 2:
                    try_bit(b, point)

            def route(b, point):
                if b == SELECT_ROUND:
                    (count_ties, select, choose, keep_prefix)[point]()
                elif point == 0:
                    place_tokens()
                    list_part(b)

            def count_ties():
                v.wait_ge(S["bit_summed"], 30)
                v.wait_ge(S["bit_counted"], 30)
                R.then(v.scalar_tensor_tensor(kept, psR[:, 0:1], float(CAP), cand, ALU.is_ge, ALU.mult))
                R.wait()
                R.then(v.tensor_tensor(t_f, t_f, kept, ALU.max))
                R.wait()
                v.tensor_scalar(oneT, selT, t_f, None, ALU.is_gt, ALU.add, accum_out=tiny[:, 5:6])
                R.then(v.tensor_scalar(work, selT, t_f, None, ALU.is_equal, ALU.add, accum_out=tiny[:, 6:7]))
                R.wait()
                assert R.k == R_COUNTS, R.k
                R.then(v.tensor_tensor_scan(win, ones[:, 0:1].to_broadcast([P, SEQ]), work, 0.0, ALU.mult, ALU.add))

            def select():
                v.wait_ge(S["route_pe"], 1)
                R.then(v.tensor_scalar(tiny[:, 7:8], psR[:, 0:1], -1.0, float(CAP), ALU.mult, ALU.add))
                R.wait()
                R.then(v.tensor_tensor(tiny[:, 8:9], tiny[:, 7:8], psR[:, 1:2], ALU.subtract))
                R.wait()
                R.then(v.scalar_tensor_tensor(win, win, tiny[:, 8:9], work, ALU.is_le, ALU.mult))
                R.wait()
                R.then(v.tensor_tensor(oneT, oneT, win, ALU.add))
                assert R.k == R_SEL, R.k

            def choose():
                v.wait_ge(S["route_pe"], 2)
                R.then(v.tensor_copy(work.rearrange("p (t j e) -> p j t e", j=J, e=E),
                                     psR[:].rearrange("p (j t e) -> p j t e", j=J, e=E)))
                R.wait()
                R.then(v.tensor_reduce(sm(6), te(work), AX_X, ALU.max))
                R.wait()
                R.then(v.tensor_scalar(sm(7), sm(6), 0.5, None, ALU.is_lt))
                R.wait()
                R.then(v.tensor_tensor(te(work), te(work), over_e(sm(7)), ALU.max))
                R.wait()
                R.then(v.tensor_tensor(win, probs, work, ALU.mult))
                R.then(v.tensor_scalar(mask8, work, -1.0, None, ALU.add))
                R.wait()
                R.then(v.tensor_tensor(win, win, mask8, ALU.add))
                R.wait()
                R.then(v.tensor_reduce(gate, te(win), AX_X, ALU.max))
                R.wait()
                R.then(v.tensor_tensor(te(work), te(win), over_e(gate), ALU.is_equal))
                R.wait()
                R.then(v.tensor_tensor(te(work), te(work),
                                       erev.rearrange("p (o e) -> p o e", o=1).to_broadcast([P, NTILE, E]), ALU.mult))
                R.wait()
                R.then(v.tensor_reduce(sm(6), te(work), AX_X, ALU.max))
                R.wait()
                R.then(v.tensor_tensor(te(pexp), te(work), over_e(sm(6)), ALU.is_equal))
                assert R.k == R_ONEHOT, R.k

            def keep_prefix():
                v.wait_ge(S["route_pe"], 3)
                R.then(v.tensor_copy(win, psR[:]))
                assert R.k == R_KEPT, R.k

            def place_tokens():
                v.wait_ge(S["route_pe"], 4)
                R.then(v.tensor_copy(et(logits), psR[:].rearrange("p (t e) -> p e t", e=E)))
                R.wait()
                R.then(v.tensor_tensor_scan(work, reset, logits, 0.0, ALU.mult, ALU.add))
                R.wait()
                c8 = lambda k: tiny[:, 16 + k * E:16 + (k + 1) * E]
                R.then(v.tensor_scalar(c8(0).bitcast(I32), et(work)[:, :, NTILE - 1], float(P - 1), None, ALU.add))
                R.wait()
                R.then(v.tensor_scalar(c8(1).bitcast(I32), c8(0).bitcast(I32), 7, None, ALU.logical_shift_right))
                R.wait()
                R.then(v.tensor_copy(c8(2), c8(1).bitcast(I32)))
                R.wait()
                R.then(v.tensor_tensor_scan(c8(3), ones[:, 0:E], c8(2), 0.0, ALU.mult, ALU.add))
                R.wait()
                R.then(v.tensor_tensor(c8(4), c8(3), c8(2), ALU.subtract))
                R.wait()
                R.then(v.tensor_scalar(c8(5), c8(4), float(P), -1.0, ALU.mult, ALU.add))
                R.then(v.tensor_tensor(work, work, logits, ALU.subtract))
                R.wait()
                R.then(v.tensor_tensor(et(work), et(work), c8(5).rearrange("p (e o) -> p e o", o=1).to_broadcast([P, E, NTILE]),
                                       ALU.add))
                R.wait()
                R.then(v.tensor_tensor(te(win), te(win), work.rearrange("p (e t) -> p t e", e=E), ALU.add))
                R.wait()
                R.then(v.tensor_tensor(win, win, pexp, ALU.mult))
                R.wait()
                R.then(v.tensor_reduce(sm(6), te(win), AX_X, ALU.add))
                R.wait()
                R.then(v.tensor_copy(place[:], sm(6)))
                R.wait()
                R.then(v.tensor_scalar(sm(2).bitcast(I32), place[:], P - 1, None, ALU.bitwise_and))
                R.then(v.tensor_scalar(sm(3).bitcast(I32), place[:], 7, None, ALU.logical_shift_right))
                R.wait()
                R.then(v.tensor_copy(sm(4), sm(2).bitcast(I32)))
                R.then(v.tensor_copy(sm(5), sm(3).bitcast(I32)))
                R.wait()
                R.then(v.scalar_tensor_tensor(place[:], sm(4), float(NT), sm(5), ALU.mult, ALU.add))
                R.then(v.tensor_scalar(info[:, :, 1:2].rearrange("p t o -> p (t o)"), gate, 0.5, None, ALU.mult))
                tw3 = tw[0:1, :].rearrange("p (n e) -> p n e", e=E)
                R.then(v.tensor_tensor(tw3, iota_sb[0:1, :].rearrange("p (n o) -> p n o", o=1).to_broadcast([1, NT, E]),
                                       c8(3)[0:1, :].rearrange("p (o e) -> p o e", o=1).to_broadcast([1, NT, E]), ALU.is_ge))
                R.wait()
                R.then(v.tensor_reduce(win[0:1, 0:NT], tw3, AX_X, ALU.add))
                R.wait()
                R.then(v.tensor_scalar(expert_at[:], win[0:1, 0:NT], float(E - 1), float(CH * F), ALU.min, ALU.mult))
                R.wait()
                v.tensor_copy(tiny[:, 60:61], tiny[:, 0:1]).then_inc(S["routed"], 1)
                R.end()

            def list_part(b):
                n = b - LIST_ROUND
                if not (isinstance(b, int) and b == LIST_ROUND):
                    wait_run(v, S["list_scattered"], n * (16 * LT))
                v.tensor_copy(place_cur[:], place[:, ds(n * LT, LT)])
                v.tensor_copy(info_cur[:].rearrange("p t w -> p (t w)"),
                              info[:].rearrange("p t w -> p (t w)")[:, ds(n * (4 * LT), 4 * LT)].bitcast(I32)
                              ).then_inc(S["list_cur"], 1)

            def listing(b, point):
                if point == 0:
                    list_part(b)

            def fetch(b):
                if not (isinstance(b, int) and b == 0):
                    wait_run(v, S["x0_ready"], b)
                v.tensor_copy(stats_cur[:].rearrange("p j s -> p (j s)"),
                              stats0[:].rearrange("p t s -> p (t s)")[:, ds(b * (2 * J), 2 * J)]
                              ).then_inc(S["fetched"], 1)

            def moments(b, mv, st, ready):
                xs = tile_row(b)
                for j in range(J):
                    ins = v.bn_stats(bnst[:, j], xs[:, j * C:(j + 1) * C])
                st.then(ins)
                st.wait()
                for j in range(J):
                    ins = v.bn_aggr(mv[:, j], bnst[:, j])
                ins.then_inc(S[ready], 1)

            def moments1(b):
                st = Steps(v, S["moments_step"], 1, b, S["waited"])
                wait_run(v, S["embedded"], b + 1)
                moments(b, mv1, st, "ln1_stats")
                st.end()

            def mix(b, ready, step, outs, done):
                st = Steps(v, S[step], 1, b, S["waited"])
                for c in range(CH):
                    v.wait_ge(S[ready], CH * b + (c + 1))
                    ins = v.tensor_tensor(dmix[:, c], hT[:, c, 1:SEQ + 1], hT[:, c, 0:SEQ], ALU.subtract)
                st.then(ins)
                st.wait()
                for dst, m in outs:
                    for c in range(CH):
                        ins = v.scalar_tensor_tensor(dst[:, c], dmix[:, c], vecs[:, c, V[m]:V[m] + 1],
                                                     hT[:, c, 0:SEQ], ALU.mult, ALU.add)
                    ins.then_inc(S[done], 1)
                st.end()

            def mix1(b):
                if not (isinstance(b, int) and b < 2):
                    wait_run(v, S["mix2_done"], b - 1)
                    wait_run(v, S["mixr2_done"], b - 1)
                mix(b, "h1_ready", "mix1_step", [(mixA[:, 0], "tmk"), (mixA[:, 1], "tmv")], "mix1_done")

            def mix2(b):
                if not (isinstance(b, int) and b == NB - 1):
                    wait_run(v, S["mix1_done"], 2 * b + 4)
                    wait_run(v, S["mixr1_done"], b + 2)
                mix(b, "h2_ready", "mix2_step", [(mixB[:, 0], "cmk")], "mix2_done")

            def wkv_before(b, c, st):
                k = kvs[:, 0, c, :]
                v.wait_ge(S["kvr_ready"], b * (3 * CH) + (c + 1))
                st.then(v.tensor_tensor_scan(pp[:, 1:SEQ + 1], wneg[:, c:c + 1].to_broadcast([P, SEQ]), k, -1e38,
                                             ALU.add, ALU.max))
                st.wait()
                st.then(v.tensor_tensor(qb[c], pp[:, 0:SEQ], k, ALU.subtract))
                st.wait()
                w, u = wneg[:, c:c + 1], uneg[:, c:c + 1]
                v.tensor_scalar(E1[c][:, 0], qb[c], w, 0.0, ALU.add, ALU.min)
                v.tensor_scalar(E1[c][:, 1], qb[c], u, 0.0, ALU.add, ALU.min).then_inc(S["pre_done"], 1)

            def wkv_after(b, c, st):
                e1, f1, e2, f2 = E1[c][:, 0], E1[c][:, 1], E2[c][:, 0], E2[c][:, 1]
                val = kvs[:, 1, c, :]
                v.wait_ge(S["exp_done"], b * (2 * CH) + (2 * c + 2))
                v.wait_ge(S["kvr_ready"], b * (3 * CH) + (CH + c + 1))
                v.tensor_tensor_scan(bb[:, 1:SEQ + 1], e1, e2, 0.0, ALU.mult, ALU.add)
                st.then(v.tensor_tensor(evb[c], e2, val, ALU.mult))
                st.wait()
                v.tensor_tensor_scan(aa[:, 1:SEQ + 1], e1, evb[c], 0.0, ALU.mult, ALU.add)
                v.tensor_tensor(t1b[c], f2, val, ALU.mult)
                st.then(v.tensor_tensor(qb[c], f1, bb[:, 0:SEQ], ALU.mult))
                st.wait()
                v.tensor_tensor(e1, f1, aa[:, 0:SEQ], ALU.mult)
                st.then(v.tensor_tensor(qb[c], qb[c], f2, ALU.add))
                st.wait()
                v.reciprocal(e2, qb[c])
                st.then(v.tensor_tensor(e1, e1, t1b[c], ALU.add))
                st.wait()
                st.then(v.tensor_tensor(e1, e1, e2, ALU.mult))
                st.wait()
                v.wait_ge(S["kvr_ready"], b * (3 * CH) + (2 * CH + c + 1))
                v.scalar_tensor_tensor(att[:, c], kvs[:, 2, c, :], 1.0, e1, ALU.add, ALU.mult
                                       ).then_inc(S["att_done"], 1)

            def wkv(b, extra, ahead):
                st = Steps(v, S["wkv_step"], 14, b, S["waited"])
                for c in range(CH):
                    wkv_before(b, c, st)
                for c in range(CH):
                    if c == 0 and not (isinstance(b, int) and b == 0):
                        wait_run(v, S["o_done"], b)
                    extra(b, c)
                    if c == 1 and ahead:
                        moments1(b + 1)
                    wkv_after(b, c, st)
                st.end()

            def residual1(b):
                st = Steps(v, S["ln2_step"], 1, b, S["waited"])
                v.wait_ge(S["o_done"], b + 1)
                xs = tile_row(b)
                v.tensor_tensor(xs, xs, psM[:, 1:3, :].rearrange("p b n -> p (b n)"), ALU.add).then_inc(S["x2_done"], 1)
                wait_run(v, S["x2_done"], b + 1)
                moments(b, mv2, st, "ln2_stats")
                st.end()

            def residual2(b):
                v.wait_ge(S["kv_done"], J * b + J)
                v.wait_ge(S["sigf_done"], 2 * b + 2)
                v.scalar_tensor_tensor(sigf, sigf, 1.0, psKV[:].rearrange("p b n -> p (b n)"), ALU.add, ALU.mult
                                       ).then_inc(S["s_mult"], 1)

            def round_(b, extra, ffn=True, ahead=True):
                if ahead:
                    fetch(b + 1)
                wkv(b, extra, ahead)
                if ahead:
                    mix1(b + 1)
                residual1(b)
                extra(b, 2)
                if ffn:
                    residual2(b - 1)
                extra(b, 3)
                mix2(b)

            statistics(0, 0, 0)
            router_weights()
            v.wait_ge(S["pow_ready"], 8)
            fetch(0)
            statistics(1, 1, 0)
            statistics(2, 0, 1)
            moments1(0)
            statistics(3, 1, 1)
            mix1(0)
            prepare()
            v.wait_ge(S["pow_ready"], 16)
            round_(0, router_point, ffn=False)
            with v.Fori(1, ROUTER_ROUNDS) as b:
                round_(b, router_point)
            v.wait_ge(S["pow_ready"], 24)
            round_(ROUTER_ROUNDS, softmax)
            with v.Fori(BIT_ROUND, SELECT_ROUND) as b:
                round_(b, try_bit)
            round_(SELECT_ROUND, route)
            round_(LIST_ROUND, route)
            with v.Fori(LIST_ROUND + 1, NB - 1) as b:
                round_(b, listing)
            round_(NB - 1, listing, ahead=False)

            def index_of(t):
                return list_sb[:, t, 0:1] if isinstance(t, int) else list_sb[:, ds(t, 1), 0:1].rearrange("p n w -> p (n w)")

            def take_index(t, i):
                v.tensor_copy(row_idx[i][:], index_of(t)).then_inc(S["idx_ready"], 1)

            def take_info(t, i):
                src = list_sb[:, t, :] if isinstance(t, int) else list_sb[:, ds(t, 1), :].rearrange("p n w -> p (n w)")
                v.tensor_copy(info_t[i][:], src.bitcast(F32)).then_inc(S["info_ready"], 1)

            def mlp_input(t, i):
                src = expert_at[0:1, t:t + 1] if isinstance(t, int) else expert_at[0:1, ds(t, 1)]
                w = v.value_load(src, min_val=0, max_val=(E - 1) * CH * F)
                if not (isinstance(t, int) and t < 2):
                    wait_run(v, S["h_done"], t - 1)
                v.tensor_copy(w1_t[i % 2].rearrange("p k f -> p (k f)"), w1_sb[:, ds(w, CH * F)])
                v.wait_ge(S["turned"], t + 1)
                v.tensor_copy(xnT[i % 2].rearrange("p k t -> p (k t)"), psT[:, i % 2, 0:C]
                              ).then_inc(S["mlp_in_ready"], 1)

            def combine(t, i, g):
                st = Steps(v, S["combine_step"], 2, t, S["waited"])
                th = th_t[i % 2]
                wait_run(v, S["tanh_done"], t + 1)
                if isinstance(t, int) and t < RING:
                    v.wait_ge(S[f"s_gathered{i}"], 16)
                v.tensor_copy(out_idx[i][:], index_of(t))
                st.then(v.scalar_tensor_tensor(out_t[i], y_ps[i % 2], info_t[i][:, 1:2],
                                               rows[i][:, C:2 * C], ALU.mult, ALU.mult))
                st.wait()
                st.then(v.scalar_tensor_tensor(th, th, 1.0, out_t[i], ALU.add, ALU.mult))
                st.wait()
                v.tensor_tensor(out_t[i], th, rows[i][:, 0:C], ALU.add).then_inc(S["combined"], 1)
                st.end()

            def step(t, i, g):
                if not isinstance(t, int) or t < NT - 3:
                    mlp_input(t + 3, (i + 3) % RING)
                if not isinstance(t, int) or t >= 0:
                    if not (isinstance(t, int) and t < RING):
                        wait_run(v, S[f"rows_out{i}"], g * 16)
                    combine(t, i, g)
                    if not isinstance(t, int) or t < NT - RING:
                        take_index(t + RING, i)
                if not isinstance(t, int) or t < NT - 4:
                    take_info(t + 4, (i + 4) % RING)

            v.wait_ge(S["list_in"], 16)
            for t in range(RING):
                take_index(t, t)
            take_info(0, 0)
            v.tensor_scalar(s_idx[:], list_sb[:, 0:RING, 0], 2.0, 1.0, ALU.mult, ALU.add).then_inc(S["s_idx_ready"], 1)
            residual2(NB - 1)
            v.wait_ge(S["w1_in"], 16 * E)
            steps(v, step)


def kernel(**inputs):
    import numpy as np
    import concourse.bacc as bacc
    from concourse.bass_utils import run_bass_kernel_spmd

    a = {k: np.asarray(v) for k, v in inputs.items()}
    x = np.ascontiguousarray(a["L0_attn_x"]).reshape(-1, a["L0_attn_x"].shape[-1])
    T, C = x.shape
    E = a["L0_ffn_Wg"].shape[1]
    names = dict(ln1_w="ln1_w", ln1_b="ln1_b", ln2_w="ln2_w", ln2_b="ln2_b", decay="time_decay",
                 first="time_first", tmk="tmk", tmv="tmv", tmr="tmr", cmk="cmk", cmr="cmr")
    p = np.arange(P)
    same = p[:, None] % E == p[None, :] % E
    consts = np.concatenate([
        p[:, None] == p[None, :], same, same & (p[:, None] < p[None, :]), p[:, None] <= p[None, :],
        np.ones((P, P)), np.broadcast_to(E - np.arange(E), (P, E))], axis=1).astype(np.float32)
    NT = T // P + E
    arrays = {
        "x": x,
        "xT": np.ascontiguousarray(x.T),
        "vec": np.stack([a["L0_attn_" + names[n]] for n in PARAMS], axis=1),
        "ln0_w": a["L0_attn_ln0_w"],
        "ln0_b": a["L0_attn_ln0_b"],
        **{n + "T": np.ascontiguousarray(a["L0_attn_" + n].T) for n in ("Wk", "Wv", "Wr", "Wo", "Wfk", "Wfr", "Wfv")},
        "Wg": a["L0_ffn_Wg"],
        "W1": a["L0_ffn_W1"],
        "W2": a["L0_ffn_W2"],
        "consts": consts,
        "tile_iota": np.arange(NT, dtype=np.float32)[None, :],
        "token_ids": np.arange(T, dtype=np.int32).reshape(T // P, P).T,
        "pad_rows": np.stack([T + np.arange(NT * P), *np.zeros((3, NT * P))], axis=1).astype(np.int32),
    }
    nc = bacc.Bacc("TRN2", target_bir_lowering=False, num_devices=1)
    feeds = {f"in_{n}": np.ascontiguousarray(v) for n, v in arrays.items()}
    args = [nc.dram_tensor(n, v.shape, mybir.dt.from_np(v.dtype), kind="ExternalInput").ap() for n, v in feeds.items()]
    args.append(nc.dram_tensor("sorted_list", (NT * P, 4), I32, kind="Internal").ap())
    args.append(nc.dram_tensor("xs_rows", (T, 2 * C), F32, kind="Internal").ap())
    args.append(nc.dram_tensor("out_0_dram", (T, C), F32, kind="ExternalOutput").ap())
    rwkv_times_moe(nc, *args)
    r = run_bass_kernel_spmd(nc, [feeds], core_ids=[0])
    return r.results[0]["out_0_dram"].reshape(a["L0_attn_x"].shape)
```

```python
from contextlib import ExitStack

import concourse.bass as bass
from concourse import mybir

F32 = mybir.dt.float32
I32 = mybir.dt.int32
F32R = mybir.dt.float32r
ALU = mybir.AluOpType
ACT = mybir.ActivationFunctionType
AX_X = mybir.AxisListType.X
ds = bass.ds

P = 128
ROUTER_ROUNDS = 3
BIT_ROUND = 4
SELECT_ROUND = BIT_ROUND + 7
LIST_ROUND = SELECT_ROUND + 1
RING = 6
R_PEXP, R_COUNTS, R_SEL, R_ONEHOT, R_KEPT, R_ALL = 9, 13, 18, 30, 31, 54
WKV_STEPS = 24
PARAMS = ["ln1_w", "ln1_b", "ln2_w", "ln2_b", "decay", "first", "tmk", "tmv", "tmr", "cmk", "cmr"]


class Steps:

    def __init__(self, eng, sem, per_run, run, waited):
        self.eng, self.sem, self.per_run, self.run, self.waited = eng, sem, per_run, run, waited
        self.k = 0

    def then(self, ins):
        ins.then_inc(self.sem, 1)
        self.k += 1
        return self.k

    def wait(self, k=None):
        self.eng.wait_ge(self.sem, self.run * self.per_run + (self.k if k is None else k))
        if not isinstance(self.run, int):
            self.eng.sem_inc(self.waited)

    def end(self):
        assert self.k == self.per_run, (self.k, self.per_run)


def rwkv_times_moe(nc, x, xT, vec, ln0_w, ln0_b, WkT, WvT, WrT, WoT, WfkT, WfrT, WfvT, Wg, W1, W2,
                   consts, tile_iota, token_ids, pad_rows, sorted_list, xs_rows, out):
    T, C = x.shape
    SEQ = 512
    NB = T // SEQ
    CH = C // P
    J = SEQ // P
    NTILE = T // P
    HID = WfkT.shape[1]
    HC = HID // P
    E, _, F = W1.shape
    FK = F // P
    CAP = max(1, T // E)
    EPS = 1e-5
    NT = sorted_list.shape[0] // P
    NCH = NTILE // J
    LT = NTILE // (NB - LIST_ROUND)
    assert CH == 2 and J == 4 and E * NCH == P and NT >= NTILE + E - 1 and NT % RING == 0
    assert NB == 4 * (ROUTER_ROUNDS + 1) and BIT_ROUND == ROUTER_ROUNDS + 1 and NTILE % LT == 0

    with ExitStack() as ctx:
        def sb(name, shape, dt=F32):
            return ctx.enter_context(nc.sbuf_tensor(name, shape, dt))

        def sem(name):
            return ctx.enter_context(nc.semaphore(name))

        s_ring = sb("s_ring", [P, 4 * J * C])
        vecs = sb("vecs", [P, CH, len(PARAMS)])
        V = {n: i for i, n in enumerate(PARAMS)}
        wneg = sb("wneg", [P, CH])
        uneg = sb("uneg", [P, CH])
        w0_bc = sb("w0_bc", [P, C])
        b0_bc = sb("b0_bc", [P, C])
        cst = sb("cst", [P, 5, P])
        ident, esum, eprefix, prefix, ones = (cst[:, i, :] for i in range(5))
        stats0 = sb("stats0", [P, NTILE, 2])
        info = sb("info", [P, NTILE, 4])
        place = sb("place", [P, NTILE], I32)
        expert_at = sb("expert_at", [1, NT], I32)
        stats_cur = sb("stats_cur", [P, J, 2])
        place_cur = sb("place_cur", [P, LT], I32)
        info_cur = sb("info_cur", [P, LT, 4], I32)
        bnst = sb("bnst", [P, J, 6])
        bnst0 = sb("bnst0", [P, J, 6])
        mv0 = sb("mv0", [P, J, 2])
        mv1 = sb("mv1", [P, J, 2])
        mv2 = sb("mv2", [P, J, 2])
        cf1 = sb("cf1", [P, 2, J])
        cf2 = sb("cf2", [P, 2, J])
        lnw1 = sb("lnw1", [P, 2, J])
        lnw2 = sb("lnw2", [P, 2, J])
        minus_half = sb("minus_half", [P, NTILE])

        mix_hi, mix_lo = (sb(n, [P, CH, SEQ], F32R) for n in ("mix_hi", "mix_lo"))
        wfk_hi, wfk_lo = (sb(n, [P, CH, HID], F32R) for n in ("wfk_hi", "wfk_lo"))

        ARENA = 30217
        arena = sb("arena", [P, ARENA])
        at = [0]

        def part(n):
            at[0] += n
            assert at[0] <= ARENA
            return arena[:, at[0] - n:at[0]]

        first_dead = at[0]
        mixA = part(3 * CH * SEQ).rearrange("p (m c t) -> p m c t", m=3, c=CH)
        dmix = part(CH * SEQ).rearrange("p (c t) -> p c t", c=CH)
        kvs = part(3 * CH * SEQ).rearrange("p (m c t) -> p m c t", m=3, c=CH)
        E1 = [part(2 * SEQ).rearrange("p (m t) -> p m t", m=2) for _ in range(CH)]
        E2 = [part(2 * SEQ).rearrange("p (m t) -> p m t", m=2) for _ in range(CH)]
        qb = [part(SEQ) for _ in range(CH)]
        kx = part(CH * SEQ).rearrange("p (c t) -> p c t", c=CH)
        evb, t1b = kx[:, 0], kx[:, 1]
        pp = [part(SEQ + 1) for _ in range(CH)]
        aa = part(SEQ + 1)
        bb = part(SEQ + 1)
        att = part(CH * SEQ).rearrange("p (c t) -> p c t", c=CH)
        hT = part(CH * (SEQ + 1)).rearrange("p (c t) -> p c t", c=CH)
        hn = part(J * C).rearrange("p (j c) -> p j c", j=J)
        moe_end = at[0]
        x_in = part(J * C).rearrange("p (j c) -> p j c", j=J)
        mixB_r = part(CH * SEQ).rearrange("p (c t) -> p c t", c=CH)
        kf2 = part(HC * SEQ).rearrange("p (h t) -> p h t", h=HC)
        sigf = part(J * C)
        wk, wv, wr, wo, wfr = (part(CH * C).rearrange("p (k n) -> p k n", k=CH) for _ in range(5))
        wfk = kf2.rearrange("p h t -> p (h t)")[:, 0:CH * HID].rearrange("p (k n) -> p k n", k=CH)
        wfv = part(HC * C).rearrange("p (k n) -> p k n", k=HC)
        DESK = 10240
        desk = sb("desk", [P, DESK])
        xa = [desk[:, i * 1024:(i + 1) * 1024].rearrange("p (j c) -> p j c", j=J) for i in range(2)]
        xta = [desk[:, 2048 + i * 1024:3072 + i * 1024].rearrange("p (k t) -> p k t", k=CH) for i in range(2)]
        ra = 4096
        NE = NTILE * E

        def routing(n=NE):
            nonlocal ra
            ra += n
            assert ra <= DESK
            return desk[:, ra - n:ra]

        logits, probs, work, pexp, selT, oneT, win, mask8 = (routing() for _ in range(8))
        small = routing(8 * NTILE)
        mvA = routing(2 * NTILE)
        wg_sb = routing(CH * E)
        wgc = routing(CH * E)
        erev = routing(E)
        gate = routing(NTILE)
        reset = routing(NE)
        ids_sb = routing(NTILE).bitcast(I32)
        tiny = routing(64)
        iota_sb = routing(NT)
        tw = routing(NT * E)
        w2_sb = desk[:, 0:E * CH * F]
        w1_sb = arena[:, first_dead:first_dead + E * CH * F]
        rc = [first_dead + E * CH * F]

        def ring(n, depth):
            rc[0] += n * depth
            assert rc[0] <= moe_end
            return [arena[:, rc[0] - n * (d + 1):rc[0] - n * d] for d in range(depth)]

        rows = ring(2 * C, RING)
        xn_t = ring(C, 2)
        xnT = [a.rearrange("p (k t) -> p k t", k=CH) for a in ring(C, 2)]
        w1_t = [a.rearrange("p (k f) -> p k f", k=CH) for a in ring(CH * F, 2)]
        hT_t = [a.rearrange("p (f t) -> p f t", f=FK) for a in ring(F, 2)]
        th_t = ring(C, 2)
        out_t = ring(C, RING)
        list_sb = sb("list_sb", [P, NT, 4], I32)
        row_idx = [sb(f"row_idx{i}", [P, 1], I32) for i in range(RING)]
        s_idx = sb("s_idx", [P, RING], I32)
        out_idx = [sb(f"out_idx{i}", [P, 1], I32) for i in range(RING)]
        info_t = [sb(f"info_t{i}", [P, 4]) for i in range(RING)]

        psT = ctx.enter_context(nc.psum_tensor("psT", [P, 2, 512], F32))
        psM = ctx.enter_context(nc.psum_tensor("psM", [P, 3, 512], F32))
        psKV = ctx.enter_context(nc.psum_tensor("psKV", [P, 2, 512], F32))
        psR = ctx.enter_context(nc.psum_tensor("psR", [P, 512], F32))

        names = """waited params_in ident_in consts_in xa_in0 xa_in1 xta_in0 xta_in1 weights_in proj_w_in wg_in halved
        a_step a_stats logits_done logits_kept wg_mean wg_ready decay_exp pool_const columns_set
        pow_ready bit_step bit_counted bit_summed route_step route_pe route_exp_in route_exp_out
        probs_turned routed pads_out list_cur list_scattered list_in w1_in w2_in
        x_in x_out s_out fetched x0_ready scaled0 embedded moments_step ln1_stats cf1_ready hn1_ready tr1_done
        h1_ready mix1_step mix1_done mixr_scaled mixr1_done proj_done kvr_ready
        wkv_step pre_done relu2_done exp_done att_done o_done
        x2_done ln2_step ln2_stats cf2_ready hn2_ready tr2_done h2_ready mix2_step
        mixk_done mixk_hi wfk_hi_done mix2_done mixr2_done
        kf_done relu_done sq_done fr_done sigf_done kv_done s_done s_mult rstd1_step rstd2_step
        rows_zeroed idx_ready s_idx_ready info_ready xn_done turned mlp_in_ready h_done gelu_done y_done tanh_done
        combine_step combined""".split()
        names += [f"{n}{i}" for n in ("gathered", "s_gathered") for i in range(RING)] + [f"rows_out{i}" for i in range(RING)]
        S = {n: sem(n) for n in names}

        def tile_row(b):
            return s_ring[:, ds((b & 3) * (J * C), J * C)]

        def wait_run(eng, s, value):
            eng.wait_ge(s, value)
            if not isinstance(value, int):
                eng.sem_inc(S["waited"])

        xT_k = xT.rearrange("(k p) t -> p k t", p=P)
        xrows = x.rearrange("(n p) c -> p n c", p=P)
        xs_store = xs_rows.rearrange("(n p) c -> p n c", p=P)
        y_ps = [psM[:, 2, 0:C], psR[:, 0:C]]

        def steps(eng, step):
            for t in range(-3, RING):
                step(t, t % RING, t // RING)
            with eng.Fori(1, NT // RING - 1) as g:
                for i in range(RING):
                    step(RING * g + i, i, g)
            for t in range(NT - RING, NT):
                step(t, t % RING, t // RING)

        block = ctx.enter_context(nc.Block())

        @block.sync
        def _(sp):
            def load_tokens(n):
                if n >= 2:
                    sp.wait_ge(S["a_stats"], n - 1)
                sp.dma_start(xa[n % 2], xrows[:, n * J:(n + 1) * J, :]).then_inc(S[f"xa_in{n % 2}"], 16)

            def load_channels(n):
                if n >= 2:
                    sp.wait_ge(S["logits_done"], n - 1)
                sp.dma_start(xta[n % 2], xT_k[:, :, n * SEQ:(n + 1) * SEQ]).then_inc(S[f"xta_in{n % 2}"], 16)

            def load_weights(ready, *pairs):
                for w_sb, w_dram in pairs:
                    sp.dma_start(w_sb, w_dram.rearrange("(k p) n -> p k n", p=P)).then_inc(S[ready], 16)

            def load_x(b):
                sp.dma_start(x_in, xrows[:, ds(b * J, J), :]).then_inc(S["x_in"], 16)
                store_x(b)

            def store_x(b):
                wait_run(sp, S["x_in"], b * 16 + 16)
                sp.dma_start(xs_store[:, ds(b * J, J), 0:C], x_in).then_inc(S["x_out"], 16)

            def x_free(b):
                wait_run(sp, S["embedded"], b)

            def store_s(b):
                wait_run(sp, S["s_done"], b + 1)
                sp.dma_start(xs_store[:, ds(b * J, J), C:2 * C],
                             tile_row(b).rearrange("p (j c) -> p j c", j=J)).then_inc(S["s_out"], 16)

            load_tokens(0)
            sp.dma_start(x_in, xrows[:, 0:J, :]).then_inc(S["x_in"], 16)
            load_tokens(1)
            sp.dma_start(cst[:], consts[:, 0:5 * P].rearrange("p (i q) -> p i q", i=5)).then_inc(S["ident_in"], 16)
            sp.dma_start(wg_sb.rearrange("p (k e) -> p k e", k=CH),
                         Wg.rearrange("(k p) e -> p k e", p=P)).then_inc(S["wg_in"], 16)
            sp.dma_start(vecs[:], vec.rearrange("(c p) n -> p c n", p=P)).then_inc(S["params_in"], 16)
            sp.dma_start(w0_bc[:], ln0_w.partition_broadcast(P)).then_inc(S["params_in"], 16)
            sp.dma_start(b0_bc[:], ln0_b.partition_broadcast(P)).then_inc(S["params_in"], 16)
            load_channels(0)
            load_channels(1)
            load_weights("proj_w_in", (wk, WkT), (wv, WvT), (wr, WrT))
            store_x(0)
            for n in (2, 3):
                load_tokens(n)
                load_channels(n)
            load_weights("weights_in", (wo, WoT), (wfv, WfvT), (wfk, WfkT), (wfr, WfrT))
            sp.dma_start(erev, consts[:, 5 * P:5 * P + E]).then_inc(S["consts_in"], 16)
            sp.dma_start(iota_sb[0:1, :], tile_iota).then_inc(S["consts_in"], 16)
            sp.dma_start(ids_sb, token_ids).then_inc(S["consts_in"], 16)
            sp.dma_start(sorted_list, pad_rows).then_inc(S["pads_out"], 16)

            x_free(1)
            load_x(1)
            for n in (4, 5):
                load_tokens(n)
                load_channels(n)
            for b in range(ROUTER_ROUNDS):
                if b + 2 == 4:
                    store_s(0)
                    sp.wait_ge(S["s_out"], 16)
                x_free(b + 2)
                load_x(b + 2)
                for n in range(4 * b + 6, min(4 * b + 10, NB)):
                    load_tokens(n)
                    load_channels(n)
            store_s(1)
            with sp.Fori(5, NB) as b:
                x_free(b)
                wait_run(sp, S["s_out"], (b - 3) * 16)
                load_x(b)
                store_s(b - 3)
            sp.wait_ge(S["routed"], 1)
            for e in range(E):
                sp.dma_start(w2_sb.rearrange("p (e k f) -> p e k f", e=E, k=FK)[:, e],
                             W2[e].rearrange("(k p) f -> p k f", p=P)).then_inc(S["w2_in"], 16)
            store_s(NB - 3)
            sp.wait_ge(S["list_scattered"], 16 * NTILE)
            sp.dma_start(list_sb[:].rearrange("p n w -> p (n w)"),
                         sorted_list.rearrange("(p n) w -> p (n w)", p=P)).then_inc(S["list_in"], 16)
            sp.wait_ge(S["mix2_done"], NB)
            sp.wait_ge(S["mixr2_done"], NB)
            for e in range(E):
                sp.dma_start(w1_sb.rearrange("p (e k f) -> p e k f", e=E, k=CH)[:, e],
                             W1[e].rearrange("(k p) f -> p k f", p=P)).then_inc(S["w1_in"], 16)
            store_s(NB - 2)
            store_s(NB - 1)

        @block.gpsimd
        def _(pool):
            pool.memset(minus_half[:], -0.5).then_inc(S["pool_const"], 1)
            pool.wait_ge(S["pool_const"], 1)

            mv = mvA.rearrange("p (n s) -> p n s", s=2)
            sv = small.rearrange("p (k n) -> p k n", n=NTILE)

            def norm_scales(g, first, last):
                st = Steps(pool, S["pow_ready"], 8, g, S["waited"])
                n = slice(first * J, (last + 1) * J)
                mean, var, half = mv[:, n, 0], mv[:, n, 1], minus_half[:, n]
                scale0, offset0, r, offset = stats0[:, n, 0], stats0[:, n, 1], info[:, n, 2], info[:, n, 3]
                pool.wait_ge(S["a_step"], 2 * last + 2)
                st.then(pool.tensor_scalar(sv[:, 0, n], var, EPS, 1.0, ALU.add, ALU.mult))
                st.wait()
                st.then(pool.tensor_tensor(r, sv[:, 0, n], half, ALU.pow))
                st.wait()
                pool.tensor_tensor(sv[:, 1, n], var, r, ALU.mult)
                st.then(pool.tensor_scalar(sv[:, 2, n], mean, -1.0, 0.0, ALU.mult, ALU.add))
                st.wait()
                st.then(pool.tensor_tensor(sv[:, 3, n], sv[:, 1, n], r, ALU.mult))
                st.wait()
                st.then(pool.tensor_scalar(sv[:, 4, n], sv[:, 3, n], EPS, 1.0, ALU.add, ALU.mult))
                st.wait()
                st.then(pool.tensor_tensor(sv[:, 5, n], sv[:, 4, n], half, ALU.pow))
                st.wait()
                st.then(pool.tensor_tensor(scale0, sv[:, 5, n], r, ALU.mult))
                st.wait()
                pool.tensor_tensor(offset0, sv[:, 2, n], scale0, ALU.mult)
                st.then(pool.tensor_tensor(offset, sv[:, 2, n], r, ALU.mult))
                st.end()

            def add_to_list(b, half):
                wait_run(pool, S["list_cur"], b - (LIST_ROUND - 1))
                if isinstance(b, int) and b == LIST_ROUND:
                    pool.wait_ge(S["pads_out"], 16)
                for j in range(half * LT // 2, (half + 1) * LT // 2):
                    pool.indirect_dma_start(sorted_list[:, :], bass.IndirectOffsetOnAxis(place_cur[:, j:j + 1], axis=0),
                                            info_cur[:, j, :], None).then_inc(S["list_scattered"], 16)

            def rstd(b, stats, mv, lnw, cf, step, ready):
                st = Steps(pool, S[step], 2, b, S["waited"])
                wait_run(pool, S[stats], b + 1)
                pool.tensor_scalar(lnw[:, 0], mv[:, :, 1], EPS, 1.0, ALU.add, ALU.mult)
                st.then(pool.tensor_scalar(lnw[:, 1], mv[:, :, 0], -1.0, 0.0, ALU.mult, ALU.add))
                st.wait()
                st.then(pool.tensor_tensor(cf[:, 0], lnw[:, 0], minus_half[:, 0:J], ALU.pow))
                st.wait()
                pool.tensor_tensor(cf[:, 1], lnw[:, 1], cf[:, 0], ALU.mult).then_inc(S[ready], 1)
                st.end()

            def embed(b):
                wait_run(pool, S["x0_ready"], b + 1)
                if isinstance(b, int) and b == 0:
                    pool.wait_ge(S["params_in"], 48)
                over_j = lambda a: a[:].rearrange("p (o c) -> p o c", o=1).to_broadcast([P, J, C])
                pool.tensor_tensor(x_in, x_in, over_j(w0_bc), ALU.mult).then_inc(S["scaled0"], 1)
                wait_run(pool, S["scaled0"], b + 1)
                pool.tensor_tensor(tile_row(b).rearrange("p (j c) -> p j c", j=J), x_in, over_j(b0_bc), ALU.add
                                   ).then_inc(S["embedded"], 1)

            def mix_r(b, step, dst, m, done, scaled):
                wait_run(pool, S[step], CH * b + CH)
                for c in range(CH):
                    ins = pool.tensor_scalar(dst[:, c], dmix[:, c], vecs[:, c, V[m]:V[m] + 1], 0.0, ALU.mult, ALU.add)
                ins.then_inc(S["mixr_scaled"], 1)
                wait_run(pool, S["mixr_scaled"], scaled)
                pool.tensor_tensor(dst, dst, hT[:, :, 0:SEQ], ALU.add).then_inc(S[done], 1)

            def mix_r1(b):
                mix_r(b, "mix1_step", mixA[:, 2], "tmr", "mixr1_done", 2 * b if not isinstance(b, int) or b else 1)

            def mix_r2(b):
                mix_r(b, "mix2_step", mixB_r, "cmr", "mixr2_done", 2 * b + (2 if isinstance(b, int) and b == NB - 1 else 3))

            def residual2(b):
                wait_run(pool, S["s_mult"], b + 1)
                xs = tile_row(b)
                pool.tensor_tensor(xs, xs, sigf, ALU.add).then_inc(S["s_done"], 1)

            def rstd1(b):
                rstd(b, "ln1_stats", mv1, lnw1, cf1, "rstd1_step", "cf1_ready")

            def rstd2(b):
                rstd(b, "ln2_stats", mv2, lnw2, cf2, "rstd2_step", "cf2_ready")

            def round_(b, listing=False, ahead=True):
                if ahead:
                    embed(b + 1)
                if listing:
                    add_to_list(b, 0)
                if not (isinstance(b, int) and b < 2):
                    residual2(b - 2)
                if ahead:
                    rstd1(b + 1)
                if listing:
                    add_to_list(b, 1)
                if ahead:
                    mix_r1(b + 1)
                rstd2(b)
                mix_r2(b)

            norm_scales(0, 0, 0)
            embed(0)
            rstd1(0)
            norm_scales(1, 1, 3)
            mix_r1(0)
            for b in range(ROUTER_ROUNDS):
                round_(b)
                norm_scales(b + 2, 4 * b + 4, 4 * b + 7)
            with pool.Fori(ROUTER_ROUNDS, LIST_ROUND) as b:
                round_(b)
            round_(LIST_ROUND, listing=True)
            with pool.Fori(LIST_ROUND + 1, NB - 1) as b:
                round_(b, listing=True)
            round_(NB - 1, listing=True, ahead=False)
            residual2(NB - 2)

            def gather(t, i, columns=slice(0, 2 * C), source=xs_rows[:, :]):
                wait_run(pool, S["idx_ready"], t + 1)
                pool.indirect_dma_start(rows[i][:, columns], None, source,
                                        bass.IndirectOffsetOnAxis(row_idx[i][:, 0:1], axis=0),
                                        bounds_check=T - 1, oob_is_err=False).then_inc(S[f"gathered{i}"], 16)

            def gather_s(t):
                pool.wait_ge(S["s_idx_ready"], 1)
                pool.indirect_dma_start(rows[t][:, C:2 * C], None, xs_rows.rearrange("t (h c) -> (t h) c", h=2),
                                        bass.IndirectOffsetOnAxis(s_idx[:, t:t + 1], axis=0),
                                        bounds_check=2 * T - 1, oob_is_err=False).then_inc(S[f"s_gathered{t}"], 16)

            def scatter(t, i):
                wait_run(pool, S["combined"], t + 1)
                pool.indirect_dma_start(out[:, :], bass.IndirectOffsetOnAxis(out_idx[i][:, 0:1], axis=0),
                                        out_t[i], None, bounds_check=T - 1, oob_is_err=False
                                        ).then_inc(S[f"rows_out{i}"], 16)

            pool.wait_ge(S["mix2_done"], NB)
            pool.wait_ge(S["mixr2_done"], NB)
            for i in range(RING):
                ins = pool.memset(rows[i], 0.0)
            ins.then_inc(S["rows_zeroed"], 1)
            pool.wait_ge(S["rows_zeroed"], 1)
            for t in range(RING):
                gather(t, t, slice(0, C), x[:, :])
            residual2(NB - 1)
            pool.wait_ge(S["x_out"], 16 * NB)
            pool.wait_ge(S["s_out"], 16 * NB)
            for t in range(RING):
                gather_s(t)
            with pool.Fori(0, NT // RING - 1) as g:
                for i in range(RING):
                    scatter(RING * g + i, i)
                    gather(RING * g + (RING + i), i)
            for i in range(RING):
                scatter(NT - RING + i, i)
            for i in range(RING):
                pool.wait_ge(S[f"rows_out{i}"], 16 * (NT // RING))

        @block.scalar
        def _(act):
            act.wait_ge(S["params_in"], 48)
            act.activation(wneg[:], vecs[:, :, V["decay"]], ACT.Exp).then_inc(S["decay_exp"], 1)

            def norm0(b):
                wait_run(act, S["fetched"], b + 1)
                wait_run(act, S["x_out"], 16 * b + 16)
                for j in range(J):
                    ins = act.activation(x_in[:, j], x_in[:, j], ACT.Identity,
                                         scale=stats_cur[:, j, 0:1], bias=stats_cur[:, j, 1:2])
                ins.then_inc(S["x0_ready"], 1)

            def norm(b, cf, cf_ready, ready):
                wait_run(act, S[cf_ready], b + 1)
                xs = tile_row(b)
                for j in range(J):
                    ins = act.activation(hn[:, j], xs[:, j * C:(j + 1) * C], ACT.Identity,
                                         scale=cf[:, 0, j:j + 1], bias=cf[:, 1, j:j + 1])
                ins.then_inc(S[ready], 1)

            def affine(b, tr_done, w, bias, ready):
                wait_run(act, S[tr_done], b + 1)
                for c in range(CH):
                    act.activation(hT[:, c, 1:SEQ + 1], psT[:, c, :], ACT.Identity,
                                   scale=vecs[:, c, V[w]:V[w] + 1], bias=vecs[:, c, V[bias]:V[bias] + 1]
                                   ).then_inc(S[ready], 1)

            def norm1(b):
                if not (isinstance(b, int) and b < 2):
                    wait_run(act, S["tr2_done"], b - 1)
                norm(b, cf1, "cf1_ready", "hn1_ready")

            def affine1(b):
                if not (isinstance(b, int) and b < 2):
                    wait_run(act, S["mixr2_done"], b - 1)
                affine(b, "tr1_done", "ln1_w", "ln1_b", "h1_ready")

            def norm2(b):
                if not (isinstance(b, int) and b == NB - 1):
                    wait_run(act, S["tr1_done"], b + 2)
                norm(b, cf2, "cf2_ready", "hn2_ready")

            def affine2(b):
                if not (isinstance(b, int) and b == NB - 1):
                    wait_run(act, S["mix1_done"], 2 * b + 4)
                    wait_run(act, S["mixr1_done"], b + 2)
                affine(b, "tr2_done", "ln2_w", "ln2_b", "h2_ready")

            def take_kvr(b, lo, hi):
                if lo == 0 and not (isinstance(b, int) and b == 0):
                    wait_run(act, S["att_done"], 2 * b)
                for u in range(lo, hi):
                    act.wait_ge(S["proj_done"], b * (3 * CH) + (u + 1))
                    dst, src = kvs[:, u // CH, u % CH, :], psM[:, u % 3, :]
                    if u // CH == 2:
                        act.activation(dst, src, ACT.Tanh, scale=0.5).then_inc(S["kvr_ready"], 1)
                    else:
                        act.activation(dst, src, ACT.Copy).then_inc(S["kvr_ready"], 1)

            def exponents(b, c):
                wait_run(act, S["pre_done"], b * CH + (c + 1))
                act.activation(E2[c][:, 0], qb[c], ACT.Relu, bias=wneg[:, c:c + 1])
                act.activation(E2[c][:, 1], qb[c], ACT.Relu, bias=uneg[:, c:c + 1]).then_inc(S["relu2_done"], 1)

            def exps(b, c):
                act.activation(E1[c], E1[c], ACT.Exp).then_inc(S["exp_done"], 1)
                wait_run(act, S["relu2_done"], b * CH + (c + 1))
                act.activation(E2[c], E2[c], ACT.Exp, scale=-1.0).then_inc(S["exp_done"], 1)

            def split_mix(b, c):
                wait_run(act, S["mixk_done"], CH * b + (c + 1))
                act.activation(mix_hi[:, c], kx[:, c], ACT.Copy).then_inc(S["mixk_hi"], 1)

            def relu(b, h):
                act.wait_ge(S["kf_done"], b * HC + (h + 1))
                act.activation(kf2[:, h], psM[:, h % 3, :], ACT.Relu).then_inc(S["relu_done"], 1)

            def square(b, h):
                act.wait_ge(S["relu_done"], b * HC + (h + 1))
                act.activation(kf2[:, h], kf2[:, h], ACT.Square).then_inc(S["sq_done"], 1)

            def sigmoid_fr(b):
                if not (isinstance(b, int) and b == 0):
                    wait_run(act, S["s_done"], b)
                for u in range(2):
                    act.wait_ge(S["fr_done"], 2 * b + (u + 1))
                    act.activation(sigf[:, u * 512:(u + 1) * 512], psM[:, (HC + u) % 3, :],
                                   ACT.Tanh, scale=0.5).then_inc(S["sigf_done"], 1)

            def relus(b, *chunks):
                for h in chunks:
                    relu(b, h)

            def squares(b, *chunks):
                for h in chunks:
                    square(b, h)

            def round_(b, ffn=True, ahead=True, softmax=False, further=True):
                if ffn:
                    exponents(b, 1)
                    relus(b - 1, 0, 1)
                    exps(b, 1)
                    relus(b - 1, 2, 3)
                    for h in range(4, HC):
                        squares(b - 1, h - 4)
                        relus(b - 1, h)
                    squares(b - 1, *range(HC - 4, HC))
                if softmax:
                    act.wait_ge(S["route_exp_in"], 1)
                    act.activation(probs, logits, ACT.Exp).then_inc(S["route_exp_out"], 1)
                if ahead:
                    norm1(b + 1)
                if ffn:
                    sigmoid_fr(b - 1)
                if ahead:
                    affine1(b + 1)
                    if further:
                        norm0(b + 2)
                    take_kvr(b + 1, 0, 2)
                norm2(b)
                if ahead:
                    take_kvr(b + 1, 2, 4)
                if ahead:
                    exponents(b + 1, 0)
                affine2(b)
                for c in range(CH):
                    if ahead:
                        take_kvr(b + 1, 4 + c, 5 + c)
                        if c == 0:
                            exps(b + 1, 0)
                    split_mix(b, c)

            norm0(0)
            norm1(0)
            act.wait_ge(S["weights_in"], 16 * 4)
            act.activation(wfk_hi[:], wfk, ACT.Copy).then_inc(S["wfk_hi_done"], 1)
            affine1(0)
            take_kvr(0, 0, 2)
            exponents(0, 0)
            exps(0, 0)
            take_kvr(0, 2, 4)
            exponents(0, 1)
            exps(0, 1)
            norm0(1)
            take_kvr(0, 4, 6)
            round_(0, ffn=False)
            with act.Fori(1, ROUTER_ROUNDS) as b:
                round_(b)
            round_(ROUTER_ROUNDS, softmax=True)
            with act.Fori(BIT_ROUND, NB - 2) as b:
                round_(b)
            round_(NB - 2, further=False)
            round_(NB - 1, ahead=False)
            relus(NB - 1, *range(HC))
            squares(NB - 1, *range(HC))
            sigmoid_fr(NB - 1)

            def xn(t, i, g):
                act.wait_ge(S[f"gathered{i}"], g * 16 + 16)
                wait_run(act, S["info_ready"], t + 1)
                if not (isinstance(t, int) and t < 2):
                    wait_run(act, S["turned"], t - 1)
                nf = info_t[i]
                act.activation(xn_t[i % 2], rows[i][:, 0:C], ACT.Identity, scale=nf[:, 2:3], bias=nf[:, 3:4]
                               ).then_inc(S["xn_done"], 1)

            def gelu(t, i):
                if not (isinstance(t, int) and t < 2):
                    wait_run(act, S["y_done"], t - 1)
                act.wait_ge(S["h_done"], t + 1)
                act.activation(hT_t[i % 2].rearrange("p f t -> p (f t)"), psM[:, i % 2, :], ACT.Gelu
                               ).then_inc(S["gelu_done"], 1)

            def tanh(t, i):
                if not (isinstance(t, int) and t < 2):
                    wait_run(act, S["combined"], t - 1)
                wait_run(act, S["y_done"], t + 1)
                act.activation(th_t[i % 2], y_ps[i % 2], ACT.Tanh, scale=info_t[i][:, 1:2]
                               ).then_inc(S["tanh_done"], 1)

            def step(t, i, g):
                if not isinstance(t, int) or -3 <= t < NT - 3:
                    xn(t + 3, (i + 3) % RING, g + (i + 3) // RING)
                if not isinstance(t, int) or -1 <= t < NT - 1:
                    gelu(t + 1, (i + 1) % RING)
                if not isinstance(t, int) or t >= 0:
                    tanh(t, i)

            steps(act, step)

        @block.tensor
        def _(pe):
            def router_weights():
                pe.wait_ge(S["wg_in"], 16)
                for k in range(CH):
                    ins = pe.matmul(psR[:, 0:E], ones, wg_sb[:, k * E:(k + 1) * E], start=(k == 0), stop=(k == CH - 1))
                ins.then_inc(S["wg_mean"], 1)
                pe.wait_ge(S["wg_ready"], 1)

            def router(n, q, g):
                pe.wait_ge(S[f"xta_in{q % 2}"], g * 16 + 16)
                if not (isinstance(n, int) and n < 4):
                    wait_run(pe, S["logits_kept"], n - 3)
                for j in range(J):
                    for k in range(CH):
                        ins = pe.matmul(psR[:, (q * J + j) * E:(q * J + j + 1) * E], xta[q % 2][:, k, j * P:(j + 1) * P],
                                        wgc[:, k * E:(k + 1) * E], start=(k == 0), stop=(k == CH - 1))
                ins.then_inc(S["logits_done"], 1)

            def router_point(b, point):
                router(b * 4 + (4 + point), point, b * 2 + (2 + point // 2))

            def sum_bit(b, point):
                pe.wait_ge(S["bit_counted"], (b - BIT_ROUND) * 4 + (point + 3))
                pe.matmul(psR[:, 0:1], esum, tiny[:, 4:5], start=True, stop=True).then_inc(S["bit_summed"], 1)

            def softmax(b, point):
                if point == 1:
                    pe.wait_ge(S["route_step"], R_PEXP)
                    for j in range(J):
                        ins = pe.transpose(psR[:, j * P:(j + 1) * P], pexp[:, j * P:(j + 1) * P], ident)
                    ins.then_inc(S["probs_turned"], 1)
                elif point >= 2:
                    sum_bit(b, point)

            def route(b, point):
                pe.wait_ge(S["route_step"], (R_COUNTS, R_SEL, R_ONEHOT, R_KEPT)[point])
                if point == 0:
                    pe.matmul(psR[:, 0:1], esum, tiny[:, 5:6], start=True, stop=True)
                    ins = pe.matmul(psR[:, 1:2], eprefix, tiny[:, 6:7], start=True, stop=True)
                elif point == 1:
                    for j in range(J):
                        ins = pe.transpose(psR[:, j * P:(j + 1) * P], oneT[:, j * P:(j + 1) * P], ident)
                elif point == 2:
                    ins = pe.matmul(psR[:], prefix, pexp, start=True, stop=True)
                else:
                    ins = pe.matmul(psR[:], ones, pexp, start=True, stop=True)
                ins.then_inc(S["route_pe"], 1)

            nothing = lambda b, point: None

            def turn(b, ready, done):
                wait_run(pe, S[ready], b + 1)
                for c in range(CH):
                    for j in range(J):
                        ins = pe.transpose(psT[:, c, j * P:(j + 1) * P], hn[:, j, c * P:(c + 1) * P], ident)
                ins.then_inc(S[done], 1)

            def turn1(b):
                if not (isinstance(b, int) and b < 2):
                    wait_run(pe, S["h2_ready"], CH * b - CH)
                turn(b, "hn1_ready", "tr1_done")

            def turn2(b):
                wait_run(pe, S["h1_ready"], CH * b + 2 * CH) if not (isinstance(b, int) and b == NB - 1) else None
                turn(b, "hn2_ready", "tr2_done")

            def project(b, *ms):
                for m in ms:
                    w = (wk, wv, wr)[m]
                    if m < 2:
                        wait_run(pe, S["mix1_done"], 2 * b + (m + 1))
                    else:
                        wait_run(pe, S["mixr1_done"], b + 1)
                    for c in range(CH):
                        u = m * CH + c
                        if u >= 3:
                            pe.wait_ge(S["kvr_ready"], b * (3 * CH) + (u - 2))
                        elif not (isinstance(b, int) and b == 0):
                            if u == 0:
                                wait_run(pe, S["kvr_ready"], b * (3 * CH))
                                if not (isinstance(b, int) and b == 1):
                                    wait_run(pe, S["sigf_done"], 2 * b - 2)
                            else:
                                wait_run(pe, S["x2_done"], b)
                        for k in range(CH):
                            ins = pe.matmul(psM[:, u % 3, :], w[:, k, c * P:(c + 1) * P], mixA[:, m, k, :],
                                            start=(k == 0), stop=(k == CH - 1))
                        ins.then_inc(S["proj_done"], 1)

            def project_out(b):
                wait_run(pe, S["att_done"], CH * b + CH)
                if not (isinstance(b, int) and b == 0):
                    wait_run(pe, S["relu_done"], HC * b)
                    wait_run(pe, S["sigf_done"], 2 * b - 1)
                for j in range(J):
                    for c in range(CH):
                        ins = pe.matmul(psM[:, 1 + j // 2, (j % 2) * C:(j % 2 + 1) * C],
                                        att[:, c, j * P:(j + 1) * P], wo[:, c, :], start=(c == 0), stop=(c == CH - 1))
                ins.then_inc(S["o_done"], 1)

            def hidden(b, extra, rnd):
                wait_run(pe, S["mixk_hi"], CH * b + CH)
                for h in range(HC):
                    if h < 3:
                        if isinstance(b, int) and b == NB - 1:
                            pe.wait_ge(S["x2_done"], NB)
                            pe.wait_ge(S["sigf_done"], 2 * NB - 2)
                        else:
                            wait_run(pe, S["kvr_ready"], b * (3 * CH) + (3 * CH + 4 + h))
                    else:
                        pe.wait_ge(S["relu_done"], b * HC + (h - 2))
                    n = slice(h * P, (h + 1) * P)
                    for k in range(CH):
                        pe.matmul(psM[:, h % 3, :], wfk_hi[:, k, n], mix_hi[:, k, :],
                                  start=(k == 0), stop=False)
                        pe.matmul(psM[:, h % 3, :], wfk_lo[:, k, n], mix_hi[:, k, :],
                                  start=False, stop=False)
                    if h == 0:
                        wait_run(pe, S["mix2_done"], b + 1)
                    for k in range(CH):
                        ins = pe.matmul(psM[:, h % 3, :], wfk_hi[:, k, n], mix_lo[:, k, :],
                                        start=False, stop=(k == CH - 1))
                    ins.then_inc(S["kf_done"], 1)
                    if h == 5:
                        extra(rnd, 0)

            def receptance(b):
                wait_run(pe, S["mixr2_done"], b + 1)
                for u in range(2):
                    pe.wait_ge(S["relu_done"], b * HC + (HC + u - 2))
                    for j in (2 * u, 2 * u + 1):
                        for k in range(CH):
                            ins = pe.matmul(psM[:, (HC + u) % 3, (j % 2) * C:(j % 2 + 1) * C],
                                            mixB_r[:, k, j * P:(j + 1) * P], wfr[:, k, :],
                                            start=(k == 0), stop=(k == CH - 1))
                    ins.then_inc(S["fr_done"], 1)

            def channel_out(b, j):
                if j == 0:
                    pe.wait_ge(S["sq_done"], b * HC + HC)
                    if not (isinstance(b, int) and b == 0):
                        wait_run(pe, S["s_mult"], b)
                for h in range(HC):
                    ins = pe.matmul(psKV[:, j // 2, (j % 2) * C:(j % 2 + 1) * C], kf2[:, h, j * P:(j + 1) * P],
                                    wfv[:, h, :], start=(h == 0), stop=(h == HC - 1))
                ins.then_inc(S["kv_done"], 1)

            def round_(b, extra, ffn=True, ahead=True):
                if ffn:
                    hidden(b - 1, extra, b)
                    receptance(b - 1)
                    channel_out(b - 1, 0)
                    extra(b, 1)
                    channel_out(b - 1, 1)
                else:
                    extra(b, 0)
                    extra(b, 1)
                if ahead:
                    turn1(b + 1)
                if ffn:
                    channel_out(b - 1, 2)
                project_out(b)
                if ahead:
                    project(b + 1, 0, 1)
                extra(b, 2)
                turn2(b)
                if ahead:
                    project(b + 1, 2)
                if ffn:
                    channel_out(b - 1, 3)
                extra(b, 3)

            pe.wait_ge(S["ident_in"], 16)
            router_weights()
            for n in range(4):
                router(n, n, n // 2)
            turn1(0)
            pe.wait_ge(S["proj_w_in"], 48)
            project(0, 0, 1, 2)
            pe.wait_ge(S["halved"], 1)
            round_(0, router_point, ffn=False)
            with pe.Fori(1, ROUTER_ROUNDS) as b:
                round_(b, router_point)
            round_(ROUTER_ROUNDS, softmax)
            with pe.Fori(BIT_ROUND, SELECT_ROUND) as b:
                round_(b, sum_bit)
            round_(SELECT_ROUND, route)
            with pe.Fori(LIST_ROUND, NB - 1) as b:
                round_(b, nothing)
            round_(NB - 1, nothing, ahead=False)
            hidden(NB - 1, nothing, NB)
            receptance(NB - 1)
            for j in range(J):
                channel_out(NB - 1, j)

            def turn_x(t, i):
                wait_run(pe, S["xn_done"], t + 1)
                if not (isinstance(t, int) and t < 2):
                    wait_run(pe, S["mlp_in_ready"], t - 1)
                for k in range(CH):
                    ins = pe.transpose(psT[:, i % 2, k * P:(k + 1) * P], xn_t[i % 2][:, k * P:(k + 1) * P], ident)
                ins.then_inc(S["turned"], 1)

            def mlp_in(t, i):
                wait_run(pe, S["mlp_in_ready"], t + 1)
                if not (isinstance(t, int) and t < 2):
                    wait_run(pe, S["gelu_done"], t - 1)
                for f in range(FK):
                    for k in range(CH):
                        ins = pe.matmul(psM[:, i % 2, f * P:(f + 1) * P], w1_t[i % 2][:, k, f * P:(f + 1) * P],
                                        xnT[i % 2][:, k, :], start=(k == 0), stop=(k == CH - 1))
                ins.then_inc(S["h_done"], 1)

            def mlp_out(t, i):
                src = expert_at[0:1, t:t + 1] if isinstance(t, int) else expert_at[0:1, ds(t, 1)]
                w = pe.value_load(src, min_val=0, max_val=(E - 1) * FK * C)
                wait_run(pe, S["gelu_done"], t + 1)
                if not (isinstance(t, int) and t < 2):
                    wait_run(pe, S["combined"], t - 1)
                for f in range(FK):
                    ins = pe.matmul(y_ps[i % 2], hT_t[i % 2][:, f, :], w2_sb[:, ds(w + f * C, C)],
                                    start=(f == 0), stop=(f == FK - 1))
                ins.then_inc(S["y_done"], 1)

            def step(t, i, g):
                if not isinstance(t, int) or -2 <= t < NT - 2:
                    turn_x(t + 2, (i + 2) % RING)
                if not isinstance(t, int) or -1 <= t < NT - 1:
                    mlp_in(t + 1, (i + 1) % RING)
                if not isinstance(t, int) or t >= 0:
                    mlp_out(t, i)

            pe.wait_ge(S["w2_in"], 16 * E)
            pe.wait_ge(S["relu_done"], HC * NB)
            pe.wait_ge(S["sigf_done"], 2 * NB)
            steps(pe, step)

        @block.vector
        def _(v):
            v.memset(hT[:, :, 0:1], 0.0)
            for c in range(CH):
                v.memset(pp[c][:, 0:1], -1e38)
            v.memset(aa[:, 0:1], 0.0)
            v.memset(bb[:, 0:1], 0.0).then_inc(S["columns_set"], 1)
            v.wait_ge(S["columns_set"], 1)

            def prepare():
                v.wait_ge(S["decay_exp"], 1)
                v.tensor_scalar(wneg[:], wneg[:], -1.0, None, ALU.mult)
                v.tensor_scalar(uneg[:], vecs[:, :, V["first"]], -1.0, None, ALU.mult)
                v.wait_ge(S["weights_in"], 16 * 4)
                v.tensor_scalar(wo.rearrange("p k n -> p (k n)"), wo.rearrange("p k n -> p (k n)"), 0.5, None, ALU.mult)
                v.tensor_scalar(wfv.rearrange("p k n -> p (k n)"), wfv.rearrange("p k n -> p (k n)"), 0.5, None,
                                ALU.mult)
                v.wait_ge(S["wfk_hi_done"], 1)
                v.tensor_tensor(wfk_lo[:], wfk, wfk_hi[:].bitcast(F32), ALU.subtract).then_inc(S["halved"], 1)
                v.wait_ge(S["halved"], 1)

            def router_weights():
                v.wait_ge(S["wg_mean"], 1)
                for k in range(CH):
                    ins = v.scalar_tensor_tensor(wgc[:, k * E:(k + 1) * E], psR[:, 0:E], -1.0 / C,
                                                 wg_sb[:, k * E:(k + 1) * E], ALU.mult, ALU.add)
                ins.then_inc(S["wg_ready"], 1)

            def statistics(b, i, g):
                st = Steps(v, S["a_step"], 2, b, S["waited"])
                wait_run(v, S[f"xa_in{i}"], g * 16 + 16)
                for j in range(J):
                    ins = v.bn_stats(bnst0[:, j], xa[i][:, j])
                ins.then_inc(S["a_stats"], 1)
                wait_run(v, S["a_stats"], b + 1)
                for j in range(J):
                    ins = v.bn_aggr(mv0[:, j], bnst0[:, j])
                st.then(ins)
                st.wait()
                st.then(v.tensor_copy(mvA[:, ds(b * (2 * J), 2 * J)], mv0[:].rearrange("p j s -> p (j s)")))
                st.wait()
                st.end()

            def keep_logits(n, q):
                wait_run(v, S["logits_done"], n + 4)
                v.tensor_copy(logits[:, ds(n * (J * E), J * E)], psR[:, q * J * E:(q + 1) * J * E]
                              ).then_inc(S["logits_kept"], 1)

            def router_point(b, point):
                statistics(b * 4 + (4 + point), point % 2, b * 2 + (2 + point // 2))
                keep_logits(b * 4 + point, point)

            R = Steps(v, S["route_step"], R_ALL, 0, S["waited"])
            te = lambda a: a.rearrange("p (t e) -> p t e", e=E)
            et = lambda a: a.rearrange("p (e t) -> p e t", e=E)
            over_e = lambda a: a.rearrange("p (t o) -> p t o", o=1).to_broadcast([P, NTILE, E])
            sm = lambda k: small[:, k * NTILE:(k + 1) * NTILE]
            def scores():
                v.wait_ge(S["logits_done"], NB)
                R.then(v.tensor_copy(logits[:, (NB - 4) * J * E:NB * J * E], psR[:, 0:4 * J * E]))
                v.wait_ge(S["logits_kept"], NB - 4)
                v.wait_ge(S["consts_in"], 48)
                v.tensor_copy(info[:, :, 0:1].rearrange("p t o -> p (t o)").bitcast(I32), ids_sb)
                R.then(v.memset(reset, 1.0))
                R.wait()
                R.then(v.memset(et(reset)[:, :, 0], 0.0))
                v.wait_ge(S["pow_ready"], 8 * (ROUTER_ROUNDS + 2))
                R.then(v.tensor_tensor(te(logits), te(logits), info[:, :, 2:3].to_broadcast([P, NTILE, E]), ALU.mult))
                R.wait()
                R.then(v.tensor_reduce(sm(6), te(logits), AX_X, ALU.max))
                R.wait()
                v.tensor_tensor(te(logits), te(logits), over_e(sm(6)), ALU.subtract).then_inc(S["route_exp_in"], 1)

            def probabilities():
                v.wait_ge(S["route_exp_out"], 1)
                R.then(v.tensor_reduce(sm(7), te(probs), AX_X, ALU.add))
                R.wait()
                R.then(v.reciprocal(sm(6), sm(7)))
                R.wait()
                R.then(v.tensor_tensor(te(probs), te(probs), over_e(sm(6)), ALU.mult))
                R.wait()
                R.then(v.tensor_copy(pexp.rearrange("p (j t e) -> p j t e", j=J, e=E),
                                     probs.rearrange("p (t j e) -> p j t e", j=J, e=E)))
                assert R.k == R_PEXP, R.k

            def turned_probabilities():
                v.wait_ge(S["probs_turned"], 1)
                R.then(v.tensor_copy(selT, psR[:]))
                R.wait()
            t_f, bit, cand, kept, cnt = (tiny[:, k:k + 1] for k in range(5))

            def try_bit(b, point):
                bits = 2 + point
                st = Steps(v, S["bit_step"], 3 * 4, b - BIT_ROUND, S["waited"])
                st.k = 3 * bits
                if isinstance(b, int) and b == ROUTER_ROUNDS and point == 2:
                    st.then(v.memset(t_f, 0.0))
                    st.then(v.memset(bit.bitcast(I32), 1 << 29))
                else:
                    wait_run(v, S["bit_summed"], (b - BIT_ROUND) * 4 + bits)
                    v.tensor_scalar(bit.bitcast(I32), bit.bitcast(I32), 1, None, ALU.logical_shift_right)
                    st.then(v.scalar_tensor_tensor(kept, psR[:, 0:1], float(CAP), cand, ALU.is_ge, ALU.mult))
                    st.wait()
                    st.then(v.tensor_tensor(t_f, t_f, kept, ALU.max))
                st.wait()
                st.then(v.tensor_tensor(cand.bitcast(I32), t_f.bitcast(I32), bit.bitcast(I32), ALU.bitwise_or))
                st.wait()
                v.tensor_scalar(work, selT, cand, None, ALU.is_ge, ALU.add, accum_out=cnt).then_inc(S["bit_counted"], 1)

            def softmax(b, point):
                if point < 3:
                    (scores, probabilities, turned_probabilities)[point]()
                if point >= 2:
                    try_bit(b, point)

            def route(b, point):
                if b == SELECT_ROUND:
                    (count_ties, select, choose, keep_prefix)[point]()
                elif point == 0:
                    place_tokens()
                    list_part(b)

            def count_ties():
                v.wait_ge(S["bit_summed"], 30)
                v.wait_ge(S["bit_counted"], 30)
                R.then(v.scalar_tensor_tensor(kept, psR[:, 0:1], float(CAP), cand, ALU.is_ge, ALU.mult))
                R.wait()
                R.then(v.tensor_tensor(t_f, t_f, kept, ALU.max))
                R.wait()
                v.tensor_scalar(oneT, selT, t_f, None, ALU.is_gt, ALU.add, accum_out=tiny[:, 5:6])
                R.then(v.tensor_scalar(work, selT, t_f, None, ALU.is_equal, ALU.add, accum_out=tiny[:, 6:7]))
                R.wait()
                assert R.k == R_COUNTS, R.k
                R.then(v.tensor_tensor_scan(win, ones[:, 0:1].to_broadcast([P, SEQ]), work, 0.0, ALU.mult, ALU.add))

            def select():
                v.wait_ge(S["route_pe"], 1)
                R.then(v.tensor_scalar(tiny[:, 7:8], psR[:, 0:1], -1.0, float(CAP), ALU.mult, ALU.add))
                R.wait()
                R.then(v.tensor_tensor(tiny[:, 8:9], tiny[:, 7:8], psR[:, 1:2], ALU.subtract))
                R.wait()
                R.then(v.scalar_tensor_tensor(win, win, tiny[:, 8:9], work, ALU.is_le, ALU.mult))
                R.wait()
                R.then(v.tensor_tensor(oneT, oneT, win, ALU.add))
                assert R.k == R_SEL, R.k

            def choose():
                v.wait_ge(S["route_pe"], 2)
                R.then(v.tensor_copy(work.rearrange("p (t j e) -> p j t e", j=J, e=E),
                                     psR[:].rearrange("p (j t e) -> p j t e", j=J, e=E)))
                R.wait()
                R.then(v.tensor_reduce(sm(6), te(work), AX_X, ALU.max))
                R.wait()
                R.then(v.tensor_scalar(sm(7), sm(6), 0.5, None, ALU.is_lt))
                R.wait()
                R.then(v.tensor_tensor(te(work), te(work), over_e(sm(7)), ALU.max))
                R.wait()
                R.then(v.tensor_tensor(win, probs, work, ALU.mult))
                R.then(v.tensor_scalar(mask8, work, -1.0, None, ALU.add))
                R.wait()
                R.then(v.tensor_tensor(win, win, mask8, ALU.add))
                R.wait()
                R.then(v.tensor_reduce(gate, te(win), AX_X, ALU.max))
                R.wait()
                R.then(v.tensor_tensor(te(work), te(win), over_e(gate), ALU.is_equal))
                R.wait()
                R.then(v.tensor_tensor(te(work), te(work),
                                       erev.rearrange("p (o e) -> p o e", o=1).to_broadcast([P, NTILE, E]), ALU.mult))
                R.wait()
                R.then(v.tensor_reduce(sm(6), te(work), AX_X, ALU.max))
                R.wait()
                R.then(v.tensor_tensor(te(pexp), te(work), over_e(sm(6)), ALU.is_equal))
                assert R.k == R_ONEHOT, R.k

            def keep_prefix():
                v.wait_ge(S["route_pe"], 3)
                R.then(v.tensor_copy(win, psR[:]))
                assert R.k == R_KEPT, R.k

            def place_tokens():
                v.wait_ge(S["route_pe"], 4)
                R.then(v.tensor_copy(et(logits), psR[:].rearrange("p (t e) -> p e t", e=E)))
                R.wait()
                R.then(v.tensor_tensor_scan(work, reset, logits, 0.0, ALU.mult, ALU.add))
                R.wait()
                c8 = lambda k: tiny[:, 16 + k * E:16 + (k + 1) * E]
                R.then(v.tensor_scalar(c8(0).bitcast(I32), et(work)[:, :, NTILE - 1], float(P - 1), None, ALU.add))
                R.wait()
                R.then(v.tensor_scalar(c8(1).bitcast(I32), c8(0).bitcast(I32), 7, None, ALU.logical_shift_right))
                R.wait()
                R.then(v.tensor_copy(c8(2), c8(1).bitcast(I32)))
                R.wait()
                R.then(v.tensor_tensor_scan(c8(3), ones[:, 0:E], c8(2), 0.0, ALU.mult, ALU.add))
                R.wait()
                R.then(v.tensor_tensor(c8(4), c8(3), c8(2), ALU.subtract))
                R.wait()
                R.then(v.tensor_scalar(c8(5), c8(4), float(P), -1.0, ALU.mult, ALU.add))
                R.then(v.tensor_tensor(work, work, logits, ALU.subtract))
                R.wait()
                R.then(v.tensor_tensor(et(work), et(work), c8(5).rearrange("p (e o) -> p e o", o=1).to_broadcast([P, E, NTILE]),
                                       ALU.add))
                R.wait()
                R.then(v.tensor_tensor(te(win), te(win), work.rearrange("p (e t) -> p t e", e=E), ALU.add))
                R.wait()
                R.then(v.tensor_tensor(win, win, pexp, ALU.mult))
                R.wait()
                R.then(v.tensor_reduce(sm(6), te(win), AX_X, ALU.add))
                R.wait()
                R.then(v.tensor_copy(place[:], sm(6)))
                R.wait()
                R.then(v.tensor_scalar(sm(2).bitcast(I32), place[:], P - 1, None, ALU.bitwise_and))
                R.then(v.tensor_scalar(sm(3).bitcast(I32), place[:], 7, None, ALU.logical_shift_right))
                R.wait()
                R.then(v.tensor_copy(sm(4), sm(2).bitcast(I32)))
                R.then(v.tensor_copy(sm(5), sm(3).bitcast(I32)))
                R.wait()
                R.then(v.scalar_tensor_tensor(place[:], sm(4), float(NT), sm(5), ALU.mult, ALU.add))
                R.then(v.tensor_scalar(info[:, :, 1:2].rearrange("p t o -> p (t o)"), gate, 0.5, None, ALU.mult))
                tw3 = tw[0:1, :].rearrange("p (n e) -> p n e", e=E)
                R.then(v.tensor_tensor(tw3, iota_sb[0:1, :].rearrange("p (n o) -> p n o", o=1).to_broadcast([1, NT, E]),
                                       c8(3)[0:1, :].rearrange("p (o e) -> p o e", o=1).to_broadcast([1, NT, E]), ALU.is_ge))
                R.wait()
                R.then(v.tensor_reduce(win[0:1, 0:NT], tw3, AX_X, ALU.add))
                R.wait()
                R.then(v.tensor_scalar(expert_at[:], win[0:1, 0:NT], float(E - 1), float(CH * F), ALU.min, ALU.mult))
                R.wait()
                v.tensor_copy(tiny[:, 60:61], tiny[:, 0:1]).then_inc(S["routed"], 1)
                R.end()

            def list_part(b):
                n = b - LIST_ROUND
                if not (isinstance(b, int) and b == LIST_ROUND):
                    wait_run(v, S["list_scattered"], n * (16 * LT))
                v.tensor_copy(place_cur[:], place[:, ds(n * LT, LT)])
                v.tensor_copy(info_cur[:].rearrange("p t w -> p (t w)"),
                              info[:].rearrange("p t w -> p (t w)")[:, ds(n * (4 * LT), 4 * LT)].bitcast(I32)
                              ).then_inc(S["list_cur"], 1)

            def listing(b, point):
                if point == 0:
                    list_part(b)

            def fetch(b):
                if not (isinstance(b, int) and b == 0):
                    wait_run(v, S["x0_ready"], b)
                v.tensor_copy(stats_cur[:].rearrange("p j s -> p (j s)"),
                              stats0[:].rearrange("p t s -> p (t s)")[:, ds(b * (2 * J), 2 * J)]
                              ).then_inc(S["fetched"], 1)

            def moments(b, mv, st, ready):
                xs = tile_row(b)
                for j in range(J):
                    ins = v.bn_stats(bnst[:, j], xs[:, j * C:(j + 1) * C])
                st.then(ins)
                st.wait()
                for j in range(J):
                    ins = v.bn_aggr(mv[:, j], bnst[:, j])
                ins.then_inc(S[ready], 1)

            def moments1(b):
                st = Steps(v, S["moments_step"], 1, b, S["waited"])
                wait_run(v, S["embedded"], b + 1)
                moments(b, mv1, st, "ln1_stats")
                st.end()

            def mix(b, ready, step, outs, done):
                st = Steps(v, S[step], CH, b, S["waited"])
                for c in range(CH):
                    v.wait_ge(S[ready], CH * b + (c + 1))
                    st.then(v.tensor_tensor(dmix[:, c], hT[:, c, 1:SEQ + 1], hT[:, c, 0:SEQ], ALU.subtract))
                for i, (dst, m) in enumerate(outs):
                    for c in range(CH):
                        if i == 0:
                            st.wait(c + 1)
                        ins = v.scalar_tensor_tensor(dst[:, c], dmix[:, c], vecs[:, c, V[m]:V[m] + 1],
                                                     hT[:, c, 0:SEQ], ALU.mult, ALU.add)
                        if done == "mixk_done":
                            ins.then_inc(S[done], 1)
                    if done != "mixk_done":
                        ins.then_inc(S[done], 1)
                st.end()

            def mix1(b):
                if not (isinstance(b, int) and b < 2):
                    wait_run(v, S["mix2_done"], b - 1)
                    wait_run(v, S["mixr2_done"], b - 1)
                mix(b, "h1_ready", "mix1_step", [(mixA[:, 0], "tmk"), (mixA[:, 1], "tmv")], "mix1_done")

            def mix2(b):
                if not (isinstance(b, int) and b == NB - 1):
                    wait_run(v, S["mix1_done"], 2 * b + 4)
                    wait_run(v, S["mixr1_done"], b + 2)
                mix(b, "h2_ready", "mix2_step", [(kx, "cmk")], "mixk_done")
                for c in range(CH):
                    v.wait_ge(S["mixk_hi"], CH * b + (c + 1))
                    ins = v.tensor_tensor(mix_lo[:, c], kx[:, c], mix_hi[:, c].bitcast(F32), ALU.subtract)
                ins.then_inc(S["mix2_done"], 1)

            def wkv_start(b):
                st = Steps(v, S["wkv_step"], WKV_STEPS, b, S["waited"])
                for c in range(CH):
                    v.wait_ge(S["kvr_ready"], b * (3 * CH) + (c + 1))
                    st.then(v.tensor_tensor_scan(pp[c][:, 1:SEQ + 1], wneg[:, c:c + 1].to_broadcast([P, SEQ]),
                                                 kvs[:, 0, c, :], -1e38, ALU.add, ALU.max))
                for c in range(CH):
                    st.wait(1 + c)
                    st.then(v.tensor_tensor(qb[c], pp[c][:, 0:SEQ], kvs[:, 0, c, :], ALU.subtract))
                for c in range(CH):
                    st.wait(3 + c)
                    v.tensor_scalar(E1[c][:, 0], qb[c], wneg[:, c:c + 1], 0.0, ALU.add, ALU.min)
                    v.tensor_scalar(E1[c][:, 1], qb[c], uneg[:, c:c + 1], 0.0, ALU.add, ALU.min).then_inc(S["pre_done"], 1)

            def wkv_end(b, c, st):
                e1, f1, e2, f2 = E1[c][:, 0], E1[c][:, 1], E2[c][:, 0], E2[c][:, 1]
                val, r = kvs[:, 1, c, :], kvs[:, 2, c, :]
                v.wait_ge(S["exp_done"], b * (2 * CH) + (2 * c + 2))
                v.wait_ge(S["kvr_ready"], b * (3 * CH) + (CH + c + 1))
                weighted = st.then(v.tensor_tensor(evb, e2, val, ALU.mult))
                state_b = st.then(v.tensor_tensor_scan(bb[:, 1:SEQ + 1], e1, e2, 0.0, ALU.mult, ALU.add))
                st.wait(weighted)
                state_a = st.then(v.tensor_tensor_scan(aa[:, 1:SEQ + 1], e1, evb, 0.0, ALU.mult, ALU.add))
                st.then(v.tensor_tensor(t1b, f2, val, ALU.mult))
                st.wait(state_b)
                past_b = st.then(v.tensor_tensor(qb[c], f1, bb[:, 0:SEQ], ALU.mult))
                st.wait(state_a)
                past_a = st.then(v.tensor_tensor(e1, f1, aa[:, 0:SEQ], ALU.mult))
                st.wait(past_b)
                below = st.then(v.tensor_tensor(qb[c], qb[c], f2, ALU.add))
                st.wait(past_a)
                above = st.then(v.tensor_tensor(e1, e1, t1b, ALU.add))
                st.wait(below)
                st.then(v.reciprocal(e2, qb[c]))
                v.wait_ge(S["kvr_ready"], b * (3 * CH) + (2 * CH + c + 1))
                st.wait(above)
                st.then(v.scalar_tensor_tensor(e1, r, 1.0, e1, ALU.add, ALU.mult))
                st.wait()
                v.tensor_tensor(att[:, c], e1, e2, ALU.mult).then_inc(S["att_done"], 1)

            def wkv(b, extra, ahead, further):
                st = Steps(v, S["wkv_step"], WKV_STEPS, b, S["waited"])
                st.k = 2 * CH
                if not (isinstance(b, int) and b == 0):
                    wait_run(v, S["mix2_done"], b)
                for c in range(CH):
                    if c == 0 and not (isinstance(b, int) and b == 0):
                        wait_run(v, S["o_done"], b)
                    extra(b, c)
                    if c == 0 and not (isinstance(b, int) and b < 2):
                        residual2(b - 2)
                    if c == 1 and ahead:
                        moments1(b + 1)
                        if further:
                            fetch(b + 2)
                    wkv_end(b, c, st)
                st.end()

            def residual1(b):
                st = Steps(v, S["ln2_step"], 1, b, S["waited"])
                v.wait_ge(S["o_done"], b + 1)
                xs = tile_row(b)
                v.tensor_tensor(xs, xs, psM[:, 1:3, :].rearrange("p b n -> p (b n)"), ALU.add).then_inc(S["x2_done"], 1)
                wait_run(v, S["x2_done"], b + 1)
                moments(b, mv2, st, "ln2_stats")
                st.end()

            def residual2(b):
                v.wait_ge(S["kv_done"], J * b + J)
                v.wait_ge(S["sigf_done"], 2 * b + 2)
                v.scalar_tensor_tensor(sigf, sigf, 1.0, psKV[:].rearrange("p b n -> p (b n)"), ALU.add, ALU.mult
                                       ).then_inc(S["s_mult"], 1)

            def round_(b, extra, ffn=True, ahead=True, further=True):
                wkv(b, extra, ahead, further)
                if ahead:
                    mix1(b + 1)
                residual1(b)
                extra(b, 2)
                if ahead:
                    wkv_start(b + 1)
                extra(b, 3)
                mix2(b)

            statistics(0, 0, 0)
            router_weights()
            v.wait_ge(S["pow_ready"], 8)
            fetch(0)
            statistics(1, 1, 0)
            statistics(2, 0, 1)
            moments1(0)
            statistics(3, 1, 1)
            mix1(0)
            prepare()
            v.wait_ge(S["pow_ready"], 16)
            fetch(1)
            wkv_start(0)
            round_(0, router_point, ffn=False)
            for b in range(1, ROUTER_ROUNDS):
                if b == 2:
                    v.wait_ge(S["pow_ready"], 24)
                round_(b, router_point)
            round_(ROUTER_ROUNDS, softmax)
            with v.Fori(BIT_ROUND, SELECT_ROUND) as b:
                round_(b, try_bit)
            round_(SELECT_ROUND, route)
            round_(LIST_ROUND, route)
            with v.Fori(LIST_ROUND + 1, NB - 2) as b:
                round_(b, listing)
            round_(NB - 2, listing, further=False)
            round_(NB - 1, listing, ahead=False, further=False)
            residual2(NB - 2)

            def index_of(t):
                return list_sb[:, t, 0:1] if isinstance(t, int) else list_sb[:, ds(t, 1), 0:1].rearrange("p n w -> p (n w)")

            def take_index(t, i):
                v.tensor_copy(row_idx[i][:], index_of(t)).then_inc(S["idx_ready"], 1)

            def take_info(t, i):
                src = list_sb[:, t, :] if isinstance(t, int) else list_sb[:, ds(t, 1), :].rearrange("p n w -> p (n w)")
                v.tensor_copy(info_t[i][:], src.bitcast(F32)).then_inc(S["info_ready"], 1)

            def mlp_input(t, i):
                src = expert_at[0:1, t:t + 1] if isinstance(t, int) else expert_at[0:1, ds(t, 1)]
                w = v.value_load(src, min_val=0, max_val=(E - 1) * CH * F)
                if not (isinstance(t, int) and t < 2):
                    wait_run(v, S["h_done"], t - 1)
                v.tensor_copy(w1_t[i % 2].rearrange("p k f -> p (k f)"), w1_sb[:, ds(w, CH * F)])
                v.wait_ge(S["turned"], t + 1)
                v.tensor_copy(xnT[i % 2].rearrange("p k t -> p (k t)"), psT[:, i % 2, 0:C]
                              ).then_inc(S["mlp_in_ready"], 1)

            def combine(t, i, g):
                st = Steps(v, S["combine_step"], 2, t, S["waited"])
                th = th_t[i % 2]
                wait_run(v, S["tanh_done"], t + 1)
                if isinstance(t, int) and t < RING:
                    v.wait_ge(S[f"s_gathered{i}"], 16)
                v.tensor_copy(out_idx[i][:], index_of(t))
                st.then(v.scalar_tensor_tensor(out_t[i], y_ps[i % 2], info_t[i][:, 1:2],
                                               rows[i][:, C:2 * C], ALU.mult, ALU.mult))
                st.wait()
                st.then(v.scalar_tensor_tensor(th, th, 1.0, out_t[i], ALU.add, ALU.mult))
                st.wait()
                v.tensor_tensor(out_t[i], th, rows[i][:, 0:C], ALU.add).then_inc(S["combined"], 1)
                st.end()

            def step(t, i, g):
                if not isinstance(t, int) or t < NT - 3:
                    mlp_input(t + 3, (i + 3) % RING)
                if not isinstance(t, int) or t >= 0:
                    if not (isinstance(t, int) and t < RING):
                        wait_run(v, S[f"rows_out{i}"], g * 16)
                    combine(t, i, g)
                    if not isinstance(t, int) or t < NT - RING:
                        take_index(t + RING, i)
                if not isinstance(t, int) or t < NT - 4:
                    take_info(t + 4, (i + 4) % RING)

            v.wait_ge(S["list_in"], 16)
            for t in range(RING):
                take_index(t, t)
            take_info(0, 0)
            v.tensor_scalar(s_idx[:], list_sb[:, 0:RING, 0], 2.0, 1.0, ALU.mult, ALU.add).then_inc(S["s_idx_ready"], 1)
            residual2(NB - 1)
            v.wait_ge(S["w1_in"], 16 * E)
            steps(v, step)


def kernel(**inputs):
    import numpy as np
    import concourse.bacc as bacc
    from concourse.bass_utils import run_bass_kernel_spmd

    a = {k: np.asarray(v) for k, v in inputs.items()}
    x = np.ascontiguousarray(a["L0_attn_x"]).reshape(-1, a["L0_attn_x"].shape[-1])
    T, C = x.shape
    E = a["L0_ffn_Wg"].shape[1]
    names = dict(ln1_w="ln1_w", ln1_b="ln1_b", ln2_w="ln2_w", ln2_b="ln2_b", decay="time_decay",
                 first="time_first", tmk="tmk", tmv="tmv", tmr="tmr", cmk="cmk", cmr="cmr")
    p = np.arange(P)
    same = p[:, None] % E == p[None, :] % E
    consts = np.concatenate([
        p[:, None] == p[None, :], same, same & (p[:, None] < p[None, :]), p[:, None] <= p[None, :],
        np.ones((P, P)), np.broadcast_to(E - np.arange(E), (P, E))], axis=1).astype(np.float32)
    NT = T // P + E
    arrays = {
        "x": x,
        "xT": np.ascontiguousarray(x.T),
        "vec": np.stack([a["L0_attn_" + names[n]] for n in PARAMS], axis=1),
        "ln0_w": a["L0_attn_ln0_w"],
        "ln0_b": a["L0_attn_ln0_b"],
        **{n + "T": np.ascontiguousarray(a["L0_attn_" + n].T) for n in ("Wk", "Wv", "Wr", "Wo", "Wfk", "Wfr", "Wfv")},
        "Wg": a["L0_ffn_Wg"],
        "W1": a["L0_ffn_W1"],
        "W2": a["L0_ffn_W2"],
        "consts": consts,
        "tile_iota": np.arange(NT, dtype=np.float32)[None, :],
        "token_ids": np.arange(T, dtype=np.int32).reshape(T // P, P).T,
        "pad_rows": np.stack([T + np.arange(NT * P), *np.zeros((3, NT * P))], axis=1).astype(np.int32),
    }
    nc = bacc.Bacc("TRN2", target_bir_lowering=False, num_devices=1)
    feeds = {f"in_{n}": np.ascontiguousarray(v) for n, v in arrays.items()}
    args = [nc.dram_tensor(n, v.shape, mybir.dt.from_np(v.dtype), kind="ExternalInput").ap() for n, v in feeds.items()]
    args.append(nc.dram_tensor("sorted_list", (NT * P, 4), I32, kind="Internal").ap())
    args.append(nc.dram_tensor("xs_rows", (T, 2 * C), F32, kind="Internal").ap())
    args.append(nc.dram_tensor("out_0_dram", (T, C), F32, kind="ExternalOutput").ap())
    rwkv_times_moe(nc, *args)
    r = run_bass_kernel_spmd(nc, [feeds], core_ids=[0])
    return r.results[0]["out_0_dram"].reshape(a["L0_attn_x"].shape)
```
